# Optimizing a Trainium2 kernel written in Bass

```python
import numpy as np
import jax
import jax.numpy as jnp

def _softmax(x, axis=-1):
    return jax.nn.softmax(x, axis=axis)

def _gelu(x):
    return jax.nn.gelu(x, approximate=True)

def _silu(x):
    return jax.nn.silu(x)

def _sigmoid(x):
    return jax.nn.sigmoid(x)

def _layernorm(x, axis=-1, eps=1e-05):
    m = jnp.mean(x, axis=axis, keepdims=True)
    v = jnp.var(x, axis=axis, keepdims=True)
    return (x - m) / jnp.sqrt(v + eps)

def _scatter_add(tgt, idx, src, axis=0):
    return tgt.at[idx].add(src)

def _segment_sum(src, seg, n):
    return jax.ops.segment_sum(src, seg, n)
kernel_name = 'mk_xattn_ffn_d2_seqx_r4_aa91db'

def setup_inputs(seed: int=0):
    np.random.seed(seed)
    _w = jnp.asarray

    def _rec_inputs():
        import jax
        import jax.numpy as jnp
        _rk = jax.random.key(seed)
        x = -0.0005207 + 1.001 * jax.random.normal(jax.random.fold_in(_rk, 1), (4, 512, 256), jnp.float32)
        _lenS = 512 - jax.random.randint(jax.random.fold_in(_rk, 7), (4,), 0, max(1, 512 // 4) + 1, jnp.int32)
        _lenS2 = 1024 - jax.random.randint(jax.random.fold_in(_rk, 8), (4,), 0, max(1, 1024 // 4) + 1, jnp.int32)
        _ctx_1024P = jax.random.normal(jax.random.fold_in(_rk, 11), (4, 16, 256), jnp.float32)
        _ctx_1024c = jax.random.dirichlet(jax.random.fold_in(_rk, 511), 0.3 * jnp.ones((16,), jnp.float32), (4, 1024))
        _ctx_1024t = jnp.einsum('bsk,bkd->bsd', _ctx_1024c, _ctx_1024P)
        _ctx_1024t = _ctx_1024t * jax.lax.rsqrt(jnp.mean(jnp.square(_ctx_1024t)) + 1e-12) * 0.953939
        ctx_1024 = -1.52775e-05 + 0.999936 * (_ctx_1024t + 0.3 * jax.random.normal(jax.random.fold_in(_rk, 611), (4, 1024, 256), jnp.float32))
        return (x, ctx_1024)
    x, ctx_1024 = _rec_inputs()

    def _L0_xattn_setup():
        import jax, jax.numpy as jnp
        import numpy as np
        DIM = 256
        HEADS = 16
        DHEAD = 64
        INNER = HEADS * DHEAD
        EPS = 1e-05

        def layer_norm(x, g, b):
            mu = jnp.mean(x, axis=-1, keepdims=True)
            var = jnp.mean(jnp.square(x - mu), axis=-1, keepdims=True)
            return (x - mu) * jax.lax.rsqrt(var + EPS) * g + b

        def apply_rope(x, cos, sin):
            d2 = x.shape[-1] // 2
            x1, x2 = (x[..., :d2], x[..., d2:])
            return jnp.concatenate([x1 * cos - x2 * sin, x2 * cos + x1 * sin], axis=-1)
        key = jax.random.key(seed)
        ks = jax.random.split(key, 10)
        B, N, S = (8, 64, 1024)
        latents = jax.random.normal(ks[0], (B, N, DIM), dtype=jnp.float32)
        context = jax.random.normal(ks[1], (B, S, DIM), dtype=jnp.float32)
        cos = jax.random.uniform(ks[2], (S, DHEAD // 2), dtype=jnp.float32)
        sin = jax.random.uniform(ks[3], (S, DHEAD // 2), dtype=jnp.float32)
        init = lambda k, shp, fan_in: jax.random.normal(k, shp, dtype=jnp.float32) / np.sqrt(fan_in)
        return {'latents': latents, 'context': context, 'cos': cos, 'sin': sin, 'ln_lat_g': jnp.ones((DIM,), jnp.float32), 'ln_lat_b': jnp.zeros((DIM,), jnp.float32), 'ln_ctx_g': jnp.ones((DIM,), jnp.float32), 'ln_ctx_b': jnp.zeros((DIM,), jnp.float32), 'Wq': init(ks[4], (DIM, INNER), DIM), 'Wkv': init(ks[5], (DIM, 2 * INNER), DIM), 'Wo': init(ks[6], (INNER, DIM), INNER), 'bo': jnp.zeros((DIM,), jnp.float32)}
    _L0_xattn_all = _L0_xattn_setup()
    _L0_xattn_in = {k: v for k, v in _L0_xattn_all.items() if k in ('cos', 'sin', 'ln_lat_g', 'ln_lat_b', 'ln_ctx_g', 'ln_ctx_b', 'Wq', 'Wkv', 'Wo', 'bo')}
    del _L0_xattn_all

    def _L0_ffn_setup():
        import jax, jax.numpy as jnp
        import numpy as np
        B, S, D, E = (2, 512, 256, 8)
        key = jax.random.key(seed)
        ks = jax.random.split(key, 5)
        x = jax.random.normal(ks[0], (B, S, D), dtype=jnp.float32)
        router_w = jax.random.normal(ks[1], (E, D), dtype=jnp.float32) * 0.02
        router_b = jnp.zeros((E,), dtype=jnp.float32)
        expert_w = jax.random.normal(ks[2], (E, D, D), dtype=jnp.float32) * 0.02
        expert_b = jnp.zeros((E, D), dtype=jnp.float32)
        return {'x': x, 'router_w': router_w, 'router_b': router_b, 'expert_w': expert_w, 'expert_b': expert_b}
    _L0_ffn_all = _L0_ffn_setup()
    _L0_ffn_in = {k: v for k, v in _L0_ffn_all.items() if k in ('router_w', 'router_b', 'expert_w', 'expert_b')}
    del _L0_ffn_all

    def _L1_xattn_setup():
        import jax, jax.numpy as jnp
        import numpy as np
        B, T, S, D, H, DK = (2, 512, 512, 256, 16, 64)
        key = jax.random.key(seed)
        ks = jax.random.split(key, 11)
        s = 1.0 / np.sqrt(D)
        return {'query': jax.random.normal(ks[0], (B, T, D), jnp.float32), 'value': jax.random.normal(ks[1], (B, S, D), jnp.float32), 'key': jax.random.normal(ks[2], (B, S, D), jnp.float32), 'Wq': jax.random.normal(ks[3], (D, H, DK), jnp.float32) * s, 'bq': jnp.zeros((H, DK), jnp.float32), 'Wk': jax.random.normal(ks[4], (D, H, DK), jnp.float32) * s, 'bk': jnp.zeros((H, DK), jnp.float32), 'Wv': jax.random.normal(ks[5], (D, H, DK), jnp.float32) * s, 'bv': jnp.zeros((H, DK), jnp.float32), 'Wo': jax.random.normal(ks[6], (H, DK, D), jnp.float32) * (1.0 / np.sqrt(H * DK)), 'bo': jnp.zeros((D,), jnp.float32)}
    _L1_xattn_all = _L1_xattn_setup()
    _L1_xattn_in = {k: v for k, v in _L1_xattn_all.items() if k in ('Wq', 'bq', 'Wk', 'bk', 'Wv', 'bv', 'Wo', 'bo')}
    del _L1_xattn_all

    def _L1_ffn_setup():
        import jax, jax.numpy as jnp
        import numpy as np
        B, T, D = (4, 512, 256)
        H, DH, E, SEL = (8, 64, 5, 2)

        def _topk_mask(logits, k):
            _, idx = jax.lax.top_k(logits, k)
            return jnp.sum(jax.nn.one_hot(idx, logits.shape[-1], dtype=logits.dtype), axis=-2)
        key = jax.random.key(seed)
        ks = jax.random.split(key, 7)
        s = 0.02
        x = jax.random.normal(ks[0], (B, T, D), dtype=jnp.float32)
        Wq = jax.random.normal(ks[1], (D, H * DH), dtype=jnp.float32) * s
        Wk = jax.random.normal(ks[2], (D, H * DH), dtype=jnp.float32) * s
        Ws = jax.random.normal(ks[3], (D, H * E), dtype=jnp.float32) * s
        Wd = jax.random.normal(ks[4], (D, H * E), dtype=jnp.float32) * s
        Wv = jax.random.normal(ks[5], (E, D, DH), dtype=jnp.float32) * s
        Wo = jax.random.normal(ks[6], (E, DH, D), dtype=jnp.float32) * s
        return {'x': x, 'Wq': Wq, 'Wk': Wk, 'Ws': Ws, 'Wd': Wd, 'Wv': Wv, 'Wo': Wo}
    _L1_ffn_all = _L1_ffn_setup()
    _L1_ffn_in = {k: v for k, v in _L1_ffn_all.items() if k in ('Wq', 'Wk', 'Ws', 'Wd', 'Wv', 'Wo')}
    del _L1_ffn_all
    return {'x': x, 'ctx_1024': ctx_1024, 'L0_xattn_cos': _L0_xattn_in['cos'], 'L0_xattn_sin': _L0_xattn_in['sin'], 'L0_xattn_ln_lat_g': _L0_xattn_in['ln_lat_g'], 'L0_xattn_ln_lat_b': _L0_xattn_in['ln_lat_b'], 'L0_xattn_ln_ctx_g': _L0_xattn_in['ln_ctx_g'], 'L0_xattn_ln_ctx_b': _L0_xattn_in['ln_ctx_b'], 'L0_xattn_Wq': _L0_xattn_in['Wq'], 'L0_xattn_Wkv': _L0_xattn_in['Wkv'], 'L0_xattn_Wo': _L0_xattn_in['Wo'], 'L0_xattn_bo': _L0_xattn_in['bo'], 'L0_ffn_router_w': _L0_ffn_in['router_w'], 'L0_ffn_router_b': _L0_ffn_in['router_b'], 'L0_ffn_expert_w': _L0_ffn_in['expert_w'], 'L0_ffn_expert_b': _L0_ffn_in['expert_b'], 'L1_xattn_Wq': _L1_xattn_in['Wq'], 'L1_xattn_bq': _L1_xattn_in['bq'], 'L1_xattn_Wk': _L1_xattn_in['Wk'], 'L1_xattn_bk': _L1_xattn_in['bk'], 'L1_xattn_Wv': _L1_xattn_in['Wv'], 'L1_xattn_bv': _L1_xattn_in['bv'], 'L1_xattn_Wo': _L1_xattn_in['Wo'], 'L1_xattn_bo': _L1_xattn_in['bo'], 'L1_ffn_Wq': _L1_ffn_in['Wq'], 'L1_ffn_Wk': _L1_ffn_in['Wk'], 'L1_ffn_Ws': _L1_ffn_in['Ws'], 'L1_ffn_Wd': _L1_ffn_in['Wd'], 'L1_ffn_Wv': _L1_ffn_in['Wv'], 'L1_ffn_Wo': _L1_ffn_in['Wo']}

def reference(x, ctx_1024, L0_xattn_cos, L0_xattn_sin, L0_xattn_ln_lat_g, L0_xattn_ln_lat_b, L0_xattn_ln_ctx_g, L0_xattn_ln_ctx_b, L0_xattn_Wq, L0_xattn_Wkv, L0_xattn_Wo, L0_xattn_bo, L0_ffn_router_w, L0_ffn_router_b, L0_ffn_expert_w, L0_ffn_expert_b, L1_xattn_Wq, L1_xattn_bq, L1_xattn_Wk, L1_xattn_bk, L1_xattn_Wv, L1_xattn_bv, L1_xattn_Wo, L1_xattn_bo, L1_ffn_Wq, L1_ffn_Wk, L1_ffn_Ws, L1_ffn_Wd, L1_ffn_Wv, L1_ffn_Wo):
    import jax
    import jax.numpy as jnp

    def _L0_xattn_ref(latents, context, cos, sin, ln_lat_g, ln_lat_b, ln_ctx_g, ln_ctx_b, Wq, Wkv, Wo, bo):
        import jax, jax.numpy as jnp
        import numpy as np
        DIM = 256
        HEADS = 16
        DHEAD = 64
        INNER = HEADS * DHEAD
        EPS = 1e-05

        def layer_norm(x, g, b):
            mu = jnp.mean(x, axis=-1, keepdims=True)
            var = jnp.mean(jnp.square(x - mu), axis=-1, keepdims=True)
            return (x - mu) * jax.lax.rsqrt(var + EPS) * g + b

        def apply_rope(x, cos, sin):
            d2 = x.shape[-1] // 2
            x1, x2 = (x[..., :d2], x[..., d2:])
            return jnp.concatenate([x1 * cos - x2 * sin, x2 * cos + x1 * sin], axis=-1)
        b, n, _ = latents.shape
        s = context.shape[1]
        lat = layer_norm(latents, ln_lat_g, ln_lat_b)
        ctx = layer_norm(context, ln_ctx_g, ln_ctx_b)
        q = (lat @ Wq).reshape(b, n, HEADS, DHEAD).transpose(0, 2, 1, 3)
        kv = ctx @ Wkv
        k, v = jnp.split(kv, 2, axis=-1)
        k = k.reshape(b, s, HEADS, DHEAD).transpose(0, 2, 1, 3)
        v = v.reshape(b, s, HEADS, DHEAD).transpose(0, 2, 1, 3)
        k = apply_rope(k, cos[None, None], sin[None, None])
        scale = DHEAD ** (-0.5)
        attn = jnp.einsum('bhnd,bhsd->bhns', q, k) * scale
        attn = jnp.clip(attn, -11.0, 11.0)
        attn = jax.nn.softmax(attn, axis=-1)
        out = jnp.einsum('bhns,bhsd->bhnd', attn, v)
        out = out.transpose(0, 2, 1, 3).reshape(b, n, INNER)
        return out @ Wo + bo

    def _L0_ffn_ref(x, router_w, router_b, expert_w, expert_b):
        import jax, jax.numpy as jnp
        import numpy as np
        B, S, D, E = (2, 512, 256, 8)
        logits = jnp.einsum('bsd,ed->bse', x, router_w) + router_b
        probs = jax.nn.softmax(logits, axis=-1)
        weights = jnp.max(probs, axis=-1)
        top1 = jnp.argmax(probs, axis=-1)
        y_all = jnp.einsum('bsd,eod->bseo', x, expert_w) + expert_b
        y = jnp.take_along_axis(y_all, top1[:, :, None, None], axis=2)[:, :, 0, :]
        out = y * weights[:, :, None]
        return out

    def _L1_xattn_ref(query, value, key, Wq, bq, Wk, bk, Wv, bv, Wo, bo):
        import jax, jax.numpy as jnp
        import numpy as np
        B, T, S, D, H, DK = (2, 512, 512, 256, 16, 64)
        q = jnp.einsum('btd,dhk->bthk', query, Wq) + bq
        k = jnp.einsum('bsd,dhk->bshk', key, Wk) + bk
        v = jnp.einsum('bsd,dhk->bshk', value, Wv) + bv
        q = q * (1.0 / np.sqrt(DK)).astype(np.float32)
        scores = jnp.einsum('bshk,bthk->bhts', k, q)
        probs = jax.nn.softmax(scores, axis=-1)
        attn = jnp.einsum('bhts,bshk->bthk', probs, v)
        out = jnp.einsum('bthk,hkd->btd', attn, Wo) + bo
        return out

    def _L1_ffn_ref(x, Wq, Wk, Ws, Wd, Wv, Wo):
        import jax, jax.numpy as jnp
        import numpy as np
        B, T, D = (4, 512, 256)
        H, DH, E, SEL = (8, 64, 5, 2)

        def _topk_mask(logits, k):
            _, idx = jax.lax.top_k(logits, k)
            return jnp.sum(jax.nn.one_hot(idx, logits.shape[-1], dtype=logits.dtype), axis=-2)
        e, d, dh = Wv.shape
        h = Wq.shape[1] // dh
        b, t, _ = x.shape
        scale = dh ** (-0.5)
        q = (x @ Wq).reshape(b, t, h, dh).transpose(0, 2, 1, 3)
        k = (x @ Wk).reshape(b, t, h, dh).transpose(0, 2, 1, 3)
        gl_v = (x @ Ws).reshape(b, t, h, e)
        wv = _topk_mask(gl_v, SEL) * jax.nn.sigmoid(gl_v)
        xv = jnp.einsum('btd,edk->btek', x, Wv)
        v = jnp.einsum('bthe,btek->bhtk', wv, xv)
        scores = jnp.einsum('bhid,bhjd->bhij', q * scale, k)
        probs = jax.nn.softmax(scores, axis=-1)
        attn = jnp.einsum('bhij,bhjd->bihd', probs, v)
        gl_o = (x @ Wd).reshape(b, t, h, e)
        mask_o = _topk_mask(gl_o, SEL)
        out = jnp.einsum('bthe,bthk,ekd->btd', mask_o, attn, Wo)
        return out
    x = x + _L0_xattn_ref(_layernorm(x, axis=-1), ctx_1024, L0_xattn_cos, L0_xattn_sin, L0_xattn_ln_lat_g, L0_xattn_ln_lat_b, L0_xattn_ln_ctx_g, L0_xattn_ln_ctx_b, L0_xattn_Wq, L0_xattn_Wkv, L0_xattn_Wo, L0_xattn_bo)
    x = x + _L0_ffn_ref(_layernorm(x, axis=-1), L0_ffn_router_w, L0_ffn_router_b, L0_ffn_expert_w, L0_ffn_expert_b)
    x = x + _L1_xattn_ref(_layernorm(x, axis=-1), ctx_1024, ctx_1024, L1_xattn_Wq, L1_xattn_bq, L1_xattn_Wk, L1_xattn_bk, L1_xattn_Wv, L1_xattn_bv, L1_xattn_Wo, L1_xattn_bo)
    x = x + _L1_ffn_ref(_layernorm(x, axis=-1), L1_ffn_Wq, L1_ffn_Wk, L1_ffn_Ws, L1_ffn_Wd, L1_ffn_Wv, L1_ffn_Wo)
    return x

_drawn_inputs = setup_inputs


def setup_inputs(seed=0):
    import zlib

    import numpy as np

    out = dict(_drawn_inputs(seed))
    spreads = {'L0_xattn_ln_lat_g': (1.0, 0.6),
     'L0_xattn_ln_lat_b': (0.0, 0.54),
     'L0_xattn_ln_ctx_g': (1.0, 0.2),
     'L0_xattn_ln_ctx_b': (0.0, 0.1),
     'L0_xattn_bo': (0.0, 0.1),
     'L0_ffn_router_b': (0.0, 0.282),
     'L0_ffn_expert_b': (0.0, 0.453),
     'L1_xattn_bq': (0.0, 0.425),
     'L1_xattn_bk': (0.0, 0.8),
     'L1_xattn_bv': (0.0, 0.1),
     'L1_xattn_bo': (0.0, 0.1)}
    factors = {'L0_xattn_cos': 5.07, 'L0_xattn_sin': 5.224, 'L1_ffn_Wq': 8.0, 'L1_ffn_Wk': 8.0}
    for name, (base, spread) in spreads.items():
        noise = np.random.default_rng([zlib.crc32(name.encode()), seed]).standard_normal(out[name].shape)
        drawn = base * np.exp(spread * noise) if base else spread * noise
        out[name] = jnp.asarray(drawn.astype(out[name].dtype))
    for name, factor in factors.items():
        out[name] = (out[name] * factor).astype(out[name].dtype)
    return out
```

```python
from contextlib import ExitStack, contextmanager
from math import exp

import concourse.bass as bass
from concourse import mybir

P = 128
D = 256
NQ = 512
QT = NQ // P
DH = 64
EPS = 1e-5
CLIP = 11.0
SCALE = DH ** -0.5
EXPERTS = 5
ROUTED = 8
AHEAD = 2


class Count:

    def __init__(self):
        self.turns, self.here = 0, 0

    @property
    def value(self):
        return self.turns + self.here


class Place:

    UNITS = ("turn", "gate", "kv", "k", "kT", "q", "max", "shift", "sum", "back", "mixT", "out")
    KINDS = UNITS + ("norm_x", "norm_c", "split", "top", "biases")

    def __init__(self):
        self.n = {kind: Count() for kind in self.KINDS}
        self.units = Count()
        self.bank = [Count(), Count()]
        self.attends = Count()

    def counts(self):
        return [self.units, *self.bank, self.attends, *self.n.values()]

    def __getitem__(self, kind):
        return self.n[kind].value

    @property
    def ring(self):
        return self.units.here % 2

    def passed(self, item):
        kind = item[0]
        if kind in self.UNITS:
            self.bank[self.ring].here += 1
            self.units.here += 1
        if kind == "end":
            self.attends.here += 1
        elif kind in self.n:
            self.n[kind].here += 1
        if kind == "max" and item[4]:
            self.n["top"].here += 1

    def mark(self):
        return [bank.value for bank in self.bank]


@contextmanager
def turns(eng, trips, place, plans):
    dry = Place()
    for plan in plans:
        for item in plan:
            dry.passed(item)
    gain = [count.here for count in dry.counts()]
    assert gain[0] % 2 == 0, "a turn leaves the ring's banks in step"
    was = [(count.turns, count.here) for count in place.counts()]
    with eng.Fori(0, trips) as i:
        for count, k in zip(place.counts(), gain):
            if k:
                count.turns = count.turns + i * k
        yield i
        for count, k, (_, here) in zip(place.counts(), gain, was):
            assert count.here == here + k
    for count, k, (turned, here) in zip(place.counts(), gain, was):
        count.turns, count.here = turned, here + trips * k


def attend_order(NC):
    order = []
    for c in range(NC):
        order.append([("S", 0, c)] + ([("soft", 1, c - 1)] if c else []))
        order.append([("S", 1, c), ("soft", 0, c)])
        if c:
            order += [[("AV", c - 1, 0)], [("AV", c - 1, 1)]]
    order.append([("soft", 1, NC - 1)])
    return order + [[("AV", NC - 1, 0)], [("AV", NC - 1, 1), ("end",)]]


def prepare_order(kind, KT):
    if kind == "self":
        units = [("vslice",), ("k",), ("q",)]
    else:
        units = [("kv", t) for t in range(KT // 2)] + [("q",)] + [("kT", i) for i in range(KT // 4)]
    if kind == "latent":
        return units
    if kind == "cross":
        units = [("biases",)] + units
    halves = KT // 4
    maxima = [[("max", h, qt, i, (qt, i) == (QT - 1, halves - 1)) for qt in range(QT) for i in range(halves)]
              for h in range(2)]
    mid = len(maxima[1]) // 2
    return units + maxima[0] + maxima[1][:mid] + [("shift", 0)] + maxima[1][mid:] + [("shift", 1)]


def step_plan(kind, KT, attend, prepare, finish, split=False):
    first = [("split",)] if split else []
    finishing = [("sum",)] + ([("back",)] if kind == "self" else []) if finish else []
    preparing = prepare_order(kind, KT) if prepare else []
    if not attend:
        return first + finishing + preparing
    if not preparing:
        preparing = [(), ()] + [()] * 12
    between = preparing[:2] + finishing[:1] + preparing[2:4] + finishing[1:] + preparing[4:]
    order = attend_order(KT // 2)
    plan, given = first, 0
    for i, items in enumerate(order):
        until = (i + 1) * len(between) // len(order)
        plan = plan + items + [item for item in between[given:until] if item]
        given = until
    return plan


def normalise(nc, dve, tiles, sems, src, dst, n, base, rounds):
    ALU = mybir.AluOpType
    stats, mv, varr, rstd, newton, carrier = tiles
    norm_steps, var_ready, rsqrt_ready = sems
    for t in range(n):
        nc.vector.bn_stats(stats[:, t, :], src(t)).then_inc(norm_steps, 1)
    dve.wait_ge(norm_steps, base + n)
    nc.vector.memset(carrier[:, :], 0.0)
    for t in range(n):
        nc.vector.bn_aggr(mv[:, t, :], stats[:, t, :]).then_inc(norm_steps, 1)
    dve.wait_ge(norm_steps, base + 2 * n)
    nc.vector.tensor_scalar(varr[:, 0:n], mv[:, 0:n, 1], EPS, None, ALU.add).then_inc(var_ready, 1)
    dve.wait_ge(rsqrt_ready, rounds + 1)
    nc.vector.tensor_tensor(newton[0][:, 0:n], rstd[:, 0:n], rstd[:, 0:n], ALU.mult).then_inc(norm_steps, 1)
    dve.wait_ge(norm_steps, base + (2 * n + 1))
    nc.vector.tensor_tensor(newton[1][:, 0:n], newton[0][:, 0:n], varr[:, 0:n], ALU.mult).then_inc(norm_steps, 1)
    dve.wait_ge(norm_steps, base + (2 * n + 2))
    nc.vector.tensor_scalar(newton[2][:, 0:n], newton[1][:, 0:n], -0.5, 1.5, ALU.mult, ALU.add).then_inc(norm_steps, 1)
    dve.wait_ge(norm_steps, base + (2 * n + 3))
    nc.vector.tensor_tensor(newton[3][:, 0:n], newton[2][:, 0:n], rstd[:, 0:n], ALU.mult).then_inc(norm_steps, 1)
    dve.wait_ge(norm_steps, base + (2 * n + 4))
    for t in range(n):
        nc.vector.tensor_scalar(dst[:, t, :], src(t), mv[:, t, 0:1], newton[3][:, t:t + 1], ALU.subtract, ALU.mult)\
          .then_inc(norm_steps, 1)


def rank_experts(nc, stepped, logits, rank, over, count):
    ALU = mybir.AluOpType
    stepped(nc.vector.memset(rank[:, :, :, :], 0.0))
    for j in range(count):
        for lo, hi, op in ((0, j, ALU.is_gt), (j + 1, count, ALU.is_ge)):
            if lo < hi:
                shape = [*logits.shape[:3], hi - lo]
                stepped(nc.vector.tensor_tensor(over[:, :, :, lo:hi], logits[:, :, :, j:j + 1].broadcast_to(shape),
                                                logits[:, :, :, lo:hi], op))
                stepped(nc.vector.tensor_tensor(rank[:, :, :, lo:hi], rank[:, :, :, lo:hi], over[:, :, :, lo:hi], ALU.add))


def attention_layer(nc, name, kind, x_in, x_out, context, weights, B, NP, KT):
    fp32, f32r = mybir.dt.float32, mybir.dt.float32r
    ALU, ACT, AX = mybir.AluOpType, mybir.ActivationFunctionType, mybir.AxisListType
    latent, cross, own = kind == "latent", kind == "cross", kind == "self"
    shifted = not latent
    NC = KT // 2
    KEYS = KT * P
    HALVES = KEYS // 512
    HEADS = 2 * NP
    NW = P * len(weights["slices"])
    NV = EXPERTS * DH
    NGATE = NV + 2 * HEADS * EXPERTS
    ROUNDS = 2 if latent else 1
    MAIN = (slice(0, 64), slice(64, 128))
    AUX = (slice(64, 128), slice(0, 64))

    ctx = ExitStack()
    with ctx:
        def sb(label, shape, dt=fp32):
            return ctx.enter_context(nc.sbuf_tensor(f"{name}_{label}", shape, dt))

        def sem(label):
            return ctx.enter_context(nc.semaphore(f"{name}_{label}"))

        X, XN = sb("X", [P, QT, D]), sb("XN", [P, QT, D])
        XTH, XTL = sb("XTH", [P, 2, NQ], f32r), sb("XTL", [P, 2, NQ], f32r)
        staging = [sb(f"staging{i}", [P, 512]) for i in range(2)]
        WRAW = sb("WRAW", [P, 2, NW])
        WH = [sb(f"WH{i}", [P, 2, NW], f32r) for i in range(2)]
        WL = [sb(f"WL{i}", [P, 2, NW], f32r) for i in range(2)]
        S1 = [sb(f"S1{i}", [P, 2, KEYS], f32r) for i in range(2)]
        S2 = [sb(f"S2{i}", [P, 2, KEYS], f32r) for i in range(2)] if shifted else S1
        Q1 = [sb(f"Q1{i}", [P, 2, NQ], f32r) for i in range(2)]
        Q2 = [sb(f"Q2{i}", [P, 2, NQ], f32r) for i in range(2)]
        probs = [[sb(f"probs{h}{i}", [P, 2, NQ]) for i in range(2)] for h in range(2)]
        acc = [sb(f"acc{h}", [P, 2, NQ]) for h in range(2)]
        folded = [sb(f"folded{h}", [P, NQ]) for h in range(2)]
        recip = sb("recip", [P, NQ])
        ident, ones = sb("ident", [P, P]), sb("ones", [P, DH])
        neghalf, scale = sb("neghalf", [P, KT]), sb("scale", [P, 2])
        stats, mv = sb("stats", [P, KT, 6]), sb("mv", [P, KT, 2])
        varr, rstd = sb("varr", [P, KT]), sb("rstd", [P, KT])
        newton = [sb(f"newton{i}", [P, KT]) for i in range(4)]
        prime, carrier, primes = sb("prime", [P, 1]), sb("carrier", [P, 1]), sb("primes", [P, 16])
        VN = [sb(f"VN{i}", [P, KT, 256 if cross else 128]) for i in range(2)]
        VC = 128 if cross else 0
        if not own:
            C = sb("C", [P, KT, D])
            CTH, CTL = sb("CTH", [P, 2, KEYS], f32r), sb("CTL", [P, 2, KEYS], f32r)
            OT = sb("OT", [P, NP, NQ])
            WO = sb("WO", [P, NP, D])
            bo = sb("bo", [P, D])
        if latent:
            KR = sb("KR", [P, KT, P])
            cos, sin, nsin = (sb(n, [P, KT, 32]) for n in ("cos", "sin", "nsin"))
            rot1s, rot2s = ([sb(f"{n}{i}", [P, 2, P]) for i in range(2)] for n in ("rot1", "rot2"))
            gbx, gbc = sb("gbx", [P, 2, 2]), sb("gbc", [P, 2, 2])
        else:
            O32 = sb("O32", [P, NQ])
            part = sb("part", [P, 2, QT, HALVES])
            top, negtop = sb("top", [P, 2, QT]), sb("negtop", [P, 2, QT])
            diag = [sb(f"diag{h}", [P, QT, P], f32r) for h in range(2)]
            spread = sb("spread", [P, P], f32r)
        if cross:
            bqkv = sb("bqkv", [P, 3, NP])
            pair_bias = [sb(f"pair_bias{i}", [P, 2]) for i in range(2)]
        if own:
            WO = sb("WO", [P, 3, D])
            gates_raw = sb("gates_raw", [P, 2, NGATE])
            gates_hi, gates_lo = sb("gates_hi", [P, 2, NGATE], f32r), sb("gates_lo", [P, 2, NGATE], f32r)
            gated = sb("gated", [P, QT, NGATE])
            rank = sb("rank", [P, QT, 2 * HEADS, EXPERTS])
            over = sb("over", [P, QT, 2 * HEADS, EXPERTS])
            sigm = sb("sigm", [P, QT, HEADS * EXPERTS])
            VALL = sb("VALL", [P, QT, HEADS * DH])
            prods = [sb(f"prod{i}", [P, HEADS, DH]) for i in range(2)]
            natural = sb("natural", [P, QT, HEADS * DH])
            mixed = sb("mixed", [P, QT, 3 * P])
            mixedT = sb("mixedT", [P, 3, NQ])

        scores = [ctx.enter_context(nc.psum_tensor(f"{name}_scores{h}", [P, 2, NQ], fp32)) for h in range(2)]
        outT = [ctx.enter_context(nc.psum_tensor(f"{name}_outT{i}", [P, NQ], fp32)) for i in range(2)]
        ring = [ctx.enter_context(nc.psum_tensor(f"{name}_ring{i}", [P, 512], fp32)) for i in range(2)]

        x_loaded, c_loaded, w_loaded = sem("x_loaded"), sem("c_loaded"), sem("w_loaded")
        const_loaded, const_set, const_made = sem("const_loaded"), sem("const_set"), sem("const_made")
        x_stored = sem("x_stored")
        norm_steps, var_ready, rsqrt_ready = sem("norm_steps"), sem("var_ready"), sem("rsqrt_ready")
        w_scaled, w_high, w_split = sem("w_scaled"), sem("w_high"), sem("w_split")
        full = sem("full")
        free = [sem(f"free{i}") for i in range(2)]
        staged, turn_high, high = sem("staged"), sem("turn_high"), sem("high")
        v_copied, rotated = sem("v_copied"), sem("rotated")
        top_found, negtop_ready, diag_ready = sem("top_found"), sem("negtop_ready"), sem("diag_ready")
        s_full, exp_done, clipped, av_done = sem("s_full"), sem("exp_done"), sem("clipped"), sem("av_done")
        added = [sem(f"added{h}") for h in range(2)]
        fold_done = [sem(f"fold_done{h}") for h in range(2)]
        normed, out_biased, rows_biased = sem("normed"), sem("out_biased"), sem("rows_biased")
        biases_ready = sem("biases_ready")
        gate_exp, gate_steps, v_sliced, mix_steps = sem("gate_exp"), sem("gate_steps"), sem("v_sliced"), sem("mix_steps")

        norm_tiles, norm_sems = (stats, mv, varr, rstd, newton, carrier), (norm_steps, var_ready, rsqrt_ready)
        p_ready, p_ahead = (clipped, 0) if latent else (exp_done, AHEAD)
        CONSTANTS = {"latent": 8, "cross": 5, "self": 4 + EXPERTS}[kind]
        MADE = {"latent": 5, "cross": 10, "self": 12}[kind]
        RANK_STEPS = 1 + 4 * (EXPERTS - 1)
        GATE_STEPS = RANK_STEPS + 4 + QT * (2 * EXPERTS - 1)
        MIX_STEPS = 2 * EXPERTS

        head = [("norm_x",)] + ([("norm_c",)] if latent else []) + [("split",), ("split",)]
        head += [("turn", "x", ch, 0) for ch in range(2)]
        if own:
            head += [("gate", t) for t in range(QT)] + [("masks",)]
        else:
            head += [("turn", "c", ch, g) for g in range(KT // 4) for ch in range(2)]
        head += step_plan(kind, KT, False, True, False)
        first_step = step_plan(kind, KT, True, True, False, split=True)
        step = step_plan(kind, KT, True, True, True, split=True)
        late_step = step_plan(kind, KT, True, True, True)
        last_step = step_plan(kind, KT, True, False, True)
        tail = step_plan(kind, KT, False, False, True)
        if own:
            tail += [("mix", t) for t in range(QT)] + [("mixT", t) for t in range(QT)]
        tail += [("out", t) for t in range(QT)]

        def walk(eng, do):
            place = Place()
            with turns(eng, B, place, [head, first_step] + [step] * (NP - 3) + [late_step, last_step, tail]) as b:
                do(place, b, -1, 1, head)
                do(place, b, 0, 0, first_step)
                loops = (NP - 3) // 2
                if loops:
                    with turns(eng, loops, place, [step, step]) as j:
                        do(place, b, 2 * j + 1, 1, step)
                        do(place, b, 2 * j + 2, 0, step)
                for p in range(1 + 2 * loops, NP - 2):
                    do(place, b, p, p % 2, step)
                do(place, b, NP - 2, NP % 2, late_step)
                do(place, b, NP - 1, 1 - NP % 2, last_step)
                do(place, b, NP, NP % 2, tail)

        def evacuated(eng, mark):
            for i in range(2):
                eng.wait_ge(free[i], mark[i] + 1)

        def norm_count(place):
            return place["norm_x"] * (ROUNDS * (3 * QT + 4)) + place["norm_c"] * (3 * KT + 4)

        def norm_rounds(place):
            return place["norm_x"] * ROUNDS + place["norm_c"]

        def add_up(eng, ops, place, h, c):
            steps = (NC - 1) * place.attends.value
            if c >= 1:
                eng.wait_ge(p_ready, place.attends.value * (2 * NC) + (2 * c + h + 1 + p_ahead))
                if c == 1:
                    eng.wait_ge(fold_done[h], place.attends.value + AHEAD)
                else:
                    eng.wait_ge(added[h], steps + (c - 1 + AHEAD))
                first = probs[h][0] if c == 1 else acc[h]
                ops.tensor_tensor(acc[h][:, :, :], first[:, :, :], probs[h][c % 2][:, :, :], ALU.add).then_inc(added[h], 1)
            if c == NC - 1:
                eng.wait_ge(added[h], steps + (NC - 1 + AHEAD))
                eng.wait_ge(normed, place["sum"] + AHEAD)
                ops.tensor_tensor(folded[h][:, :], acc[h][:, 0, :], acc[h][:, 1, :], ALU.add).then_inc(fold_done[h], 1)

        block = ctx.enter_context(nc.Block())

        @block.sync
        def _(sp):
            n_const = [0]

            def constant(dst, src, columns=False):
                sp.dma_start(dst, src, allow_slow_non_contiguous=columns).then_inc(const_loaded, 16)
                n_const[0] += 1

            if own:
                sp.wait_ge(const_set, 1)
                constant(WO[:, 0:2, :], weights["Wo"][0:256, :].rearrange("(c p) n -> p c n", p=P))
                constant(WO[0:64, 2, :], weights["Wo"][256:320, :])
                for e in range(EXPERTS):
                    constant(gates_raw[:, :, e * DH:(e + 1) * DH], weights["Wv"][e].rearrange("(c p) n -> p c n", p=P))
                for i, w in enumerate(("Ws", "Wd")):
                    at = NV + i * HEADS * EXPERTS
                    constant(gates_raw[:, :, at:at + HEADS * EXPERTS], weights[w].rearrange("(c p) n -> p c n", p=P))
            else:
                constant(WO[:, :, :], weights["Wo"].rearrange("(c p) n -> p c n", p=P))
                constant(bo[:, :], weights["bo"].rearrange("(a n) -> a n", a=1).broadcast_to([P, D]))
            if latent:
                constant(cos[:, :, :], weights["cos"].rearrange("(t p) n -> p t n", p=P))
                constant(sin[:, :, :], weights["sin"].rearrange("(t p) n -> p t n", p=P))
                for tile, g, b_ in ((gbx, "gx", "bx"), (gbc, "gc", "bc")):
                    constant(tile[:, 0, :], weights[g].rearrange("(c p) -> p c", p=P), columns=True)
                    constant(tile[:, 1, :], weights[b_].rearrange("(c p) -> p c", p=P), columns=True)
            if cross:
                for i, w in enumerate(("bq", "bk", "bv")):
                    constant(bqkv[:, i, :], weights[w].rearrange("(c p) -> p c", p=P), columns=True)
            assert n_const[0] == CONSTANTS

            def do(place, b, p, par, plan):
                splits = 0
                for item in plan:
                    if item[0] == "norm_x":
                        sp.wait_ge(x_stored, 16 * b + 16)
                        sp.dma_start(X[:, :, :], x_in[bass.ds(b * NQ, NQ), :].rearrange("(t p) d -> p t d", p=P))\
                          .then_inc(x_loaded, 16)
                        if not own:
                            sp.wait_ge(full, place.units.value + AHEAD)
                            sp.dma_start(C[:, :, :], context[bass.ds(b * KEYS, KEYS), :].rearrange("(t p) d -> p t d", p=P))\
                              .then_inc(c_loaded, 16)
                    elif item[0] == "split":
                        sp.wait_ge(w_split, place["split"] + 1)
                        at = splits * P if plan is head else (p + 2) * P
                        splits += 1
                        for i, (w, off) in enumerate(weights["slices"]):
                            sp.dma_start(WRAW[:, :, i * P:(i + 1) * P],
                                         w[:, bass.ds(at + off, P)].rearrange("(c p) n -> p c n", p=P)).then_inc(w_loaded, 16)
                    place.passed(item)
                    if item == ("out", QT - 1):
                        evacuated(sp, place.mark())
                        sp.dma_start(x_out[bass.ds(b * NQ, NQ), :].rearrange("(t p) d -> p t d", p=P), X[:, :, :])\
                          .then_inc(x_stored, 16)

            walk(sp, do)
            sp.wait_ge(x_stored, 16 * B + 16)

        @block.gpsimd
        def _(pool):
            nc.gpsimd.memset(WO[:, 2, :] if own else prime[:, :], 0.0).then_inc(const_set, 1)
            nc.gpsimd.memset(ident[:, :], 0.0).then_inc(const_set, 1)
            pool.wait_ge(const_set, 2)
            nc.gpsimd.affine_select(out=ident[:, :], in_=ident[:, :], compare_op=ALU.not_equal, fill=1.0, base=0,
                                    pattern=[[-1, P]], channel_multiplier=1).then_inc(const_made, 1)
            nc.gpsimd.memset(ones[:, :], 1.0).then_inc(const_made, 1)
            nc.gpsimd.memset(neghalf[:, :], -0.5).then_inc(const_made, 1)
            nc.gpsimd.memset(scale[:, :], SCALE).then_inc(const_made, 1)
            if shifted:
                nc.gpsimd.memset(spread[:, :].bitcast(fp32), 1.0 / DH).then_inc(const_made, 1)
                for i in range(2):
                    for h in range(2):
                        pool.wait_ge(const_made, 5 + 2 * i + h)
                        nc.gpsimd.memset(S2[i][AUX[h], h, :].bitcast(fp32), 1.0).then_inc(const_made, 1)
            pool.wait_ge(const_loaded, 16 * CONSTANTS)
            if latent:
                nc.gpsimd.tensor_scalar(nsin[:, :, :], sin[:, :, :], -1.0, None, ALU.mult).then_inc(const_made, 1)
            if cross:
                nc.gpsimd.tensor_scalar(bqkv[:, 0, :], bqkv[:, 0, :], SCALE, None, ALU.mult).then_inc(const_made, 1)
            if own:
                nc.gpsimd.memset(mixed[:, :, :], 0.0).then_inc(const_made, 1)
                nc.gpsimd.tensor_copy(gates_hi[:, :, :], gates_raw[:, :, :]).then_inc(const_made, 1)
                pool.wait_ge(const_made, MADE - 1)
                nc.gpsimd.tensor_tensor(gates_lo[:, :, :], gates_raw[:, :, :], gates_hi[:, :, :].bitcast(fp32),
                                        ALU.subtract).then_inc(const_made, 1)
            pool.wait_ge(const_made, MADE)
            for i, (s, k) in enumerate(((free[0], 1), (free[1], 1), (full, AHEAD), (w_split, 1), (exp_done, AHEAD),
                                        (av_done, AHEAD), (added[0], AHEAD), (added[1], AHEAD),
                                        (fold_done[0], AHEAD), (fold_done[1], AHEAD), (normed, AHEAD),
                                        (out_biased, AHEAD), (x_stored, 16))):
                nc.gpsimd.memset(primes[:, i:i + 1], 0.0).then_inc(s, k)

            def do(place, b, p, par, plan):
                splits = 0
                for item in plan:
                    if item[0] in ("norm_x", "norm_c"):
                        n = QT if item[0] == "norm_x" else KT
                        for r in range(ROUNDS if item[0] == "norm_x" else 1):
                            pool.wait_ge(var_ready, norm_rounds(place) + (r + 1))
                            nc.gpsimd.tensor_tensor(rstd[:, 0:n], varr[:, 0:n], neghalf[:, 0:n], ALU.pow)\
                              .then_inc(rsqrt_ready, 1)
                    elif item[0] == "split":
                        i = splits if plan is head else par
                        splits += 1
                        pool.wait_ge(w_loaded, 16 * len(weights["slices"]) * (place["split"] + 1))
                        pool.wait_ge(full, place.units.value + AHEAD)
                        nc.gpsimd.tensor_tensor(WRAW[:, :, 0:P], WRAW[:, :, 0:P],
                                                scale[:, :].unsqueeze(2).broadcast_to([P, 2, P]), ALU.mult).then_inc(w_scaled, 1)
                        pool.wait_ge(w_scaled, place["split"] + 1)
                        nc.gpsimd.tensor_tensor(WH[i][:, :, :], WRAW[:, :, :], ones[:, 0:2].unsqueeze(2).broadcast_to([P, 2, NW]),
                                                ALU.mult).then_inc(w_high, 1)
                        pool.wait_ge(w_high, place["split"] + 1)
                        nc.gpsimd.tensor_tensor(WL[i][:, :, :], WRAW[:, :, :], WH[i][:, :, :].bitcast(fp32), ALU.subtract)\
                          .then_inc(w_split, 1)
                    elif item[0] == "soft" and item[1] == 1:
                        add_up(pool, nc.gpsimd, place, 1, item[2])
                    elif item[0] == "max" and item[4]:
                        h = item[1]
                        pool.wait_ge(negtop_ready, place["top"] + 1)
                        nc.gpsimd.tensor_tensor(diag[h][:, :, :], ident[:, :].unsqueeze(1).broadcast_to([P, QT, P]),
                                                negtop[:, h, :].unsqueeze(2).broadcast_to([P, QT, P]), ALU.mult)\
                          .then_inc(diag_ready, 1)
                    place.passed(item)

            walk(pool, do)

        @block.scalar
        def _(act):
            act.wait_ge(const_made, MADE)
            waited = act.alloc_register(f"{name}_waited")
            act.reg_mov(waited, 0)

            def take_wait():
                act.reg_add(waited, waited, 1)

            def do(place, b, p, par, plan):
                nxt = 1 - par
                for item in plan:
                    u = item[0]
                    bank = ring[place.ring]
                    if u in Place.UNITS and u not in ("max", "out") and not (u == "sum" and not cross):
                        if u != "sum":
                            act.wait_ge(full, place.units.value + (1 + AHEAD))
                    taken = free[place.ring]
                    if u == "turn":
                        gb = {"x": gbx, "c": gbc}[item[1]] if latent else None
                        ch = item[2]
                        nc.scalar.activation(staging[place.ring][:, :], bank[:, :], ACT.Identity,
                                             scale=gb[:, 0, ch:ch + 1] if latent else 1.0,
                                             bias=gb[:, 1, ch:ch + 1] if latent else 0.0).then_inc(staged, 1)
                    elif u == "gate":
                        nc.scalar.activation(gated[:, item[1], :], bank[:, 0:NGATE], ACT.Copy).then_inc(taken, 1)
                    elif u == "masks":
                        evacuated(act, place.mark())
                        nc.scalar.activation(sigm[:, :, :], gated[:, :, NV:NV + HEADS * EXPERTS], ACT.Exp, scale=-1.0)\
                          .then_inc(gate_exp, 1)
                    elif u == "biases":
                        nc.scalar.activation(pair_bias[nxt][:, :].unsqueeze(2), bqkv[:, 0:2, bass.ds(p + 1, 1)], ACT.Copy)\
                          .then_inc(biases_ready, 1)
                    elif u == "vslice":
                        act.wait_ge(gate_steps, GATE_STEPS * (b + 1))
                        act.wait_ge(av_done, NC * place.attends.value + AHEAD)
                        take_wait()
                        nc.scalar.activation(VN[nxt][:, :, :], VALL[:, :, bass.ds((p + 1) * P, P)], ACT.Copy)\
                          .then_inc(v_sliced, 1)
                    elif u == "kv":
                        t = item[1]
                        src = bank[:, :].rearrange("p (s n) -> p s n", s=2)
                        if latent:
                            nc.scalar.activation(VN[nxt][:, 2 * t:2 * t + 2, :], src[:, :, 128:256], ACT.Copy)\
                              .then_inc(v_copied, 1)
                        else:
                            nc.scalar.activation(VN[nxt][:, 2 * t:2 * t + 2, :], src[:, :, :], ACT.Copy).then_inc(taken, 1)
                    elif u in ("k", "kT"):
                        cols = slice(item[1] * 512, item[1] * 512 + 512) if u == "kT" else slice(0, 512)
                        dsts = [(S, h) for h in range(2) for S in ([S1, S2] if shifted else [S1])]
                        for S, h in dsts:
                            last = nc.scalar.activation(S[nxt][MAIN[h], h, cols], bank[MAIN[h], :], ACT.Identity,
                                                        bias=pair_bias[nxt][MAIN[h], 1:2] if cross else 0.0)
                        last.then_inc(high, 1)
                    elif u == "q":
                        if cross:
                            act.wait_ge(biases_ready, place["biases"])
                        for h in range(2):
                            for rows in MAIN:
                                last = nc.scalar.activation(Q1[nxt][rows, h, :], bank[MAIN[h], :], ACT.Identity,
                                                            bias=pair_bias[nxt][MAIN[h], 0:1] if cross else 0.0)
                        last.then_inc(high, 1)
                    elif u == "shift":
                        h = item[1]
                        nc.scalar.activation(Q2[nxt][AUX[h], h, :], bank[AUX[h], :], ACT.Copy).then_inc(taken, 1)
                    elif u == "S":
                        _, h, c = item
                        act.wait_ge(s_full, place.attends.value * (2 * NC) + (2 * c + h + 1))
                        act.wait_ge(av_done, place.attends.value * NC + (c - 1 + AHEAD))
                        rel = max(NC - 2, 1) - (NC - 1) if c == 0 else 0 if c == 1 else 1
                        act.wait_ge(added[h], place.attends.value * (NC - 1) + (rel + AHEAD))
                        nc.scalar.activation(probs[h][c % 2][:, :, :], scores[h][:, :, :], ACT.Exp).then_inc(exp_done, 1)
                    elif u == "sum" and cross:
                        act.wait_ge(normed, place["sum"] + (1 + AHEAD))
                        take_wait()
                        nc.scalar.activation(OT[:, bass.ds(p - 1, 1), :], O32[:, :].unsqueeze(1), ACT.Identity,
                                             bias=bqkv[:, 2, bass.ds(p - 1, 1)]).then_inc(out_biased, 1)
                    elif u == "back":
                        take_wait()
                        nc.scalar.activation(natural[:, :, bass.ds((p - 1) * P, P)],
                                             bank[:, :].rearrange("p (t n) -> p t n", t=QT), ACT.Copy).then_inc(taken, 1)
                    elif u == "mixT":
                        nc.scalar.activation(mixedT[:, :, item[1] * P:(item[1] + 1) * P],
                                             bank[:, 0:3 * P].rearrange("p (c n) -> p c n", c=3), ACT.Copy).then_inc(taken, 1)
                    place.passed(item)

            walk(act, do)

        @block.vector
        def _(dve):
            dve.wait_ge(const_made, MADE)

            def masks(place, b):
                base = b * GATE_STEPS
                n = [0]

                def stepped(ins):
                    ins.then_inc(gate_steps, 1)
                    n[0] += 1
                    dve.wait_ge(gate_steps, base + n[0])

                G = gated[:, :, NV:NGATE].rearrange("p t (g e) -> p t g e", e=EXPERTS)
                rank_experts(nc, stepped, G, rank, over, EXPERTS)
                stepped(nc.vector.tensor_scalar(rank[:, :, :, :], rank[:, :, :, :], 1.5, None, ALU.is_lt))
                dve.wait_ge(gate_exp, b + 1)
                stepped(nc.vector.tensor_scalar(sigm[:, :, :], sigm[:, :, :], 1.0, None, ALU.add))
                stepped(nc.vector.reciprocal(sigm[:, :, :], sigm[:, :, :]))
                wv = rank[:, :, 0:HEADS, :]
                stepped(nc.vector.tensor_tensor(wv, wv, sigm[:, :, :].rearrange("p t (h e) -> p t h e", e=EXPERTS), ALU.mult))
                for t in range(QT):
                    V = VALL[:, t, :].rearrange("p (h k) -> p h k", h=HEADS)
                    for e in range(EXPERTS):
                        shape = [P, HEADS, DH]
                        stepped(nc.vector.tensor_tensor(V if e == 0 else prods[0][:, :, :],
                                                        gated[:, t, e * DH:(e + 1) * DH].unsqueeze(1).broadcast_to(shape),
                                                        rank[:, t, 0:HEADS, e:e + 1].broadcast_to(shape), ALU.mult))
                        if e:
                            stepped(nc.vector.tensor_tensor(V, V, prods[0][:, :, :], ALU.add))
                assert n[0] == GATE_STEPS

            def do(place, b, p, par, plan):
                nxt = 1 - par
                for item in plan:
                    u = item[0]
                    bank = ring[place.ring]
                    taken = free[place.ring]
                    bank_count = place.bank[place.ring].value
                    this_full = place.units.value + (1 + AHEAD)
                    if u == "norm_x":
                        dve.wait_ge(x_loaded, 16 * b + 16)
                        normalise(nc, dve, norm_tiles, norm_sems, lambda t: X[:, t, :], XN, QT, norm_count(place), norm_rounds(place))
                        if latent:
                            base = norm_count(place) + (3 * QT + 4)
                            dve.wait_ge(norm_steps, base)
                            normalise(nc, dve, norm_tiles, norm_sems, lambda t: XN[:, t, :], XN, QT, base, norm_rounds(place) + 1)
                    elif u == "norm_c":
                        dve.wait_ge(c_loaded, 16 * b + 16)
                        normalise(nc, dve, norm_tiles, norm_sems, lambda t: C[:, t, :], C, KT, norm_count(place), norm_rounds(place))
                    elif u == "turn":
                        _, src, ch, g = item
                        H, L = (XTH, XTL) if src == "x" else (CTH, CTL)
                        cols = slice(g * 512, g * 512 + 512)
                        dve.wait_ge(staged, place["turn"] + 1)
                        nc.vector.tensor_copy(H[:, ch, cols], staging[place.ring][:, :]).then_inc(turn_high, 1)
                        dve.wait_ge(turn_high, place["turn"] + 1)
                        nc.vector.tensor_tensor(L[:, ch, cols], staging[place.ring][:, :], H[:, ch, cols].bitcast(fp32),
                                                ALU.subtract).then_inc(taken, 1)
                    elif u == "masks":
                        evacuated(dve, place.mark())
                        masks(place, b)
                    elif u == "kv" and latent:
                        t = item[1]
                        rot1, rot2 = rot1s[place.ring], rot2s[place.ring]
                        tiles = slice(2 * t, 2 * t + 2)
                        K = bank[:, :].rearrange("p (s n) -> p s n", s=2)[:, :, 0:128]
                        K4 = K.rearrange("p s (g i) -> p s g i", i=32)
                        K5 = K.rearrange("p s (h f i) -> p s h f i", f=2, i=32)
                        R5 = rot2[:, :, :].rearrange("p s (h f i) -> p s h f i", f=2, i=32)
                        dve.wait_ge(taken, bank_count + 1)
                        dve.wait_ge(v_copied, place["kv"] + 1)
                        nc.vector.tensor_tensor(rot1[:, :, :].rearrange("p s (g i) -> p s g i", i=32), K4,
                                                cos[:, tiles, :].unsqueeze(2).broadcast_to([P, 2, 4, 32]), ALU.mult)\
                          .then_inc(rotated, 1)
                        for f, table in ((0, nsin), (1, sin)):
                            nc.vector.tensor_tensor(R5[:, :, :, f, :], K5[:, :, :, 1 - f, :],
                                                    table[:, tiles, :].unsqueeze(2).broadcast_to([P, 2, 2, 32]), ALU.mult)\
                              .then_inc(rotated, 1)
                        dve.wait_ge(rotated, 3 * place["kv"] + 3)
                        nc.vector.tensor_tensor(KR[:, tiles, :], rot1[:, :, :], rot2[:, :, :], ALU.add).then_inc(taken, 1)
                    elif u in ("k", "kT"):
                        cols = slice(item[1] * 512, item[1] * 512 + 512) if u == "kT" else slice(0, 512)
                        dve.wait_ge(high, place["k"] + place["kT"] + place["q"] + 1)
                        for h in range(2):
                            last = nc.vector.scalar_tensor_tensor(
                                out=S1[nxt][AUX[h], h, cols], in0=bank[MAIN[h], :],
                                scalar=pair_bias[nxt][MAIN[h], 1:2] if cross else 0.0,
                                in1=S1[nxt][MAIN[h], h, cols].bitcast(fp32), op0=ALU.add, op1=ALU.subtract)
                        last.then_inc(taken, 1)
                    elif u == "q":
                        dve.wait_ge(high, place["k"] + place["kT"] + place["q"] + 1)
                        for h in range(2):
                            for rows in (MAIN if latent else (MAIN[h],)):
                                last = nc.vector.scalar_tensor_tensor(
                                    out=Q2[nxt][rows, h, :], in0=bank[MAIN[h], :],
                                    scalar=pair_bias[nxt][MAIN[h], 0:1] if cross else 0.0,
                                    in1=Q1[nxt][MAIN[h], h, :].bitcast(fp32), op0=ALU.add, op1=ALU.subtract)
                        last.then_inc(taken, 1)
                    elif u == "max":
                        _, h, qt, i, is_last = item
                        dve.wait_ge(full, this_full)
                        nc.vector.reduce_max(part[:, h, qt, i:i + 1], bank[:, :], AX.X).then_inc(taken, 1)
                        if is_last:
                            dve.wait_ge(taken, bank_count + 2)
                            dve.wait_ge(free[1 - place.ring], place.bank[1 - place.ring].value + 1)
                            nc.vector.reduce_max(top[:, h, :], part[:, h, :, :], AX.X).then_inc(top_found, 1)
                            dve.wait_ge(top_found, place["top"] + 1)
                            nc.vector.tensor_scalar(negtop[:, h, :], top[:, h, :], -1.0, None, ALU.mult)\
                              .then_inc(negtop_ready, 1)
                    elif u == "soft":
                        _, h, c = item
                        if latent:
                            tile = probs[h][c % 2]
                            s = place.attends.value * (2 * NC) + (2 * c + h + 1)
                            dve.wait_ge(exp_done, s + AHEAD)
                            nc.vector.tensor_scalar(tile[:, :, :], tile[:, :, :], exp(CLIP), exp(-CLIP), ALU.min, ALU.max)\
                              .then_inc(clipped, 1)
                        if h == 0:
                            add_up(dve, nc.vector, place, 0, c)
                    elif u == "sum":
                        dve.wait_ge(full, this_full)
                        nc.vector.reciprocal(recip[:, :], bank[:, :]).then_inc(taken, 1)
                        dve.wait_ge(taken, bank_count + 2)
                        dve.wait_ge(av_done, NC * (place["sum"] + 1) + AHEAD)
                        if latent:
                            dst = OT[:, bass.ds(p - 1, 1), :]
                        else:
                            dst = O32[:, :].unsqueeze(1)
                        if cross:
                            dve.wait_ge(out_biased, place["sum"] + AHEAD)
                        nc.vector.tensor_tensor(dst, outT[nxt][:, :].unsqueeze(1), recip[:, :].unsqueeze(1), ALU.mult)\
                          .then_inc(normed, 1)
                    elif u == "mix":
                        t = item[1]
                        evacuated(dve, place.mark())
                        for e in range(EXPERTS):
                            m = t * EXPERTS + e
                            prod = prods[m % 2]
                            if m >= 2:
                                dve.wait_ge(mix_steps, MIX_STEPS * QT * b + 2 * (m - 1))
                            nc.vector.tensor_tensor(prod[:, :, :], natural[:, t, :].rearrange("p (h k) -> p h k", h=HEADS),
                                                    rank[:, t, HEADS:, e:e + 1].broadcast_to([P, HEADS, DH]), ALU.mult)\
                              .then_inc(mix_steps, 1)
                            dve.wait_ge(mix_steps, MIX_STEPS * QT * b + (2 * m + 1))
                            nc.vector.reduce_sum(mixed[:, t, e * DH:(e + 1) * DH],
                                                 prod[:, :, :].rearrange("p h k -> p k h"), AX.X).then_inc(mix_steps, 1)
                    elif u == "out":
                        t = item[1]
                        if t == 0 and not own:
                            nc.vector.tensor_tensor(X[:, :, :], X[:, :, :], bo[:, :].unsqueeze(1).broadcast_to([P, QT, D]),
                                                    ALU.add).then_inc(rows_biased, 1)
                            dve.wait_ge(rows_biased, b + 1)
                        dve.wait_ge(full, this_full)
                        nc.vector.tensor_tensor(X[:, t, :], bank[:, 0:D], X[:, t, :], ALU.add).then_inc(taken, 1)
                    place.passed(item)

            walk(dve, do)

        @block.tensor
        def _(pe):
            pe.wait_ge(const_made, MADE)

            def product(out, passes, start=True, stop=True):
                for i, (still, moving) in enumerate(passes):
                    last = nc.tensor.matmul(out, still, moving, start=start and i == 0, stop=stop and i == len(passes) - 1)
                return last

            def three(highs, lows, highs2, lows2):
                return [pair for a, al, w, wl in zip(highs, lows, highs2, lows2) for pair in ((a, w), (a, wl), (al, w))]

            def do(place, b, p, par, plan):
                nxt = 1 - par
                made = place.mark()
                kv_mark = None
                for item in plan:
                    u = item[0]
                    bank = ring[place.ring]
                    if u in Place.UNITS:
                        pe.wait_ge(free[place.ring], place.bank[place.ring].value + 1)
                    if u == "turn":
                        _, src, ch, g = item
                        if src == "x":
                            pe.wait_ge(norm_steps, norm_count(place))
                        elif cross:
                            pe.wait_ge(c_loaded, 16 * b + 16)
                        rows = XN if src == "x" else C
                        for k in range(4):
                            last = nc.tensor.transpose(bank[:, k * P:(k + 1) * P],
                                                       rows[:, 4 * g + k, ch * P:(ch + 1) * P], ident[:, :])
                        last.then_inc(full, 1)
                    elif u == "gate":
                        t = item[1]
                        evacuated(pe, place.mark())
                        ts = slice(t * P, (t + 1) * P)
                        product(bank[:, 0:NGATE], three(*([T[:, ch, ts] for ch in range(2)] for T in (XTH, XTL)),
                                                        *([T[:, ch, :] for ch in range(2)] for T in (gates_hi, gates_lo))))\
                            .then_inc(full, 1)
                    elif u == "kv":
                        t = item[1]
                        if t == 0:
                            pe.wait_ge(w_split, place["q"] + 2)
                            if plan is head:
                                evacuated(pe, place.mark())
                        for s in range(2):
                            ts = slice((2 * t + s) * P, (2 * t + s + 1) * P)
                            last = product(bank[:, s * 256:(s + 1) * 256],
                                           three(*([T[:, ch, ts] for ch in range(2)] for T in (CTH, CTL)),
                                                 *([T[nxt][:, ch, P:3 * P] for ch in range(2)] for T in (WH, WL))))
                        last.then_inc(full, 1)
                    elif u in ("q", "k"):
                        if u == "k":
                            pe.wait_ge(w_split, place["q"] + 2)
                        at = P if u == "k" else 0
                        product(bank[:, :], three(*([T[nxt][:, ch, at:at + P] for ch in range(2)] for T in (WH, WL)),
                                                  *([T[:, ch, :] for ch in range(2)] for T in (XTH, XTL)))).then_inc(full, 1)
                    elif u == "kT":
                        evacuated(pe, kv_mark)
                        for k in range(4):
                            t = 4 * item[1] + k
                            last = nc.tensor.transpose(bank[:, k * P:(k + 1) * P],
                                                       KR[:, t, :] if latent else VN[nxt][:, t, 0:P], ident[:, :])
                        last.then_inc(full, 1)
                    elif u == "max":
                        _, h, qt, i, _ = item
                        if (h, qt, i) == (0, 0, 0):
                            evacuated(pe, place.mark())
                        nc.tensor.matmul(bank[:, :], Q1[nxt][:, h, qt * P:(qt + 1) * P], S1[nxt][:, h, i * 512:(i + 1) * 512],
                                         start=True, stop=True).then_inc(full, 1)
                    elif u == "shift":
                        pe.wait_ge(diag_ready, place["shift"] + 1)
                        nc.tensor.matmul(bank[:, :], spread[:, :], diag[item[1]][:, :, :].rearrange("p t n -> p (t n)"),
                                         start=True, stop=True).then_inc(full, 1)
                    elif u == "S":
                        _, h, c = item
                        if c == 0 and h == 0:
                            evacuated(pe, made)
                        pe.wait_ge(exp_done, place.attends.value * (2 * NC) + (2 * c + h - 1 + AHEAD))
                        for k in range(2):
                            ks = slice((2 * c + k) * P, (2 * c + k + 1) * P)
                            last = product(scores[h][:, k, :], [(S1[par][:, h, ks], Q1[par][:, h, :]),
                                                                (S2[par][:, h, ks], Q2[par][:, h, :])])
                        last.then_inc(s_full, 1)
                    elif u == "AV":
                        _, c, k = item
                        if k == 0:
                            pe.wait_ge(p_ready, place.attends.value * (2 * NC) + (2 * c + 2 + p_ahead))
                            if c == 0:
                                pe.wait_ge(normed, place.attends.value + (AHEAD - 1))
                                if own:
                                    pe.wait_ge(v_sliced, place.attends.value + 1)
                        for h in range(2):
                            last = nc.tensor.matmul(outT[par][MAIN[h], :], VN[par][:, 2 * c + k, VC + h * DH:VC + (h + 1) * DH],
                                                    probs[h][c % 2][:, k, :], start=(c == 0 and k == 0),
                                                    stop=(c == NC - 1 and k == 1))
                        if k == 1:
                            last.then_inc(av_done, 1)
                    elif u == "sum":
                        for h in range(2):
                            pe.wait_ge(fold_done[h], place["sum"] + (1 + AHEAD))
                            last = nc.tensor.matmul(bank[MAIN[h], :], ones[:, :], folded[h][:, :], start=True, stop=True)
                        last.then_inc(full, 1)
                    elif u == "back":
                        pe.wait_ge(normed, place["back"] + (1 + AHEAD))
                        for t in range(QT):
                            last = nc.tensor.transpose(bank[:, t * P:(t + 1) * P], O32[:, t * P:(t + 1) * P], ident[:, :])
                        last.then_inc(full, 1)
                    elif u == "mixT":
                        t = item[1]
                        pe.wait_ge(mix_steps, MIX_STEPS * (QT * b + (t + 1)))
                        for c in range(3):
                            last = nc.tensor.transpose(bank[:, c * P:(c + 1) * P], mixed[:, t, c * P:(c + 1) * P], ident[:, :])
                        last.then_inc(full, 1)
                    elif u == "out":
                        t = item[1]
                        ts = slice(t * P, (t + 1) * P)
                        if t == 0:
                            if own:
                                evacuated(pe, place.mark())
                            else:
                                pe.wait_ge(normed if latent else out_biased, place["sum"] + AHEAD)
                        O, chunks = (mixedT, 3) if own else (OT, NP)
                        product(bank[:, 0:D], [(O[:, c, ts], WO[:, c, :]) for c in range(chunks)]).then_inc(full, 1)
                    place.passed(item)
                    if u == "kv":
                        kv_mark = place.mark()

            walk(pe, do)



def expert_layer(nc, name, x_in, x_out, weights, B):
    fp32, f32r = mybir.dt.float32, mybir.dt.float32r
    ALU, ACT, AX = mybir.AluOpType, mybir.ActivationFunctionType, mybir.AxisListType
    E = ROUTED
    WIDE = E * D
    BANKS = 4
    SETUP = 2 * E
    PER_BATCH = QT * E // 2

    ctx = ExitStack()
    with ctx:
        def sb(label, shape, dt=fp32):
            return ctx.enter_context(nc.sbuf_tensor(f"{name}_{label}", shape, dt))

        def sem(label):
            return ctx.enter_context(nc.semaphore(f"{name}_{label}"))

        X, XN = sb("X", [P, QT, D]), sb("XN", [P, QT, D])
        XT = [sb(f"XT{part}", [P, 2, NQ], f32r) for part in ("high", "low")]
        raw = sb("raw", [P, 2 * E, D])
        W = [sb(f"W{part}", [P, 2, WIDE], f32r) for part in ("high", "low")]
        router_raw = sb("router_raw", [P, 2, E])
        router = [sb(f"router_{part}", [P, 2, E], f32r) for part in ("high", "low")]
        router_b = sb("router_b", [P, E])
        bias_raw, bias_high = sb("bias_raw", [64, WIDE]), sb("bias_high", [64, WIDE], f32r)
        bias, ones = sb("bias", [P, WIDE], f32r), sb("ones", [P, P], f32r)
        ident, neghalf = sb("ident", [P, P]), sb("neghalf", [P, QT])
        tiles = (sb("stats", [P, QT, 6]), sb("mv", [P, QT, 2]), sb("varr", [P, QT]), sb("rstd", [P, QT]),
                 [sb(f"newton{i}", [P, QT]) for i in range(4)], sb("carrier", [P, 1]))
        varr, rstd = tiles[2], tiles[3]
        logits, less = sb("logits", [P, QT, 1, E]), sb("less", [P, QT, E])
        rank, over = sb("rank", [P, QT, 1, E]), sb("over", [P, QT, 1, E])
        top, total, weight = sb("top", [P, QT]), sb("total", [P, QT]), sb("weight", [P, QT])
        pick = sb("pick", [P, QT, E])

        turned = [ctx.enter_context(nc.psum_tensor(f"{name}_turned{i}", [P, NQ], fp32)) for i in range(2)]
        routed = ctx.enter_context(nc.psum_tensor(f"{name}_routed", [P, QT, E], fp32))
        ring = [ctx.enter_context(nc.psum_tensor(f"{name}_ring{i}", [P, 512], fp32)) for i in range(BANKS)]

        const_loaded, const_made, router_split = sem("const_loaded"), sem("const_made"), sem("router_split")
        bias_steps = sem("bias_steps")
        x_loaded, x_stored = sem("x_loaded"), sem("x_stored")
        norm_steps, var_ready, rsqrt_ready = sem("norm_steps"), sem("var_ready"), sem("rsqrt_ready")
        w_full, w_high = sem("w_full"), sem("w_high")
        free = [sem(f"free{i}") for i in range(BANKS)]
        turn_full, turn_high, turn_done = sem("turn_full"), sem("turn_high"), sem("turn_done")
        route_full, route_steps, exp_done = sem("route_full"), sem("route_steps"), sem("exp_done")
        full, first_added = sem("full"), sem("first_added")

        ROUTE_STEPS = 3 + (4 * (E - 1) + 1) + 4
        NORM_STEPS = 3 * QT + 4
        block = ctx.enter_context(nc.Block())

        @block.sync
        def _(sp):
            sp.dma_start(raw[:, :, :], weights["L0_ffn_expert_w"].rearrange("e (c p) d -> p (e c) d", p=P))\
              .then_inc(const_loaded, 16)
            sp.dma_start(router_b[:, :], weights["L0_ffn_router_b"].rearrange("(a n) -> a n", a=1).broadcast_to([P, E]))\
              .then_inc(const_loaded, 16)
            for c in range(2):
                sp.dma_start(router_raw[:, c, :], weights["L0_ffn_router_w"][:, c * P:(c + 1) * P].rearrange("e p -> p e"),
                             allow_slow_non_contiguous=True).then_inc(const_loaded, 16)
            for row in (0, 32):
                sp.dma_start(bias_raw[row:row + 1, :], weights["L0_ffn_expert_b"].rearrange("(a e) d -> a (e d)", a=1))\
                  .then_inc(const_loaded, 16)
            sp.wait_ge(const_made, 1)
            with sp.Fori(0, B) as b:
                sp.wait_ge(x_stored, 16 * b + 16)
                sp.dma_start(X[:, :, :], x_in[bass.ds(b * NQ, NQ), :].rearrange("(t p) d -> p t d", p=P)).then_inc(x_loaded, 16)
                for i in range(BANKS):
                    sp.wait_ge(free[i], (SETUP + PER_BATCH) // BANKS + (PER_BATCH // BANKS) * b)
                sp.dma_start(x_out[bass.ds(b * NQ, NQ), :].rearrange("(t p) d -> p t d", p=P), X[:, :, :]).then_inc(x_stored, 16)
            sp.wait_ge(x_stored, 16 * B + 16)

        @block.gpsimd
        def _(pool):
            nc.gpsimd.memset(ident[:, :], 0.0).then_inc(const_made, 1)
            nc.gpsimd.memset(bias[:, :].bitcast(fp32), 0.0).then_inc(const_made, 1)
            nc.gpsimd.memset(ones[:, :].bitcast(fp32), 1.0).then_inc(const_made, 1)
            nc.gpsimd.memset(neghalf[:, :], -0.5).then_inc(x_stored, 16)
            pool.wait_ge(const_made, 3)
            nc.gpsimd.affine_select(out=ident[:, :], in_=ident[:, :], compare_op=ALU.not_equal, fill=1.0, base=0,
                                    pattern=[[-1, P]], channel_multiplier=1).then_inc(const_made, 1)
            pool.wait_ge(const_made, 4)
            pool.wait_ge(x_stored, 16)
            with pool.Fori(0, B) as b:
                pool.wait_ge(var_ready, b + 1)
                nc.gpsimd.tensor_tensor(rstd[:, :], varr[:, :], neghalf[:, :], ALU.pow).then_inc(rsqrt_ready, 1)

        @block.scalar
        def _(act):
            for u in range(SETUP):
                ch, pair = u % 2, u // 2
                act.wait_ge(w_full, u + 1)
                nc.scalar.activation(W[0][:, ch, pair * 256:pair * 256 + 256], ring[u % BANKS][:, 0:256], ACT.Copy)\
                  .then_inc(w_high, 1)
            with act.Fori(0, B) as b:
                for ch in range(2):
                    act.wait_ge(turn_full, 2 * b + (ch + 1))
                    nc.scalar.activation(XT[0][:, ch, :], turned[ch][:, :], ACT.Copy).then_inc(turn_high, 1)
                act.wait_ge(route_steps, ROUTE_STEPS * b + 3)
                nc.scalar.activation(less[:, :, :], less[:, :, :], ACT.Exp).then_inc(exp_done, 1)

        @block.vector
        def _(dve):
            dve.wait_ge(const_made, 4)
            dve.wait_ge(const_loaded, 96)
            nc.vector.tensor_copy(router[0][:, :, :], router_raw[:, :, :]).then_inc(router_split, 1)
            dve.wait_ge(router_split, 1)
            nc.vector.tensor_tensor(router[1][:, :, :], router_raw[:, :, :], router[0][:, :, :].bitcast(fp32), ALU.subtract)\
              .then_inc(router_split, 1)
            nc.vector.tensor_copy(bias[0:1, :], bias_raw[0:1, :]).then_inc(bias_steps, 1)
            nc.vector.tensor_copy(bias_high[32:33, :], bias_raw[32:33, :]).then_inc(bias_steps, 1)
            dve.wait_ge(bias_steps, 2)
            nc.vector.tensor_tensor(bias[32:33, :], bias_raw[32:33, :], bias_high[32:33, :].bitcast(fp32), ALU.subtract)\
              .then_inc(bias_steps, 1)
            for u in range(SETUP):
                ch, pair = u % 2, u // 2
                dve.wait_ge(w_high, u + 1)
                nc.vector.tensor_tensor(W[1][:, ch, pair * 256:pair * 256 + 256], ring[u % BANKS][:, 0:256],
                                        W[0][:, ch, pair * 256:pair * 256 + 256].bitcast(fp32), ALU.subtract)\
                  .then_inc(free[u % BANKS], 1)
            with dve.Fori(0, B) as b:
                dve.wait_ge(x_loaded, 16 * b + 16)
                normalise(nc, dve, tiles, (norm_steps, var_ready, rsqrt_ready), lambda t: X[:, t, :], XN, QT,
                          NORM_STEPS * b, b)
                for ch in range(2):
                    dve.wait_ge(turn_high, 2 * b + (ch + 1))
                    nc.vector.tensor_tensor(XT[1][:, ch, :], turned[ch][:, :], XT[0][:, ch, :].bitcast(fp32), ALU.subtract)\
                      .then_inc(turn_done, 1)
                n = [0]

                def stepped(ins):
                    ins.then_inc(route_steps, 1)
                    n[0] += 1
                    dve.wait_ge(route_steps, ROUTE_STEPS * b + n[0])

                dve.wait_ge(route_full, b + 1)
                stepped(nc.vector.tensor_tensor(logits[:, :, 0, :], routed[:, :, :],
                                                router_b[:, :].unsqueeze(1).broadcast_to([P, QT, E]), ALU.add))
                stepped(nc.vector.reduce_max(top[:, :], logits[:, :, 0, :], AX.X))
                stepped(nc.vector.tensor_tensor(less[:, :, :], logits[:, :, 0, :],
                                                top[:, :].unsqueeze(2).broadcast_to([P, QT, E]), ALU.subtract))
                rank_experts(nc, stepped, logits, rank, over, E)
                dve.wait_ge(exp_done, b + 1)
                stepped(nc.vector.reduce_sum(total[:, :], less[:, :, :], AX.X))
                stepped(nc.vector.reciprocal(weight[:, :], total[:, :]))
                stepped(nc.vector.tensor_scalar(pick[:, :, :], rank[:, :, 0, :], 0.5, None, ALU.is_lt))
                stepped(nc.vector.tensor_tensor(pick[:, :, :], pick[:, :, :],
                                                weight[:, :].unsqueeze(2).broadcast_to([P, QT, E]), ALU.mult))
                assert n[0] == ROUTE_STEPS
                for k in range(PER_BATCH):
                    t, pair = k // (E // 2), k % (E // 2)
                    dve.wait_ge(full, PER_BATCH * b + (k + 1))
                    if k:
                        dve.wait_ge(free[(k - 1) % BANKS], (PER_BATCH // BANKS) * b + (SETUP // BANKS + (k - 1) // BANKS + 1))
                    for i in range(2):
                        e = 2 * pair + i
                        ins = nc.vector.scalar_tensor_tensor(out=X[:, t, :], in0=ring[k % BANKS][:, i * D:(i + 1) * D],
                                                             scalar=pick[:, t, e:e + 1], in1=X[:, t, :],
                                                             op0=ALU.mult, op1=ALU.add)
                        if i == 0:
                            ins.then_inc(first_added, 1)
                            dve.wait_ge(first_added, PER_BATCH * b + (k + 1))
                        else:
                            ins.then_inc(free[k % BANKS], 1)

        @block.tensor
        def _(pe):
            pe.wait_ge(const_made, 4)
            pe.wait_ge(const_loaded, 96)
            for u in range(SETUP):
                ch, e = u % 2, u // 2
                if u >= BANKS:
                    pe.wait_ge(free[u % BANKS], u // BANKS)
                for c in range(2):
                    last = nc.tensor.transpose(ring[u % BANKS][:, c * P:(c + 1) * P], raw[:, 2 * e + c, ch * P:(ch + 1) * P],
                                               ident[:, :])
                last.then_inc(w_full, 1)
            pe.wait_ge(router_split, 2)
            pe.wait_ge(bias_steps, 3)
            with pe.Fori(0, B) as b:
                pe.wait_ge(norm_steps, NORM_STEPS * b + NORM_STEPS)
                for ch in range(2):
                    for t in range(QT):
                        last = nc.tensor.transpose(turned[ch][:, t * P:(t + 1) * P], XN[:, t, ch * P:(ch + 1) * P], ident[:, :])
                    last.then_inc(turn_full, 1)
                pe.wait_ge(turn_done, 2 * b + 2)
                for t in range(QT):
                    ts = slice(t * P, (t + 1) * P)
                    for i, (a, w, ch) in enumerate([(a, w, ch) for ch in range(2) for a, w in ((0, 0), (0, 1), (1, 0))]):
                        last = nc.tensor.matmul(routed[:, t, :], XT[a][:, ch, ts], router[w][:, ch, :],
                                                start=(i == 0), stop=(i == 5))
                last.then_inc(route_full, 1)
                for k in range(PER_BATCH):
                    t, pair = k // (E // 2), k % (E // 2)
                    ts, es = slice(t * P, (t + 1) * P), slice(pair * 512, pair * 512 + 512)
                    pe.wait_ge(free[k % BANKS], (PER_BATCH // BANKS) * b + (SETUP // BANKS + k // BANKS))
                    nc.tensor.matmul(ring[k % BANKS][:, :], ones[:, :], bias[:, es], start=True, stop=False)
                    for i, (a, w, ch) in enumerate([(a, w, ch) for ch in range(2) for a, w in ((0, 0), (0, 1), (1, 0))]):
                        last = nc.tensor.matmul(ring[k % BANKS][:, :], XT[a][:, ch, ts], W[w][:, ch, es], start=False,
                                                stop=(i == 5))
                    last.then_inc(full, 1)


def latent_weights(i):
    return {"slices": [(i["L0_xattn_Wq"], 0), (i["L0_xattn_Wkv"], 0), (i["L0_xattn_Wkv"], 1024)],
            "Wo": i["L0_xattn_Wo"], "bo": i["L0_xattn_bo"], "cos": i["L0_xattn_cos"], "sin": i["L0_xattn_sin"],
            "gx": i["L0_xattn_ln_lat_g"], "bx": i["L0_xattn_ln_lat_b"], "gc": i["L0_xattn_ln_ctx_g"],
            "bc": i["L0_xattn_ln_ctx_b"]}


def cross_weights(i):
    flat = {w: i[f"L1_xattn_{w}"].rearrange("d h k -> d (h k)") for w in ("Wq", "Wk", "Wv")}
    return {"slices": [(flat["Wq"], 0), (flat["Wk"], 0), (flat["Wv"], 0)],
            "Wo": i["L1_xattn_Wo"].rearrange("h k d -> (h k) d"), "bo": i["L1_xattn_bo"],
            **{b: i[f"L1_xattn_{b}"].rearrange("h k -> (h k)") for b in ("bq", "bk", "bv")}}


def self_weights(i):
    return {"slices": [(i["L1_ffn_Wq"], 0), (i["L1_ffn_Wk"], 0)], "Wo": i["L1_ffn_Wo"].rearrange("e k d -> (e k) d"),
            "Wv": i["L1_ffn_Wv"], "Ws": i["L1_ffn_Ws"], "Wd": i["L1_ffn_Wd"]}


def build(nc, ins, out):
    B, S, _ = ins["x"].shape
    assert S == NQ
    KEYS = ins["ctx_1024"].shape[1]
    between = [nc.dram_tensor(f"x_after_{i}", (B * S, D), mybir.dt.float32).ap() for i in range(3)]
    x, y = ins["x"].rearrange("b n d -> (b n) d"), out.rearrange("b n d -> (b n) d")
    context = ins["ctx_1024"].rearrange("b n d -> (b n) d")
    attention_layer(nc, "latent", "latent", x, between[0], context, latent_weights(ins), B, 8, KEYS // P)
    expert_layer(nc, "experts", between[0], between[1], ins, B)
    attention_layer(nc, "cross", "cross", between[1], between[2], context, cross_weights(ins), B, 8, KEYS // P)
    attention_layer(nc, "self", "self", between[2], y, None, self_weights(ins), B, 4, S // P)


_INS = ["x", "ctx_1024", "L0_xattn_cos", "L0_xattn_sin", "L0_xattn_ln_lat_g", "L0_xattn_ln_lat_b", "L0_xattn_ln_ctx_g",
        "L0_xattn_ln_ctx_b", "L0_xattn_Wq", "L0_xattn_Wkv", "L0_xattn_Wo", "L0_xattn_bo", "L0_ffn_router_w",
        "L0_ffn_router_b", "L0_ffn_expert_w", "L0_ffn_expert_b", "L1_xattn_Wq", "L1_xattn_bq", "L1_xattn_Wk",
        "L1_xattn_bk", "L1_xattn_Wv", "L1_xattn_bv", "L1_xattn_Wo", "L1_xattn_bo", "L1_ffn_Wq", "L1_ffn_Wk", "L1_ffn_Ws",
        "L1_ffn_Wd", "L1_ffn_Wv", "L1_ffn_Wo"]


def kernel(**inputs):
    import numpy as _np
    import concourse.bacc as _bacc
    from concourse import mybir as _mybir
    from concourse.bass_utils import run_bass_kernel_spmd as _run

    nc = _bacc.Bacc("TRN2", target_bir_lowering=False, num_devices=1)
    arrays, ins = {}, {}
    for name in _INS:
        a = _np.ascontiguousarray(inputs[name])
        arrays[f"in_{name}_dram"] = a
        ins[name] = nc.dram_tensor(f"in_{name}_dram", a.shape, _mybir.dt.from_np(a.dtype), kind="ExternalInput").ap()
    shape = inputs["x"].shape
    out = nc.dram_tensor("out_0_dram", shape, _mybir.dt.float32, kind="ExternalOutput").ap()
    build(nc, ins, out)
    r = _run(nc, [arrays], core_ids=[0])
    return r.results[0]["out_0_dram"]
```

```python
from contextlib import ExitStack, contextmanager
from math import exp

import concourse.bass as bass
from concourse import mybir

P = 128
D = 256
NQ = 512
QT = NQ // P
DH = 64
EPS = 1e-5
CLIP = 11.0
SCALE = DH ** -0.5
EXPERTS = 5
ROUTED = 8
AHEAD = 2
BEHIND = {"latent": [1, 0, 0, 1, 1, 1, 0, 1, 1, 0, 1, 1, 0, 0, 0, 0], "cross": [2, 1, 0, 7, 0, 0, 2, 2, 3, 2, 2, 2, 2, 2, 2, 1],
          "self": [2, 1, 1, 0, 5, 4, 2, 0]}
SUM_AFTER = {"latent": 1, "cross": 3, "self": 2}
FINISH_AFTER = {"latent": 0, "cross": 7, "self": 8}


class Count:

    def __init__(self):
        self.turns, self.here = 0, 0

    @property
    def value(self):
        return self.turns + self.here


class Place:

    UNITS = ("turn", "gate", "kv", "k", "kT", "q", "max", "shift", "sum", "back", "mixT", "out")
    KINDS = UNITS + ("norm_x", "norm_c", "split", "top", "biases", "biased", "load", "masks", "vslice", "kept")

    def __init__(self):
        self.n = {kind: Count() for kind in self.KINDS}
        self.units = Count()
        self.bank = [Count(), Count()]
        self.attends = Count()

    def counts(self):
        return [self.units, *self.bank, self.attends, *self.n.values()]

    def __getitem__(self, kind):
        return self.n[kind].value

    @property
    def ring(self):
        return self.units.here % 2

    def passed(self, item):
        kind = item[0]
        if kind in self.UNITS:
            self.bank[self.ring].here += 1
            self.units.here += 1
        if kind == "end":
            self.attends.here += 1
        elif kind in self.n:
            self.n[kind].here += 1
        if kind == "max" and item[4]:
            self.n["top"].here += 1

    def mark(self):
        return [bank.value for bank in self.bank]


@contextmanager
def turns(eng, trips, place, plans):
    dry = Place()
    for plan in plans:
        for item in plan:
            dry.passed(item)
    gain = [count.here for count in dry.counts()]
    assert gain[0] % 2 == 0, "a turn leaves the ring's banks in step"
    was = [(count.turns, count.here) for count in place.counts()]
    with eng.Fori(0, trips) as i:
        for count, k in zip(place.counts(), gain):
            if k:
                count.turns = count.turns + i * k
        yield i
        for count, k, (_, here) in zip(place.counts(), gain, was):
            assert count.here == here + k
    for count, k, (turned, here) in zip(place.counts(), gain, was):
        count.turns, count.here = turned, here + trips * k


def attend_order(NC, late):
    order = []
    for c in range(NC):
        order += [[("S", 0, c)], [("S", 1, c), ("soft", 0, c)]]
        if c or late:
            order += [[("AV", c - 1, 0), ("soft", 1, c)], [("AV", c - 1, 1)]]
        else:
            order[-1] += [("soft", 1, c)]
    order[-1] += [("end",)]
    return order


def prepare_order(kind, KT):
    if kind == "self":
        units = [("k",), ("q",), ("vslice",)]
    else:
        units = [("q",)] + [("kv", t) for t in range(KT // 2)] + [("kT", i) for i in range(KT // 4)]
    if kind == "latent":
        return units
    if kind == "cross":
        units = [("biases",)] + units
    halves = KT // 4
    maxima = [[("max", h, qt, i, (qt, i) == (QT - 1, halves - 1)) for qt in range(QT) for i in range(halves)]
              for h in range(2)]
    mid = len(maxima[1]) // 2
    return units + maxima[0] + maxima[1][:mid] + [("shift", 0)] + maxima[1][mid:] + [("shift", 1)]


def enter_order(kind, KT):
    turn_x = [("turn", "x", ch, 0) for ch in range(2)]
    if kind == "self":
        return turn_x + [("turned",)] + [("gate", t) for t in range(QT)] + [("masks",)]
    turn_c = [("turn", "c", ch, g) for g in range(KT // 4) for ch in range(2)]
    return turn_x + ([("norm_c",)] if kind == "latent" else []) + turn_c + [("turned",)]


def step_plan(kind, KT, attend, prepare, finish, split=False, enter=False):
    begin = [("split", None)] if split else []
    finishing = [("sum",)] + {"self": [("back",)], "cross": [("biased",)], "latent": []}[kind] if finish else []
    preparing = prepare_order(kind, KT) if prepare else []
    if not attend:
        return begin + ([("AV", -1, 0), ("AV", -1, 1)] if finish else []) + finishing + preparing
    order, counts = attend_order(KT // 2, finish), list(BEHIND[kind])
    if not finish:
        counts = [counts[0], sum(counts[1:4])] + counts[4:]
    at = SUM_AFTER[kind]
    between = preparing[:at] + finishing[:1] + preparing[at:]
    at = FINISH_AFTER[kind]
    between = between[:at] + finishing[1:] + between[at:]
    if not preparing:
        counts = [0, 0, 0, len(finishing)]
    if enter:
        order[3] = order[3] + finishing[:1]
        order[5] = order[5] + finishing[1:]
        between = enter_order(kind, KT) + preparing
        n = len(between)
        counts = [(i + 1) * n // len(order) - i * n // len(order) for i in range(len(order))]
    plan = begin
    for i, items in enumerate(order):
        n = counts[i] if i < len(counts) else 0
        plan = plan + items + between[:n]
        between = between[n:]
    assert not between
    return plan


def normalise(nc, dve, tiles, sems, src, dst, n, base, rounds):
    ALU = mybir.AluOpType
    stats, mv, varr, rstd, newton, carrier = tiles
    norm_steps, var_ready, rsqrt_ready = sems
    for t in range(n):
        nc.vector.bn_stats(stats[:, t, :], src(t)).then_inc(norm_steps, 1)
    dve.wait_ge(norm_steps, base + n)
    nc.vector.memset(carrier[:, :], 0.0)
    for t in range(n):
        nc.vector.bn_aggr(mv[:, t, :], stats[:, t, :]).then_inc(norm_steps, 1)
    dve.wait_ge(norm_steps, base + 2 * n)
    nc.vector.tensor_scalar(varr[:, 0:n], mv[:, 0:n, 1], EPS, None, ALU.add).then_inc(var_ready, 1)
    dve.wait_ge(rsqrt_ready, rounds + 1)
    nc.vector.tensor_tensor(newton[0][:, 0:n], rstd[:, 0:n], rstd[:, 0:n], ALU.mult).then_inc(norm_steps, 1)
    dve.wait_ge(norm_steps, base + (2 * n + 1))
    nc.vector.tensor_tensor(newton[1][:, 0:n], newton[0][:, 0:n], varr[:, 0:n], ALU.mult).then_inc(norm_steps, 1)
    dve.wait_ge(norm_steps, base + (2 * n + 2))
    nc.vector.tensor_scalar(newton[2][:, 0:n], newton[1][:, 0:n], -0.5, 1.5, ALU.mult, ALU.add).then_inc(norm_steps, 1)
    dve.wait_ge(norm_steps, base + (2 * n + 3))
    nc.vector.tensor_tensor(newton[3][:, 0:n], newton[2][:, 0:n], rstd[:, 0:n], ALU.mult).then_inc(norm_steps, 1)
    dve.wait_ge(norm_steps, base + (2 * n + 4))
    for t in range(n):
        nc.vector.tensor_scalar(dst[:, t, :], src(t), mv[:, t, 0:1], newton[3][:, t:t + 1], ALU.subtract, ALU.mult)\
          .then_inc(norm_steps, 1)


def rank_experts(nc, stepped, logits, rank, over, count):
    ALU = mybir.AluOpType
    stepped(nc.vector.memset(rank[:, :, :, :], 0.0))
    for j in range(count):
        for lo, hi, op in ((0, j, ALU.is_gt), (j + 1, count, ALU.is_ge)):
            if lo < hi:
                shape = [*logits.shape[:3], hi - lo]
                stepped(nc.vector.tensor_tensor(over[:, :, :, lo:hi], logits[:, :, :, j:j + 1].broadcast_to(shape),
                                                logits[:, :, :, lo:hi], op))
                stepped(nc.vector.tensor_tensor(rank[:, :, :, lo:hi], rank[:, :, :, lo:hi], over[:, :, :, lo:hi], ALU.add))


def attention_layer(nc, name, kind, x_in, x_out, context, weights, B, NP, KT):
    fp32, f32r = mybir.dt.float32, mybir.dt.float32r
    ALU, ACT, AX = mybir.AluOpType, mybir.ActivationFunctionType, mybir.AxisListType
    latent, cross, own = kind == "latent", kind == "cross", kind == "self"
    shifted = not latent
    NC = KT // 2
    KEYS = KT * P
    HALVES = KEYS // 512
    HEADS = 2 * NP
    NW = P * len(weights["slices"])
    NV = EXPERTS * DH
    NGATE = NV + 2 * HEADS * EXPERTS
    ROUNDS = 2 if latent else 1
    MAIN = (slice(0, 64), slice(64, 128))
    AUX = (slice(64, 128), slice(0, 64))

    ctx = ExitStack()
    with ctx:
        def sb(label, shape, dt=fp32):
            return ctx.enter_context(nc.sbuf_tensor(f"{name}_{label}", shape, dt))

        def sem(label):
            return ctx.enter_context(nc.semaphore(f"{name}_{label}"))

        X, XN = sb("X", [P, QT, D]), sb("XN", [P, QT, D])
        XTH, XTL = sb("XTH", [P, 2, NQ], f32r), sb("XTL", [P, 2, NQ], f32r)
        staging = [sb(f"staging{i}", [P, 512]) for i in range(2)]
        WRAW = sb("WRAW", [P, 2, NW])
        WH = [sb(f"WH{i}", [P, 2, NW], f32r) for i in range(2)]
        WL = [sb(f"WL{i}", [P, 2, NW], f32r) for i in range(2)]
        S1 = [sb(f"S1{i}", [P, 2, KEYS], f32r) for i in range(2)]
        S2 = [sb(f"S2{i}", [P, 2, KEYS], f32r) for i in range(2)] if shifted else S1
        Q1 = [sb(f"Q1{i}", [P, 2, NQ], f32r) for i in range(2)]
        Q2 = [sb(f"Q2{i}", [P, 2, NQ], f32r) for i in range(2)]
        probs = [[sb(f"probs{h}{i}", [P, 2, NQ]) for i in range(2)] for h in range(2)]
        acc = [sb(f"acc{h}", [P, 2, NQ]) for h in range(2)]
        folded = [sb(f"folded{h}", [P, NQ]) for h in range(2)]
        sums, recip = sb("sums", [P, NQ]), sb("recip", [P, NQ])
        ident, ones = sb("ident", [P, P]), sb("ones", [P, DH])
        neghalf, scale = sb("neghalf", [P, KT]), sb("scale", [P, 2])
        stats, mv = sb("stats", [P, KT, 6]), sb("mv", [P, KT, 2])
        varr, rstd = sb("varr", [P, KT]), sb("rstd", [P, KT])
        newton = [sb(f"newton{i}", [P, KT]) for i in range(4)]
        prime, carrier, primes = sb("prime", [P, 1]), sb("carrier", [P, 1]), sb("primes", [P, 16])
        VN = [sb(f"VN{i}", [P, KT, 256 if cross else 128]) for i in range(2)]
        VC = 128 if cross else 0
        if not own:
            C = sb("C", [P, KT, D])
            CTH, CTL = sb("CTH", [P, 2, KEYS], f32r), sb("CTL", [P, 2, KEYS], f32r)
            OT = sb("OT", [P, NP, NQ])
            WO = sb("WO", [P, NP, D])
            bo = sb("bo", [P, D])
        if latent:
            KR = sb("KR", [P, KT, P])
            cos, sin, nsin = (sb(n, [P, KT, 32]) for n in ("cos", "sin", "nsin"))
            rot1s, rot2s = ([sb(f"{n}{i}", [P, 2, P]) for i in range(2)] for n in ("rot1", "rot2"))
            gbx, gbc = sb("gbx", [P, 2, 2]), sb("gbc", [P, 2, 2])
        else:
            O32 = sb("O32", [P, NQ])
            part = sb("part", [P, 2, QT, HALVES])
            top, negtop = sb("top", [P, 2, QT]), sb("negtop", [P, 2, QT])
            diag = [sb(f"diag{h}", [P, QT, P], f32r) for h in range(2)]
            spread = sb("spread", [P, P], f32r)
        if cross:
            bqkv = sb("bqkv", [P, 3, NP])
            pair_bias = [sb(f"pair_bias{i}", [P, 2]) for i in range(2)]
        if own:
            WO = sb("WO", [P, 3, D])
            gates_raw = sb("gates_raw", [P, 2, NGATE])
            gates_hi, gates_lo = sb("gates_hi", [P, 2, NGATE], f32r), sb("gates_lo", [P, 2, NGATE], f32r)
            gated = sb("gated", [P, QT, NGATE])
            rank = sb("rank", [P, QT, 2 * HEADS, EXPERTS])
            over = sb("over", [P, QT, 2 * HEADS, EXPERTS])
            out_mask = sb("out_mask", [P, QT, HEADS, EXPERTS])
            sigm = sb("sigm", [P, QT, HEADS * EXPERTS])
            VALL = sb("VALL", [P, QT, HEADS * DH])
            prods = [sb(f"prod{i}", [P, HEADS, DH]) for i in range(2)]
            natural = sb("natural", [P, QT, HEADS * DH])
            mixed = sb("mixed", [P, QT, 3 * P])
            mixedT = sb("mixedT", [P, 3, NQ])

        scores = [ctx.enter_context(nc.psum_tensor(f"{name}_scores{h}", [P, 2, NQ], fp32)) for h in range(2)]
        outT = [ctx.enter_context(nc.psum_tensor(f"{name}_outT{i}", [P, NQ], fp32)) for i in range(2)]
        ring = [ctx.enter_context(nc.psum_tensor(f"{name}_ring{i}", [P, 512], fp32)) for i in range(2)]

        x_loaded, rows_loaded, c_loaded, w_loaded = (sem(n) for n in ("x_loaded", "rows_loaded", "c_loaded", "w_loaded"))
        const_loaded, const_set, const_made = sem("const_loaded"), sem("const_set"), sem("const_made")
        x_stored = sem("x_stored")
        norm_steps, var_ready, rsqrt_ready = sem("norm_steps"), sem("var_ready"), sem("rsqrt_ready")
        w_scaled, w_high, w_split = sem("w_scaled"), sem("w_high"), sem("w_split")
        full = sem("full")
        free = [sem(f"free{i}") for i in range(2)]
        staged, turn_high, high = sem("staged"), sem("turn_high"), sem("high")
        v_copied, rotated = sem("v_copied"), sem("rotated")
        top_found, negtop_ready, diag_ready = sem("top_found"), sem("negtop_ready"), sem("diag_ready")
        s_full, exp_done, clipped, av_done = sem("s_full"), sem("exp_done"), sem("clipped"), sem("av_done")
        added = [sem(f"added{h}") for h in range(2)]
        fold_done = [sem(f"fold_done{h}") for h in range(2)]
        normed, out_biased, rows_biased = sem("normed"), sem("out_biased"), sem("rows_biased")
        copied, mask_kept = sem("copied"), sem("mask_kept")
        biases_ready, recip_made = sem("biases_ready"), sem("recip_made")
        gate_exp, gate_steps, v_sliced, mix_steps = sem("gate_exp"), sem("gate_steps"), sem("v_sliced"), sem("mix_steps")

        norm_tiles, norm_sems = (stats, mv, varr, rstd, newton, carrier), (norm_steps, var_ready, rsqrt_ready)
        p_ready, p_ahead = (clipped, 0) if latent else (exp_done, AHEAD)
        CONSTANTS = {"latent": 8, "cross": 5, "self": 4 + EXPERTS}[kind]
        MADE = {"latent": 5, "cross": 10, "self": 12}[kind]
        RANK_STEPS = 1 + 4 * (EXPERTS - 1)
        GATE_STEPS = RANK_STEPS + 4 + QT * (2 * EXPERTS - 1)
        MIX_STEPS = 2 * EXPERTS

        head = [("load",), ("norm_x",), ("split", 0), ("split", 1)] + enter_order(kind, KT)
        head += step_plan(kind, KT, False, True, False)
        first_step = ([("kept",)] if own else []) + step_plan(kind, KT, True, True, False, split=True)
        step = step_plan(kind, KT, True, True, True, split=True)
        late_step = step_plan(kind, KT, True, True, True)
        last_step = step_plan(kind, KT, True, False, True)
        late_more = [("load",)] + step_plan(kind, KT, True, True, True, split=True) + [("norm_x",)]
        last_more = step_plan(kind, KT, True, True, True, split=True, enter=True)
        tail = step_plan(kind, KT, False, False, True)
        if own:
            tail += [("mix", t) for t in range(QT)] + [("mixT", t) for t in range(QT)]
        tail += [("out", t) for t in range(QT)]

        def walk(eng, do):
            place = Place()

            def batch(b, late, last):
                do(place, b, 0, 0, first_step)
                loops = (NP - 3) // 2
                if loops:
                    with turns(eng, loops, place, [step, step]) as j:
                        do(place, b, 2 * j + 1, 1, step)
                        do(place, b, 2 * j + 2, 0, step)
                for p in range(1 + 2 * loops, NP - 2):
                    do(place, b, p, p % 2, step)
                do(place, b, NP - 2, NP % 2, late)
                do(place, b, NP - 1, 1 - NP % 2, last)
                do(place, b, NP, NP % 2, tail)

            do(place, 0, -1, 1, head)
            if B > 1:
                with turns(eng, B - 1, place, [first_step] + [step] * (NP - 3) + [late_more, last_more, tail]) as b:
                    batch(b, late_more, last_more)
            batch(B - 1, late_step, last_step)

        def following(p, ahead=1):
            return (p + ahead) % NP if isinstance(p, int) else p + ahead

        def evacuated(eng, mark):
            for i in range(2):
                eng.wait_ge(free[i], mark[i] + 1)

        behind_shift = QT * (KT // 4) // 2 + 1 if shifted else 0

        def copies(place):
            return place["q"] + place["k"] + place["kT"] if shifted else place["q"]

        def norm_count(place):
            return place["norm_x"] * (ROUNDS * (3 * QT + 4)) + place["norm_c"] * (3 * KT + 4)

        def norm_rounds(place):
            return place["norm_x"] * ROUNDS + place["norm_c"]

        def add_up(eng, ops, place, h, c):
            steps = (NC - 1) * place.attends.value
            if c >= 1:
                eng.wait_ge(p_ready, place.attends.value * (2 * NC) + (2 * c + h + 1 + p_ahead))
                if c == 1:
                    eng.wait_ge(fold_done[h], place.attends.value + AHEAD)
                else:
                    eng.wait_ge(added[h], steps + (c - 1 + AHEAD))
                first = probs[h][0] if c == 1 else acc[h]
                ops.tensor_tensor(acc[h][:, :, :], first[:, :, :], probs[h][c % 2][:, :, :], ALU.add).then_inc(added[h], 1)
            if c == NC - 1:
                eng.wait_ge(added[h], steps + (NC - 1 + AHEAD))
                eng.wait_ge(normed, place["sum"] + AHEAD)
                ops.tensor_tensor(folded[h][:, :], acc[h][:, 0, :], acc[h][:, 1, :], ALU.add).then_inc(fold_done[h], 1)

        block = ctx.enter_context(nc.Block())

        @block.sync
        def _(sp):
            n_const = [0]

            def constant(dst, src, columns=False):
                sp.dma_start(dst, src, allow_slow_non_contiguous=columns).then_inc(const_loaded, 16)
                n_const[0] += 1

            if own:
                sp.wait_ge(const_set, 1)
                constant(WO[:, 0:2, :], weights["Wo"][0:256, :].rearrange("(c p) n -> p c n", p=P))
                constant(WO[0:64, 2, :], weights["Wo"][256:320, :])
                for e in range(EXPERTS):
                    constant(gates_raw[:, :, e * DH:(e + 1) * DH], weights["Wv"][e].rearrange("(c p) n -> p c n", p=P))
                for i, w in enumerate(("Ws", "Wd")):
                    at = NV + i * HEADS * EXPERTS
                    constant(gates_raw[:, :, at:at + HEADS * EXPERTS], weights[w].rearrange("(c p) n -> p c n", p=P))
            else:
                constant(WO[:, :, :], weights["Wo"].rearrange("(c p) n -> p c n", p=P))
                constant(bo[:, :], weights["bo"].rearrange("(a n) -> a n", a=1).broadcast_to([P, D]))
            if latent:
                constant(cos[:, :, :], weights["cos"].rearrange("(t p) n -> p t n", p=P))
                constant(sin[:, :, :], weights["sin"].rearrange("(t p) n -> p t n", p=P))
                for tile, g, b_ in ((gbx, "gx", "bx"), (gbc, "gc", "bc")):
                    constant(tile[:, 0, :], weights[g].rearrange("(c p) -> p c", p=P), columns=True)
                    constant(tile[:, 1, :], weights[b_].rearrange("(c p) -> p c", p=P), columns=True)
            if cross:
                for i, w in enumerate(("bq", "bk", "bv")):
                    constant(bqkv[:, i, :], weights[w].rearrange("(c p) -> p c", p=P), columns=True)
            assert n_const[0] == CONSTANTS

            def do(place, b, p, par, plan):
                for item in plan:
                    if item[0] == "load":
                        sp.wait_ge(full, place.units.value + AHEAD)
                        sp.dma_start(XN[:, :, :], x_in[bass.ds(place["load"] * NQ, NQ), :].rearrange("(t p) d -> p t d", p=P))\
                          .then_inc(rows_loaded, 16)
                        if not own:
                            sp.dma_start(C[:, :, :], context[bass.ds(place["load"] * KEYS, KEYS), :]
                                         .rearrange("(t p) d -> p t d", p=P)).then_inc(c_loaded, 16)
                    elif item[0] == "split":
                        sp.wait_ge(w_split, place["split"] + 1)
                        at = (following(p, 2) if item[1] is None else item[1]) * P
                        for i, (w, off) in enumerate(weights["slices"]):
                            sp.dma_start(WRAW[:, :, i * P:(i + 1) * P],
                                         w[:, bass.ds(at + off, P)].rearrange("(c p) n -> p c n", p=P)).then_inc(w_loaded, 16)
                    place.passed(item)
                if plan is first_step:
                    sp.wait_ge(x_stored, 16 * b + 16)
                    sp.dma_start(X[:, :, :], x_in[bass.ds(b * NQ, NQ), :].rearrange("(t p) d -> p t d", p=P))\
                      .then_inc(x_loaded, 16)
                if plan is tail:
                    sp.wait_ge(free[1 - place.ring], place.mark()[1 - place.ring] + 1)
                    sp.dma_start(x_out[bass.ds(b * NQ, NQ), :].rearrange("(t p) d -> p t d", p=P), X[:, :, :])\
                      .then_inc(x_stored, 16)

            walk(sp, do)
            sp.wait_ge(x_stored, 16 * B + 16)

        @block.gpsimd
        def _(pool):
            nc.gpsimd.memset(WO[:, 2, :] if own else prime[:, :], 0.0).then_inc(const_set, 1)
            nc.gpsimd.memset(ident[:, :], 0.0).then_inc(const_set, 1)
            pool.wait_ge(const_set, 2)
            nc.gpsimd.affine_select(out=ident[:, :], in_=ident[:, :], compare_op=ALU.not_equal, fill=1.0, base=0,
                                    pattern=[[-1, P]], channel_multiplier=1).then_inc(const_made, 1)
            nc.gpsimd.memset(ones[:, :], 1.0).then_inc(const_made, 1)
            nc.gpsimd.memset(neghalf[:, :], -0.5).then_inc(const_made, 1)
            nc.gpsimd.memset(scale[:, :], SCALE).then_inc(const_made, 1)
            if shifted:
                nc.gpsimd.memset(spread[:, :].bitcast(fp32), 1.0 / DH).then_inc(const_made, 1)
                for i in range(2):
                    for h in range(2):
                        pool.wait_ge(const_made, 5 + 2 * i + h)
                        nc.gpsimd.memset(S2[i][AUX[h], h, :].bitcast(fp32), 1.0).then_inc(const_made, 1)
            pool.wait_ge(const_loaded, 16 * CONSTANTS)
            if latent:
                nc.gpsimd.tensor_scalar(nsin[:, :, :], sin[:, :, :], -1.0, None, ALU.mult).then_inc(const_made, 1)
            if cross:
                nc.gpsimd.tensor_scalar(bqkv[:, 0, :], bqkv[:, 0, :], SCALE, None, ALU.mult).then_inc(const_made, 1)
            if own:
                nc.gpsimd.memset(mixed[:, :, :], 0.0).then_inc(const_made, 1)
                nc.gpsimd.tensor_copy(gates_hi[:, :, :], gates_raw[:, :, :]).then_inc(const_made, 1)
                pool.wait_ge(const_made, MADE - 1)
                nc.gpsimd.tensor_tensor(gates_lo[:, :, :], gates_raw[:, :, :], gates_hi[:, :, :].bitcast(fp32),
                                        ALU.subtract).then_inc(const_made, 1)
            pool.wait_ge(const_made, MADE)
            for i, (s, k) in enumerate(((free[0], 1), (free[1], 1), (full, AHEAD), (w_split, 1), (exp_done, AHEAD),
                                        (av_done, AHEAD), (added[0], AHEAD), (added[1], AHEAD),
                                        (fold_done[0], AHEAD), (fold_done[1], AHEAD), (normed, AHEAD),
                                        (out_biased, AHEAD), (x_stored, 16), (v_sliced, AHEAD),
                                        (mask_kept, AHEAD), (mix_steps, AHEAD))):
                nc.gpsimd.memset(primes[:, i:i + 1], 0.0).then_inc(s, k)

            def do(place, b, p, par, plan):
                for item in plan:
                    if item[0] in ("norm_x", "norm_c"):
                        n = QT if item[0] == "norm_x" else KT
                        for r in range(ROUNDS if item[0] == "norm_x" else 1):
                            pool.wait_ge(var_ready, norm_rounds(place) + (r + 1))
                            nc.gpsimd.tensor_tensor(rstd[:, 0:n], varr[:, 0:n], neghalf[:, 0:n], ALU.pow)\
                              .then_inc(rsqrt_ready, 1)
                    elif item[0] == "split":
                        i = par if item[1] is None else item[1]
                        pool.wait_ge(w_loaded, 16 * len(weights["slices"]) * (place["split"] + 1))
                        pool.wait_ge(full, place.units.value + AHEAD)
                        nc.gpsimd.tensor_tensor(WRAW[:, :, 0:P], WRAW[:, :, 0:P],
                                                scale[:, :].unsqueeze(2).broadcast_to([P, 2, P]), ALU.mult).then_inc(w_scaled, 1)
                        pool.wait_ge(w_scaled, place["split"] + 1)
                        nc.gpsimd.tensor_tensor(WH[i][:, :, :], WRAW[:, :, :], ones[:, 0:2].unsqueeze(2).broadcast_to([P, 2, NW]),
                                                ALU.mult).then_inc(w_high, 1)
                        pool.wait_ge(w_high, place["split"] + 1)
                        nc.gpsimd.tensor_tensor(WL[i][:, :, :], WRAW[:, :, :], WH[i][:, :, :].bitcast(fp32), ALU.subtract)\
                          .then_inc(w_split, 1)
                    elif item[0] == "soft" and item[1] == 1:
                        add_up(pool, nc.gpsimd, place, 1, item[2])
                    elif item[0] == "max" and item[4]:
                        h = item[1]
                        pool.wait_ge(negtop_ready, place["top"] + 1)
                        nc.gpsimd.tensor_tensor(diag[h][:, :, :], ident[:, :].unsqueeze(1).broadcast_to([P, QT, P]),
                                                negtop[:, h, :].unsqueeze(2).broadcast_to([P, QT, P]), ALU.mult)\
                          .then_inc(diag_ready, 1)
                    place.passed(item)

            walk(pool, do)

        @block.scalar
        def _(act):
            act.wait_ge(const_made, MADE)
            waited = act.alloc_register(f"{name}_waited")
            act.reg_mov(waited, 0)

            def take_wait():
                act.reg_add(waited, waited, 1)

            def do(place, b, p, par, plan):
                nxt = 1 - par
                for item in plan:
                    u = item[0]
                    bank = ring[place.ring]
                    if u in Place.UNITS and u not in ("max", "out"):
                        act.wait_ge(full, place.units.value + (1 + AHEAD))
                    taken = free[place.ring]
                    if u == "turn":
                        gb = {"x": gbx, "c": gbc}[item[1]] if latent else None
                        ch = item[2]
                        nc.scalar.activation(staging[place.ring][:, :], bank[:, :], ACT.Identity,
                                             scale=gb[:, 0, ch:ch + 1] if latent else 1.0,
                                             bias=gb[:, 1, ch:ch + 1] if latent else 0.0).then_inc(staged, 1)
                    elif u == "gate":
                        nc.scalar.activation(gated[:, item[1], :], bank[:, 0:NGATE], ACT.Copy).then_inc(taken, 1)
                    elif u == "masks":
                        evacuated(act, place.mark())
                        nc.scalar.activation(sigm[:, :, :], gated[:, :, NV:NV + HEADS * EXPERTS], ACT.Exp, scale=-1.0)\
                          .then_inc(gate_exp, 1)
                    elif u == "biases":
                        nc.scalar.activation(pair_bias[nxt][:, :].unsqueeze(2), bqkv[:, 0:2, bass.ds(following(p), 1)], ACT.Copy)\
                          .then_inc(biases_ready, 1)
                    elif u == "vslice":
                        act.wait_ge(gate_steps, GATE_STEPS * place["masks"])
                        act.wait_ge(av_done, NC * place.attends.value + AHEAD)
                        take_wait()
                        nc.scalar.activation(VN[nxt][:, :, :], VALL[:, :, bass.ds(following(p) * P, P)], ACT.Copy)\
                          .then_inc(v_sliced, 1)
                    elif u == "kv":
                        t = item[1]
                        src = bank[:, :].rearrange("p (s n) -> p s n", s=2)
                        if t == 0:
                            act.wait_ge(av_done, NC * place.attends.value + AHEAD)
                        if latent:
                            nc.scalar.activation(VN[nxt][:, 2 * t:2 * t + 2, :], src[:, :, 128:256], ACT.Copy)\
                              .then_inc(v_copied, 1)
                        else:
                            nc.scalar.activation(VN[nxt][:, 2 * t:2 * t + 2, :], src[:, :, :], ACT.Copy).then_inc(taken, 1)
                    elif u in ("k", "kT"):
                        cols = slice(item[1] * 512, item[1] * 512 + 512) if u == "kT" else slice(0, 512)
                        for h in range(2):
                            last = nc.scalar.activation(S1[nxt][MAIN[h], h, cols], bank[MAIN[h], :], ACT.Identity,
                                                        bias=pair_bias[nxt][MAIN[h], 1:2] if cross else 0.0)
                        last.then_inc(high, 1)
                        if shifted:
                            act.wait_ge(high, place["k"] + place["kT"] + place["q"] + 1)
                            for h in range(2):
                                last = nc.scalar.activation(S2[nxt][MAIN[h], h, cols], S1[nxt][MAIN[h], h, cols].bitcast(fp32),
                                                            ACT.Copy)
                            last.then_inc(copied, 1)
                    elif u == "q":
                        if cross:
                            act.wait_ge(biases_ready, place["biases"])
                        for h in range(2):
                            last = nc.scalar.activation(Q1[nxt][MAIN[h], h, :], bank[MAIN[h], :], ACT.Identity,
                                                        bias=pair_bias[nxt][MAIN[h], 0:1] if cross else 0.0)
                        last.then_inc(high, 1)
                        act.wait_ge(high, place["k"] + place["kT"] + place["q"] + 1)
                        for h in range(2):
                            last = nc.scalar.activation(Q1[nxt][AUX[h], h, :], Q1[nxt][MAIN[h], h, :].bitcast(fp32), ACT.Copy)
                        last.then_inc(copied, 1)
                    elif u == "shift":
                        h = item[1]
                        nc.scalar.activation(Q2[nxt][AUX[h], h, :], bank[AUX[h], :], ACT.Copy).then_inc(taken, 1)
                    elif u == "S":
                        _, h, c = item
                        act.wait_ge(s_full, place.attends.value * (2 * NC) + (2 * c + h + 1))
                        act.wait_ge(av_done, place.attends.value * NC + (c - 1 + AHEAD))
                        rel = max(NC - 2, 1) - (NC - 1) if c == 0 else 0 if c == 1 else 1
                        act.wait_ge(added[h], place.attends.value * (NC - 1) + (rel + AHEAD))
                        nc.scalar.activation(probs[h][c % 2][:, :, :], scores[h][:, :, :], ACT.Exp).then_inc(exp_done, 1)
                    elif u == "sum":
                        act.wait_ge(normed, place["sum"] + AHEAD)
                        nc.scalar.activation(sums[:, :], bank[:, :], ACT.Copy).then_inc(taken, 1)
                    elif u == "biased":
                        act.wait_ge(normed, place["sum"] + AHEAD)
                        take_wait()
                        nc.scalar.activation(OT[:, bass.ds(p - 1, 1), :], O32[:, :].unsqueeze(1), ACT.Identity,
                                             bias=bqkv[:, 2, bass.ds(p - 1, 1)]).then_inc(out_biased, 1)
                    elif u == "back":
                        take_wait()
                        nc.scalar.activation(natural[:, :, bass.ds((p - 1) * P, P)],
                                             bank[:, :].rearrange("p (t n) -> p t n", t=QT), ACT.Copy).then_inc(taken, 1)
                    elif u == "mixT":
                        nc.scalar.activation(mixedT[:, :, item[1] * P:(item[1] + 1) * P],
                                             bank[:, 0:3 * P].rearrange("p (c n) -> p c n", c=3), ACT.Copy).then_inc(taken, 1)
                    place.passed(item)

            walk(act, do)

        @block.vector
        def _(dve):
            dve.wait_ge(const_made, MADE)

            def masks(place, b):
                base = place["masks"] * GATE_STEPS
                n = [0]

                def stepped(ins):
                    ins.then_inc(gate_steps, 1)
                    n[0] += 1
                    dve.wait_ge(gate_steps, base + n[0])

                G = gated[:, :, NV:NGATE].rearrange("p t (g e) -> p t g e", e=EXPERTS)
                rank_experts(nc, stepped, G, rank, over, EXPERTS)
                stepped(nc.vector.tensor_scalar(rank[:, :, :, :], rank[:, :, :, :], 1.5, None, ALU.is_lt))
                dve.wait_ge(gate_exp, place["masks"] + 1)
                stepped(nc.vector.tensor_scalar(sigm[:, :, :], sigm[:, :, :], 1.0, None, ALU.add))
                stepped(nc.vector.reciprocal(sigm[:, :, :], sigm[:, :, :]))
                wv = rank[:, :, 0:HEADS, :]
                stepped(nc.vector.tensor_tensor(wv, wv, sigm[:, :, :].rearrange("p t (h e) -> p t h e", e=EXPERTS), ALU.mult))
                for t in range(QT):
                    V = VALL[:, t, :].rearrange("p (h k) -> p h k", h=HEADS)
                    for e in range(EXPERTS):
                        shape = [P, HEADS, DH]
                        stepped(nc.vector.tensor_tensor(V if e == 0 else prods[0][:, :, :],
                                                        gated[:, t, e * DH:(e + 1) * DH].unsqueeze(1).broadcast_to(shape),
                                                        rank[:, t, 0:HEADS, e:e + 1].broadcast_to(shape), ALU.mult))
                        if e:
                            stepped(nc.vector.tensor_tensor(V, V, prods[0][:, :, :], ALU.add))
                assert n[0] == GATE_STEPS

            def do(place, b, p, par, plan):
                nxt = 1 - par
                for item in plan:
                    u = item[0]
                    bank = ring[place.ring]
                    taken = free[place.ring]
                    bank_count = place.bank[place.ring].value
                    this_full = place.units.value + (1 + AHEAD)
                    if u == "norm_x":
                        dve.wait_ge(rows_loaded, 16 * place["norm_x"] + 16)
                        normalise(nc, dve, norm_tiles, norm_sems, lambda t: XN[:, t, :], XN, QT, norm_count(place), norm_rounds(place))
                        if latent:
                            base = norm_count(place) + (3 * QT + 4)
                            dve.wait_ge(norm_steps, base)
                            normalise(nc, dve, norm_tiles, norm_sems, lambda t: XN[:, t, :], XN, QT, base, norm_rounds(place) + 1)
                    elif u == "norm_c":
                        dve.wait_ge(c_loaded, 16 * place["norm_c"] + 16)
                        normalise(nc, dve, norm_tiles, norm_sems, lambda t: C[:, t, :], C, KT, norm_count(place), norm_rounds(place))
                    elif u == "turn":
                        _, src, ch, g = item
                        H, L = (XTH, XTL) if src == "x" else (CTH, CTL)
                        cols = slice(g * 512, g * 512 + 512)
                        dve.wait_ge(staged, place["turn"] + 1)
                        nc.vector.tensor_copy(H[:, ch, cols], staging[place.ring][:, :]).then_inc(turn_high, 1)
                        dve.wait_ge(turn_high, place["turn"] + 1)
                        nc.vector.tensor_tensor(L[:, ch, cols], staging[place.ring][:, :], H[:, ch, cols].bitcast(fp32),
                                                ALU.subtract).then_inc(taken, 1)
                    elif u == "kept":
                        if True:
                            dve.wait_ge(mix_steps, MIX_STEPS * QT * place["kept"] + AHEAD)
                        nc.vector.tensor_copy(out_mask[:, :, :, :], rank[:, :, HEADS:, :]).then_inc(mask_kept, 1)
                    elif u == "masks":
                        evacuated(dve, place.mark())
                        dve.wait_ge(v_sliced, place["vslice"] + AHEAD)
                        dve.wait_ge(mask_kept, place["masks"] + AHEAD)
                        masks(place, b)
                    elif u == "kv" and latent:
                        t = item[1]
                        rot1, rot2 = rot1s[place.ring], rot2s[place.ring]
                        tiles = slice(2 * t, 2 * t + 2)
                        K = bank[:, :].rearrange("p (s n) -> p s n", s=2)[:, :, 0:128]
                        K4 = K.rearrange("p s (g i) -> p s g i", i=32)
                        K5 = K.rearrange("p s (h f i) -> p s h f i", f=2, i=32)
                        R5 = rot2[:, :, :].rearrange("p s (h f i) -> p s h f i", f=2, i=32)
                        dve.wait_ge(taken, bank_count + 1)
                        dve.wait_ge(v_copied, place["kv"] + 1)
                        nc.vector.tensor_tensor(rot1[:, :, :].rearrange("p s (g i) -> p s g i", i=32), K4,
                                                cos[:, tiles, :].unsqueeze(2).broadcast_to([P, 2, 4, 32]), ALU.mult)\
                          .then_inc(rotated, 1)
                        for f, table in ((0, nsin), (1, sin)):
                            nc.vector.tensor_tensor(R5[:, :, :, f, :], K5[:, :, :, 1 - f, :],
                                                    table[:, tiles, :].unsqueeze(2).broadcast_to([P, 2, 2, 32]), ALU.mult)\
                              .then_inc(rotated, 1)
                        dve.wait_ge(rotated, 3 * place["kv"] + 3)
                        nc.vector.tensor_tensor(KR[:, tiles, :], rot1[:, :, :], rot2[:, :, :], ALU.add).then_inc(taken, 1)
                    elif u in ("k", "kT"):
                        cols = slice(item[1] * 512, item[1] * 512 + 512) if u == "kT" else slice(0, 512)
                        dve.wait_ge(high, place["k"] + place["kT"] + place["q"] + 1)
                        for h in range(2):
                            last = nc.vector.scalar_tensor_tensor(
                                out=S1[nxt][AUX[h], h, cols], in0=bank[MAIN[h], :],
                                scalar=pair_bias[nxt][MAIN[h], 1:2] if cross else 0.0,
                                in1=S1[nxt][MAIN[h], h, cols].bitcast(fp32), op0=ALU.add, op1=ALU.subtract)
                        last.then_inc(taken, 1)
                    elif u == "q":
                        dve.wait_ge(high, place["k"] + place["kT"] + place["q"] + 1)
                        for h in range(2):
                            for rows in (MAIN if latent else (MAIN[h],)):
                                last = nc.vector.scalar_tensor_tensor(
                                    out=Q2[nxt][rows, h, :], in0=bank[MAIN[h], :],
                                    scalar=pair_bias[nxt][MAIN[h], 0:1] if cross else 0.0,
                                    in1=Q1[nxt][MAIN[h], h, :].bitcast(fp32), op0=ALU.add, op1=ALU.subtract)
                        last.then_inc(taken, 1)
                    elif u == "max":
                        _, h, qt, i, is_last = item
                        dve.wait_ge(full, this_full)
                        nc.vector.reduce_max(part[:, h, qt, i:i + 1], bank[:, :], AX.X).then_inc(taken, 1)
                        if is_last:
                            dve.wait_ge(taken, bank_count + 2)
                            dve.wait_ge(free[1 - place.ring], place.bank[1 - place.ring].value + 1)
                            nc.vector.reduce_max(top[:, h, :], part[:, h, :, :], AX.X).then_inc(top_found, 1)
                            dve.wait_ge(top_found, place["top"] + 1)
                            nc.vector.tensor_scalar(negtop[:, h, :], top[:, h, :], -1.0, None, ALU.mult)\
                              .then_inc(negtop_ready, 1)
                    elif u == "soft":
                        _, h, c = item
                        if latent:
                            tile = probs[h][c % 2]
                            s = place.attends.value * (2 * NC) + (2 * c + h + 1)
                            dve.wait_ge(exp_done, s + AHEAD)
                            nc.vector.tensor_scalar(tile[:, :, :], tile[:, :, :], exp(CLIP), exp(-CLIP), ALU.min, ALU.max)\
                              .then_inc(clipped, 1)
                        if h == 0:
                            add_up(dve, nc.vector, place, 0, c)
                    elif u == "sum":
                        dve.wait_ge(taken, bank_count + 2)
                        nc.vector.reciprocal(recip[:, :], sums[:, :]).then_inc(recip_made, 1)
                        dve.wait_ge(recip_made, place["sum"] + 1)
                        dve.wait_ge(av_done, NC * (place["sum"] + 1) + AHEAD)
                        if latent:
                            dst = OT[:, bass.ds(p - 1, 1), :]
                        else:
                            dst = O32[:, :].unsqueeze(1)
                        if cross:
                            dve.wait_ge(out_biased, place["sum"] + AHEAD)
                        nc.vector.tensor_tensor(dst, outT[nxt][:, :].unsqueeze(1), recip[:, :].unsqueeze(1), ALU.mult)\
                          .then_inc(normed, 1)
                    elif u == "mix":
                        t = item[1]
                        evacuated(dve, place.mark())
                        for e in range(EXPERTS):
                            m = t * EXPERTS + e
                            prod = prods[m % 2]
                            if m >= 2:
                                dve.wait_ge(mix_steps, MIX_STEPS * QT * b + (2 * (m - 1) + AHEAD))
                            nc.vector.tensor_tensor(prod[:, :, :], natural[:, t, :].rearrange("p (h k) -> p h k", h=HEADS),
                                                    out_mask[:, t, :, e:e + 1].broadcast_to([P, HEADS, DH]), ALU.mult)\
                              .then_inc(mix_steps, 1)
                            dve.wait_ge(mix_steps, MIX_STEPS * QT * b + (2 * m + 1 + AHEAD))
                            nc.vector.reduce_sum(mixed[:, t, e * DH:(e + 1) * DH],
                                                 prod[:, :, :].rearrange("p h k -> p k h"), AX.X).then_inc(mix_steps, 1)
                    elif u == "out":
                        t = item[1]
                        if t == 0:
                            dve.wait_ge(x_loaded, 16 * b + 16)
                        if t == 0 and not own:
                            nc.vector.tensor_tensor(X[:, :, :], X[:, :, :], bo[:, :].unsqueeze(1).broadcast_to([P, QT, D]),
                                                    ALU.add).then_inc(rows_biased, 1)
                            dve.wait_ge(rows_biased, b + 1)
                        dve.wait_ge(full, this_full)
                        nc.vector.tensor_tensor(X[:, t, :], bank[:, 0:D], X[:, t, :], ALU.add).then_inc(taken, 1)
                    place.passed(item)

            walk(dve, do)

        @block.tensor
        def _(pe):
            pe.wait_ge(const_made, MADE)

            def product(out, passes, start=True, stop=True):
                for i, (still, moving) in enumerate(passes):
                    last = nc.tensor.matmul(out, still, moving, start=start and i == 0, stop=stop and i == len(passes) - 1)
                return last

            def three(highs, lows, highs2, lows2):
                return [pair for a, al, w, wl in zip(highs, lows, highs2, lows2) for pair in ((a, w), (a, wl), (al, w))]

            def do(place, b, p, par, plan):
                nxt = 1 - par
                made = place.mark()
                last_bank, made0 = 1 - place.ring, list(made)
                if plan is not first_step:
                    made0[last_bank] = made0[last_bank] - (behind_shift + 1) // 2
                    made0[1 - last_bank] = made0[1 - last_bank] - behind_shift // 2
                kv_mark = None
                for item in plan:
                    u = item[0]
                    bank = ring[place.ring]
                    if u in Place.UNITS:
                        pe.wait_ge(free[place.ring], place.bank[place.ring].value + 1)
                    if u == "turned":
                        evacuated(pe, place.mark())
                    elif u == "turn":
                        _, src, ch, g = item
                        if src == "x" or latent:
                            pe.wait_ge(norm_steps, norm_count(place))
                        elif cross:
                            pe.wait_ge(c_loaded, 16 * place["load"])
                        rows = XN if src == "x" else C
                        for k in range(4):
                            last = nc.tensor.transpose(bank[:, k * P:(k + 1) * P],
                                                       rows[:, 4 * g + k, ch * P:(ch + 1) * P], ident[:, :])
                        last.then_inc(full, 1)
                    elif u == "gate":
                        t = item[1]
                        ts = slice(t * P, (t + 1) * P)
                        product(bank[:, 0:NGATE], three(*([T[:, ch, ts] for ch in range(2)] for T in (XTH, XTL)),
                                                        *([T[:, ch, :] for ch in range(2)] for T in (gates_hi, gates_lo))))\
                            .then_inc(full, 1)
                    elif u == "kv":
                        t = item[1]
                        for s in range(2):
                            ts = slice((2 * t + s) * P, (2 * t + s + 1) * P)
                            last = product(bank[:, s * 256:(s + 1) * 256],
                                           three(*([T[:, ch, ts] for ch in range(2)] for T in (CTH, CTL)),
                                                 *([T[nxt][:, ch, P:3 * P] for ch in range(2)] for T in (WH, WL))))
                        last.then_inc(full, 1)
                    elif u in ("q", "k"):
                        if u == "k" or not own:
                            pe.wait_ge(w_split, place["q"] + 2)
                        at = P if u == "k" else 0
                        product(bank[:, :], three(*([T[nxt][:, ch, at:at + P] for ch in range(2)] for T in (WH, WL)),
                                                  *([T[:, ch, :] for ch in range(2)] for T in (XTH, XTL)))).then_inc(full, 1)
                    elif u == "kT":
                        evacuated(pe, kv_mark)
                        for k in range(4):
                            t = 4 * item[1] + k
                            last = nc.tensor.transpose(bank[:, k * P:(k + 1) * P],
                                                       KR[:, t, :] if latent else VN[nxt][:, t, 0:P], ident[:, :])
                        last.then_inc(full, 1)
                    elif u == "max":
                        _, h, qt, i, _ = item
                        if (h, qt, i) == (0, 0, 0):
                            evacuated(pe, place.mark())
                            pe.wait_ge(copied, copies(place))
                        nc.tensor.matmul(bank[:, :], Q1[nxt][:, h, qt * P:(qt + 1) * P], S1[nxt][:, h, i * 512:(i + 1) * 512],
                                         start=True, stop=True).then_inc(full, 1)
                    elif u == "shift":
                        pe.wait_ge(diag_ready, place["shift"] + 1)
                        nc.tensor.matmul(bank[:, :], spread[:, :], diag[item[1]][:, :, :].rearrange("p t n -> p (t n)"),
                                         start=True, stop=True).then_inc(full, 1)
                    elif u == "S":
                        _, h, c = item
                        if c == 0:
                            evacuated(pe, made if h else made0)
                        if c == 0 and h == 0:
                            pe.wait_ge(copied, copies(place))
                        pe.wait_ge(exp_done, place.attends.value * (2 * NC) + (2 * c + h - 1 + AHEAD))
                        for k in range(2):
                            ks = slice((2 * c + k) * P, (2 * c + k + 1) * P)
                            last = product(scores[h][:, k, :], [(S1[par][:, h, ks], Q1[par][:, h, :]),
                                                                (S2[par][:, h, ks], Q2[par][:, h, :])])
                        last.then_inc(s_full, 1)
                    elif u == "AV":
                        _, c, k = item
                        if k == 0:
                            pe.wait_ge(p_ready, place.attends.value * (2 * NC) + (2 * c + 2 + p_ahead))
                            if c == 0:
                                pe.wait_ge(normed, place.attends.value + (AHEAD - 1))
                                if own:
                                    pe.wait_ge(v_sliced, place.attends.value + (1 + AHEAD))
                        whose, tile = (par, 2 * c + k) if c >= 0 else (nxt, 2 * (NC - 1) + k)
                        for h in range(2):
                            last = nc.tensor.matmul(outT[whose][MAIN[h], :], VN[whose][:, tile, VC + h * DH:VC + (h + 1) * DH],
                                                    probs[h][c % 2][:, k, :], start=(c == 0 and k == 0),
                                                    stop=(c == -1 and k == 1))
                        if k == 1:
                            last.then_inc(av_done, 1)
                    elif u == "sum":
                        for h in range(2):
                            pe.wait_ge(fold_done[h], place["sum"] + (1 + AHEAD))
                            last = nc.tensor.matmul(bank[MAIN[h], :], ones[:, :], folded[h][:, :], start=True, stop=True)
                        last.then_inc(full, 1)
                    elif u == "back":
                        pe.wait_ge(normed, place["back"] + (1 + AHEAD))
                        for t in range(QT):
                            last = nc.tensor.transpose(bank[:, t * P:(t + 1) * P], O32[:, t * P:(t + 1) * P], ident[:, :])
                        last.then_inc(full, 1)
                    elif u == "mixT":
                        t = item[1]
                        pe.wait_ge(mix_steps, MIX_STEPS * QT * b + (MIX_STEPS * (t + 1) + AHEAD))
                        for c in range(3):
                            last = nc.tensor.transpose(bank[:, c * P:(c + 1) * P], mixed[:, t, c * P:(c + 1) * P], ident[:, :])
                        last.then_inc(full, 1)
                    elif u == "out":
                        t = item[1]
                        ts = slice(t * P, (t + 1) * P)
                        if t == 0:
                            if own:
                                evacuated(pe, place.mark())
                            else:
                                pe.wait_ge(normed if latent else out_biased, place["sum"] + AHEAD)
                        O, chunks = (mixedT, 3) if own else (OT, NP)
                        product(bank[:, 0:D], [(O[:, c, ts], WO[:, c, :]) for c in range(chunks)]).then_inc(full, 1)
                    place.passed(item)
                    if u == "kv":
                        kv_mark = place.mark()

            walk(pe, do)



def expert_layer(nc, name, x_in, x_out, weights, B):
    fp32, f32r = mybir.dt.float32, mybir.dt.float32r
    ALU, ACT, AX = mybir.AluOpType, mybir.ActivationFunctionType, mybir.AxisListType
    E = ROUTED
    WIDE = E * D
    BANKS = 4
    SETUP = 2 * E
    PER_BATCH = QT * E // 2

    ctx = ExitStack()
    with ctx:
        def sb(label, shape, dt=fp32):
            return ctx.enter_context(nc.sbuf_tensor(f"{name}_{label}", shape, dt))

        def sem(label):
            return ctx.enter_context(nc.semaphore(f"{name}_{label}"))

        X, XN = sb("X", [P, QT, D]), sb("XN", [P, QT, D])
        XT = [sb(f"XT{part}", [P, 2, NQ], f32r) for part in ("high", "low")]
        raw = sb("raw", [P, 2 * E, D])
        W = [sb(f"W{part}", [P, 2, WIDE], f32r) for part in ("high", "low")]
        router_raw = sb("router_raw", [P, 2, E])
        router = [sb(f"router_{part}", [P, 2, E], f32r) for part in ("high", "low")]
        router_b = sb("router_b", [P, E])
        bias_raw, bias_high = sb("bias_raw", [64, WIDE]), sb("bias_high", [64, WIDE], f32r)
        bias, ones = sb("bias", [P, WIDE], f32r), sb("ones", [P, P], f32r)
        ident, neghalf = sb("ident", [P, P]), sb("neghalf", [P, QT])
        tiles = (sb("stats", [P, QT, 6]), sb("mv", [P, QT, 2]), sb("varr", [P, QT]), sb("rstd", [P, QT]),
                 [sb(f"newton{i}", [P, QT]) for i in range(4)], sb("carrier", [P, 1]))
        varr, rstd = tiles[2], tiles[3]
        logits, less = sb("logits", [P, QT, 1, E]), sb("less", [P, QT, E])
        rank, over = sb("rank", [P, QT, 1, E]), sb("over", [P, QT, 1, E])
        top, total, weight = sb("top", [P, QT]), sb("total", [P, QT]), sb("weight", [P, QT])
        pick = sb("pick", [P, QT, E])

        turned = [ctx.enter_context(nc.psum_tensor(f"{name}_turned{i}", [P, NQ], fp32)) for i in range(2)]
        routed = ctx.enter_context(nc.psum_tensor(f"{name}_routed", [P, QT, E], fp32))
        ring = [ctx.enter_context(nc.psum_tensor(f"{name}_ring{i}", [P, 512], fp32)) for i in range(BANKS)]

        const_loaded, const_made, router_split = sem("const_loaded"), sem("const_made"), sem("router_split")
        bias_steps = sem("bias_steps")
        x_loaded, x_stored = sem("x_loaded"), sem("x_stored")
        norm_steps, var_ready, rsqrt_ready = sem("norm_steps"), sem("var_ready"), sem("rsqrt_ready")
        w_full, w_high = sem("w_full"), sem("w_high")
        free = [sem(f"free{i}") for i in range(BANKS)]
        turn_full, turn_high, turn_done = sem("turn_full"), sem("turn_high"), sem("turn_done")
        route_full, route_steps, exp_done = sem("route_full"), sem("route_steps"), sem("exp_done")
        full, first_added = sem("full"), sem("first_added")

        ROUTE_STEPS = 3 + (4 * (E - 1) + 1) + 4
        NORM_STEPS = 3 * QT + 4
        block = ctx.enter_context(nc.Block())

        @block.sync
        def _(sp):
            sp.dma_start(raw[:, :, :], weights["L0_ffn_expert_w"].rearrange("e (c p) d -> p (e c) d", p=P))\
              .then_inc(const_loaded, 16)
            sp.dma_start(router_b[:, :], weights["L0_ffn_router_b"].rearrange("(a n) -> a n", a=1).broadcast_to([P, E]))\
              .then_inc(const_loaded, 16)
            for c in range(2):
                sp.dma_start(router_raw[:, c, :], weights["L0_ffn_router_w"][:, c * P:(c + 1) * P].rearrange("e p -> p e"),
                             allow_slow_non_contiguous=True).then_inc(const_loaded, 16)
            for row in (0, 32):
                sp.dma_start(bias_raw[row:row + 1, :], weights["L0_ffn_expert_b"].rearrange("(a e) d -> a (e d)", a=1))\
                  .then_inc(const_loaded, 16)
            sp.wait_ge(const_made, 1)
            with sp.Fori(0, B) as b:
                sp.wait_ge(x_stored, 16 * b + 16)
                sp.dma_start(X[:, :, :], x_in[bass.ds(b * NQ, NQ), :].rearrange("(t p) d -> p t d", p=P)).then_inc(x_loaded, 16)
                for i in range(BANKS):
                    sp.wait_ge(free[i], (SETUP + PER_BATCH) // BANKS + (PER_BATCH // BANKS) * b)
                sp.dma_start(x_out[bass.ds(b * NQ, NQ), :].rearrange("(t p) d -> p t d", p=P), X[:, :, :]).then_inc(x_stored, 16)
            sp.wait_ge(x_stored, 16 * B + 16)

        @block.gpsimd
        def _(pool):
            nc.gpsimd.memset(ident[:, :], 0.0).then_inc(const_made, 1)
            nc.gpsimd.memset(bias[:, :].bitcast(fp32), 0.0).then_inc(const_made, 1)
            nc.gpsimd.memset(ones[:, :].bitcast(fp32), 1.0).then_inc(const_made, 1)
            nc.gpsimd.memset(neghalf[:, :], -0.5).then_inc(x_stored, 16)
            pool.wait_ge(const_made, 3)
            nc.gpsimd.affine_select(out=ident[:, :], in_=ident[:, :], compare_op=ALU.not_equal, fill=1.0, base=0,
                                    pattern=[[-1, P]], channel_multiplier=1).then_inc(const_made, 1)
            pool.wait_ge(const_made, 4)
            pool.wait_ge(x_stored, 16)
            with pool.Fori(0, B) as b:
                pool.wait_ge(var_ready, b + 1)
                nc.gpsimd.tensor_tensor(rstd[:, :], varr[:, :], neghalf[:, :], ALU.pow).then_inc(rsqrt_ready, 1)

        @block.scalar
        def _(act):
            for u in range(SETUP):
                ch, pair = u % 2, u // 2
                act.wait_ge(w_full, u + 1)
                nc.scalar.activation(W[0][:, ch, pair * 256:pair * 256 + 256], ring[u % BANKS][:, 0:256], ACT.Copy)\
                  .then_inc(w_high, 1)
            with act.Fori(0, B) as b:
                for ch in range(2):
                    act.wait_ge(turn_full, 2 * b + (ch + 1))
                    nc.scalar.activation(XT[0][:, ch, :], turned[ch][:, :], ACT.Copy).then_inc(turn_high, 1)
                act.wait_ge(route_steps, ROUTE_STEPS * b + 3)
                nc.scalar.activation(less[:, :, :], less[:, :, :], ACT.Exp).then_inc(exp_done, 1)

        @block.vector
        def _(dve):
            dve.wait_ge(const_made, 4)
            dve.wait_ge(const_loaded, 96)
            nc.vector.tensor_copy(router[0][:, :, :], router_raw[:, :, :]).then_inc(router_split, 1)
            dve.wait_ge(router_split, 1)
            nc.vector.tensor_tensor(router[1][:, :, :], router_raw[:, :, :], router[0][:, :, :].bitcast(fp32), ALU.subtract)\
              .then_inc(router_split, 1)
            nc.vector.tensor_copy(bias[0:1, :], bias_raw[0:1, :]).then_inc(bias_steps, 1)
            nc.vector.tensor_copy(bias_high[32:33, :], bias_raw[32:33, :]).then_inc(bias_steps, 1)
            dve.wait_ge(bias_steps, 2)
            nc.vector.tensor_tensor(bias[32:33, :], bias_raw[32:33, :], bias_high[32:33, :].bitcast(fp32), ALU.subtract)\
              .then_inc(bias_steps, 1)
            for u in range(SETUP):
                ch, pair = u % 2, u // 2
                dve.wait_ge(w_high, u + 1)
                nc.vector.tensor_tensor(W[1][:, ch, pair * 256:pair * 256 + 256], ring[u % BANKS][:, 0:256],
                                        W[0][:, ch, pair * 256:pair * 256 + 256].bitcast(fp32), ALU.subtract)\
                  .then_inc(free[u % BANKS], 1)
            with dve.Fori(0, B) as b:
                dve.wait_ge(x_loaded, 16 * b + 16)
                normalise(nc, dve, tiles, (norm_steps, var_ready, rsqrt_ready), lambda t: X[:, t, :], XN, QT,
                          NORM_STEPS * b, b)
                for ch in range(2):
                    dve.wait_ge(turn_high, 2 * b + (ch + 1))
                    nc.vector.tensor_tensor(XT[1][:, ch, :], turned[ch][:, :], XT[0][:, ch, :].bitcast(fp32), ALU.subtract)\
                      .then_inc(turn_done, 1)
                n = [0]

                def stepped(ins):
                    ins.then_inc(route_steps, 1)
                    n[0] += 1
                    dve.wait_ge(route_steps, ROUTE_STEPS * b + n[0])

                dve.wait_ge(route_full, b + 1)
                stepped(nc.vector.tensor_tensor(logits[:, :, 0, :], routed[:, :, :],
                                                router_b[:, :].unsqueeze(1).broadcast_to([P, QT, E]), ALU.add))
                stepped(nc.vector.reduce_max(top[:, :], logits[:, :, 0, :], AX.X))
                stepped(nc.vector.tensor_tensor(less[:, :, :], logits[:, :, 0, :],
                                                top[:, :].unsqueeze(2).broadcast_to([P, QT, E]), ALU.subtract))
                rank_experts(nc, stepped, logits, rank, over, E)
                dve.wait_ge(exp_done, b + 1)
                stepped(nc.vector.reduce_sum(total[:, :], less[:, :, :], AX.X))
                stepped(nc.vector.reciprocal(weight[:, :], total[:, :]))
                stepped(nc.vector.tensor_scalar(pick[:, :, :], rank[:, :, 0, :], 0.5, None, ALU.is_lt))
                stepped(nc.vector.tensor_tensor(pick[:, :, :], pick[:, :, :],
                                                weight[:, :].unsqueeze(2).broadcast_to([P, QT, E]), ALU.mult))
                assert n[0] == ROUTE_STEPS
                for k in range(PER_BATCH):
                    t, pair = k // (E // 2), k % (E // 2)
                    dve.wait_ge(full, PER_BATCH * b + (k + 1))
                    if k:
                        dve.wait_ge(free[(k - 1) % BANKS], (PER_BATCH // BANKS) * b + (SETUP // BANKS + (k - 1) // BANKS + 1))
                    for i in range(2):
                        e = 2 * pair + i
                        ins = nc.vector.scalar_tensor_tensor(out=X[:, t, :], in0=ring[k % BANKS][:, i * D:(i + 1) * D],
                                                             scalar=pick[:, t, e:e + 1], in1=X[:, t, :],
                                                             op0=ALU.mult, op1=ALU.add)
                        if i == 0:
                            ins.then_inc(first_added, 1)
                            dve.wait_ge(first_added, PER_BATCH * b + (k + 1))
                        else:
                            ins.then_inc(free[k % BANKS], 1)

        @block.tensor
        def _(pe):
            pe.wait_ge(const_made, 4)
            pe.wait_ge(const_loaded, 96)
            for u in range(SETUP):
                ch, e = u % 2, u // 2
                if u >= BANKS:
                    pe.wait_ge(free[u % BANKS], u // BANKS)
                for c in range(2):
                    last = nc.tensor.transpose(ring[u % BANKS][:, c * P:(c + 1) * P], raw[:, 2 * e + c, ch * P:(ch + 1) * P],
                                               ident[:, :])
                last.then_inc(w_full, 1)
            pe.wait_ge(router_split, 2)
            pe.wait_ge(bias_steps, 3)
            with pe.Fori(0, B) as b:
                pe.wait_ge(norm_steps, NORM_STEPS * b + NORM_STEPS)
                for ch in range(2):
                    for t in range(QT):
                        last = nc.tensor.transpose(turned[ch][:, t * P:(t + 1) * P], XN[:, t, ch * P:(ch + 1) * P], ident[:, :])
                    last.then_inc(turn_full, 1)
                pe.wait_ge(turn_done, 2 * b + 2)
                for t in range(QT):
                    ts = slice(t * P, (t + 1) * P)
                    for i, (a, w, ch) in enumerate([(a, w, ch) for ch in range(2) for a, w in ((0, 0), (0, 1), (1, 0))]):
                        last = nc.tensor.matmul(routed[:, t, :], XT[a][:, ch, ts], router[w][:, ch, :],
                                                start=(i == 0), stop=(i == 5))
                last.then_inc(route_full, 1)
                for k in range(PER_BATCH):
                    t, pair = k // (E // 2), k % (E // 2)
                    ts, es = slice(t * P, (t + 1) * P), slice(pair * 512, pair * 512 + 512)
                    pe.wait_ge(free[k % BANKS], (PER_BATCH // BANKS) * b + (SETUP // BANKS + k // BANKS))
                    nc.tensor.matmul(ring[k % BANKS][:, :], ones[:, :], bias[:, es], start=True, stop=False)
                    for i, (a, w, ch) in enumerate([(a, w, ch) for ch in range(2) for a, w in ((0, 0), (0, 1), (1, 0))]):
                        last = nc.tensor.matmul(ring[k % BANKS][:, :], XT[a][:, ch, ts], W[w][:, ch, es], start=False,
                                                stop=(i == 5))
                    last.then_inc(full, 1)


def latent_weights(i):
    return {"slices": [(i["L0_xattn_Wq"], 0), (i["L0_xattn_Wkv"], 0), (i["L0_xattn_Wkv"], 1024)],
            "Wo": i["L0_xattn_Wo"], "bo": i["L0_xattn_bo"], "cos": i["L0_xattn_cos"], "sin": i["L0_xattn_sin"],
            "gx": i["L0_xattn_ln_lat_g"], "bx": i["L0_xattn_ln_lat_b"], "gc": i["L0_xattn_ln_ctx_g"],
            "bc": i["L0_xattn_ln_ctx_b"]}


def cross_weights(i):
    flat = {w: i[f"L1_xattn_{w}"].rearrange("d h k -> d (h k)") for w in ("Wq", "Wk", "Wv")}
    return {"slices": [(flat["Wq"], 0), (flat["Wk"], 0), (flat["Wv"], 0)],
            "Wo": i["L1_xattn_Wo"].rearrange("h k d -> (h k) d"), "bo": i["L1_xattn_bo"],
            **{b: i[f"L1_xattn_{b}"].rearrange("h k -> (h k)") for b in ("bq", "bk", "bv")}}


def self_weights(i):
    return {"slices": [(i["L1_ffn_Wq"], 0), (i["L1_ffn_Wk"], 0)], "Wo": i["L1_ffn_Wo"].rearrange("e k d -> (e k) d"),
            "Wv": i["L1_ffn_Wv"], "Ws": i["L1_ffn_Ws"], "Wd": i["L1_ffn_Wd"]}


def build(nc, ins, out):
    B, S, _ = ins["x"].shape
    assert S == NQ
    KEYS = ins["ctx_1024"].shape[1]
    between = [nc.dram_tensor(f"x_after_{i}", (B * S, D), mybir.dt.float32).ap() for i in range(3)]
    x, y = ins["x"].rearrange("b n d -> (b n) d"), out.rearrange("b n d -> (b n) d")
    context = ins["ctx_1024"].rearrange("b n d -> (b n) d")
    attention_layer(nc, "latent", "latent", x, between[0], context, latent_weights(ins), B, 8, KEYS // P)
    expert_layer(nc, "experts", between[0], between[1], ins, B)
    attention_layer(nc, "cross", "cross", between[1], between[2], context, cross_weights(ins), B, 8, KEYS // P)
    attention_layer(nc, "self", "self", between[2], y, None, self_weights(ins), B, 4, S // P)


_INS = ["x", "ctx_1024", "L0_xattn_cos", "L0_xattn_sin", "L0_xattn_ln_lat_g", "L0_xattn_ln_lat_b", "L0_xattn_ln_ctx_g",
        "L0_xattn_ln_ctx_b", "L0_xattn_Wq", "L0_xattn_Wkv", "L0_xattn_Wo", "L0_xattn_bo", "L0_ffn_router_w",
        "L0_ffn_router_b", "L0_ffn_expert_w", "L0_ffn_expert_b", "L1_xattn_Wq", "L1_xattn_bq", "L1_xattn_Wk",
        "L1_xattn_bk", "L1_xattn_Wv", "L1_xattn_bv", "L1_xattn_Wo", "L1_xattn_bo", "L1_ffn_Wq", "L1_ffn_Wk", "L1_ffn_Ws",
        "L1_ffn_Wd", "L1_ffn_Wv", "L1_ffn_Wo"]


def kernel(**inputs):
    import numpy as _np
    import concourse.bacc as _bacc
    from concourse import mybir as _mybir
    from concourse.bass_utils import run_bass_kernel_spmd as _run

    nc = _bacc.Bacc("TRN2", target_bir_lowering=False, num_devices=1)
    arrays, ins = {}, {}
    for name in _INS:
        a = _np.ascontiguousarray(inputs[name])
        arrays[f"in_{name}_dram"] = a
        ins[name] = nc.dram_tensor(f"in_{name}_dram", a.shape, _mybir.dt.from_np(a.dtype), kind="ExternalInput").ap()
    shape = inputs["x"].shape
    out = nc.dram_tensor("out_0_dram", shape, _mybir.dt.float32, kind="ExternalOutput").ap()
    build(nc, ins, out)
    r = _run(nc, [arrays], core_ids=[0])
    return r.results[0]["out_0_dram"]
```

```python
from contextlib import ExitStack, contextmanager
from math import exp

import concourse.bass as bass
from concourse import mybir

P = 128
D = 256
NQ = 512
QT = NQ // P
DH = 64
EPS = 1e-5
CLIP = 11.0
SCALE = DH ** -0.5
EXPERTS = 5
ROUTED = 8
AHEAD = 2
BEHIND = {"latent": [1, 0, 0, 2, 1, 0, 1, 1, 0, 0, 0, 2, 0, 0, 0, 0],
          "cross": [2, 1, 0, 7, 0, 0, 2, 1, 5, 2, 0, 3, 4, 0, 2, 1],
          "self": [2, 2, 0, 2, 7, 6, 3, 2]}
SUM_AFTER = {"latent": 2, "cross": 2, "self": 7}
FINISH_AFTER = {"latent": 0, "cross": 7, "self": 10}


class Count:

    def __init__(self):
        self.turns, self.here = 0, 0

    @property
    def value(self):
        return self.turns + self.here


class Place:

    UNITS = ("turn", "gate", "kv", "k", "kT", "q", "max", "shift", "sum", "back", "mixT", "out")
    KINDS = UNITS + ("moments_x", "moments_c", "scaled_x", "scaled_c", "split", "top", "biases", "biased", "load", "masks",
                     "vmix", "kept")

    def __init__(self):
        self.n = {kind: Count() for kind in self.KINDS}
        self.units = Count()
        self.bank = [Count(), Count()]
        self.attends = Count()

    def counts(self):
        return [self.units, *self.bank, self.attends, *self.n.values()]

    def __getitem__(self, kind):
        return self.n[kind].value

    @property
    def ring(self):
        return self.units.here % 2

    def passed(self, item):
        kind = item[0]
        if kind in self.UNITS:
            self.bank[self.ring].here += 1
            self.units.here += 1
        if kind in ("mix", "vmix") and item[1] < EXPERTS - 1:
            return
        if kind in ("moments", "scaled"):
            kind = f"{kind}_{item[1]}"
        if kind == "end":
            self.attends.here += 1
        elif kind in self.n:
            self.n[kind].here += 1
        if kind == "max" and item[4]:
            self.n["top"].here += 1

    def mark(self):
        return [bank.value for bank in self.bank]


@contextmanager
def turns(eng, trips, place, plans):
    dry = Place()
    for plan in plans:
        for item in plan:
            dry.passed(item)
    gain = [count.here for count in dry.counts()]
    assert gain[0] % 2 == 0, "a turn leaves the ring's banks in step"
    was = [(count.turns, count.here) for count in place.counts()]
    with eng.Fori(0, trips) as i:
        for count, k in zip(place.counts(), gain):
            if k:
                count.turns = count.turns + i * k
        yield i
        for count, k, (_, here) in zip(place.counts(), gain, was):
            assert count.here == here + k
    for count, k, (turned, here) in zip(place.counts(), gain, was):
        count.turns, count.here = turned, here + trips * k


def attend_order(NC, late):
    order = []
    for c in range(NC):
        order += [[("S", 0, c)], [("S", 1, c), ("soft", 0, c)]]
        if c or late:
            order += [[("AV", c - 1, 0), ("soft", 1, c)], [("AV", c - 1, 1)]]
        else:
            order[-1] += [("soft", 1, c)]
    order[-1] += [("end",)]
    return order


def prepare_order(kind, KT):
    if kind == "self":
        units = [("k",), ("q",)]
    else:
        units = [("q",)] + [("kv", t) for t in range(KT // 2)] + [("kT", i) for i in range(KT // 4)]
    if kind == "latent":
        return units
    if kind == "cross":
        units = [("biases",)] + units
    halves = KT // 4
    maxima = [[("max", h, qt, i, (qt, i) == (QT - 1, halves - 1)) for qt in range(QT) for i in range(halves)]
              for h in range(2)]
    mid = len(maxima[1]) // 2
    behind = maxima[1][mid:] + [("shift", 1)]
    if kind == "self":
        mixing = [("vmix", e) for e in range(EXPERTS)]
        behind = [item for pair in zip(mixing, behind) for item in pair] + mixing[len(behind):]
    return units + maxima[0] + maxima[1][:mid] + [("shift", 0)] + behind


def enter_order(kind, KT):
    turn_x = [("turn", "x", ch, 0) for ch in range(2)]
    if kind == "self":
        return turn_x + [("turned",)] + [("gate", t) for t in range(QT)]
    turn_c = [("turn", "c", ch, g) for g in range(KT // 4) for ch in range(2)]
    return turn_x + turn_c + [("turned",)]


def with_masks(units):
    at = units.index(("vmix", 0)) if ("vmix", 0) in units else 0
    return units[:at] + [("masks",)] * (("vmix", 0) in units) + units[at:]


def norm_order(kind):
    return [(what, of) for of in {"latent": "xxc"}.get(kind, "x") for what in ("moments", "scaled")]


def among(plan, extras):
    out, n = [], len(plan)
    at = [round((k + 1.5) / (len(extras) + 1.5) * n) for k in range(len(extras))]
    for i, item in enumerate(plan):
        out += [extra for extra, j in zip(extras, at) if j == i] + [item]
    assert len(out) == n + len(extras)
    return out


def step_plan(kind, KT, attend, prepare, finish, split=False, enter=False):
    begin = [("split", None)] if split else []
    finish_order = {"latent": [], "cross": [("biased",)], "self": [("back",)] + [("mix", e) for e in range(EXPERTS)]}[kind]
    finishing = [("sum",)] + finish_order if finish else []
    preparing = prepare_order(kind, KT) if prepare else []
    if not attend:
        return begin + ([("AV", -1, 0), ("AV", -1, 1)] if finish else []) + finishing + preparing
    order, counts = attend_order(KT // 2, finish), list(BEHIND[kind])
    if not finish:
        counts = [counts[0], sum(counts[1:4])] + counts[4:]
    at = SUM_AFTER[kind]
    between = preparing[:at] + finishing[:1] + preparing[at:]
    at = FINISH_AFTER[kind]
    for k, item in enumerate(finishing[1:]):
        between.insert(at + 2 * k, item)
    if not preparing:
        counts = [0, 0, 0, 3, 1, 1, 1, 1]
    if enter:
        order[3] = order[3] + finishing[:1]
        for k, item in enumerate(finishing[1:]):
            order[min(5 + k, len(order) - 1)].append(item)
        between = enter_order(kind, KT) + with_masks(preparing)
        n = len(between)
        counts = [(i + 1) * n // len(order) - i * n // len(order) for i in range(len(order))]
    plan = begin
    for i, items in enumerate(order):
        n = counts[i] if i < len(counts) else 0
        plan = plan + items + between[:n]
        between = between[n:]
    assert not between, "the slots hold all"
    return plan


def take_moments(nc, dve, tiles, sems, src, n, base):
    stats, mv, varr, _, _, carrier = tiles
    norm_steps, var_ready, _ = sems
    for t in range(n):
        nc.vector.bn_stats(stats[:, t, :], src(t)).then_inc(norm_steps, 1)
    dve.wait_ge(norm_steps, base + n)
    nc.vector.memset(carrier[:, :], 0.0)
    for t in range(n):
        nc.vector.bn_aggr(mv[:, t, :], stats[:, t, :]).then_inc(norm_steps, 1)
    dve.wait_ge(norm_steps, base + 2 * n)
    nc.vector.tensor_scalar(varr[:, 0:n], mv[:, 0:n, 1], EPS, None, mybir.AluOpType.add).then_inc(var_ready, 1)


def scale_rows(nc, dve, tiles, sems, src, dst, n, base, rounds):
    ALU = mybir.AluOpType
    _, mv, varr, rstd, newton, _ = tiles
    norm_steps, _, rsqrt_ready = sems
    dve.wait_ge(rsqrt_ready, rounds + 1)
    nc.vector.tensor_tensor(newton[0][:, 0:n], rstd[:, 0:n], rstd[:, 0:n], ALU.mult).then_inc(norm_steps, 1)
    dve.wait_ge(norm_steps, base + 1)
    nc.vector.tensor_tensor(newton[1][:, 0:n], newton[0][:, 0:n], varr[:, 0:n], ALU.mult).then_inc(norm_steps, 1)
    dve.wait_ge(norm_steps, base + 2)
    nc.vector.tensor_scalar(newton[2][:, 0:n], newton[1][:, 0:n], -0.5, 1.5, ALU.mult, ALU.add).then_inc(norm_steps, 1)
    dve.wait_ge(norm_steps, base + 3)
    nc.vector.tensor_tensor(newton[3][:, 0:n], newton[2][:, 0:n], rstd[:, 0:n], ALU.mult).then_inc(norm_steps, 1)
    dve.wait_ge(norm_steps, base + 4)
    for t in range(n):
        nc.vector.tensor_scalar(dst[:, t, :], src(t), mv[:, t, 0:1], newton[3][:, t:t + 1], ALU.subtract, ALU.mult)\
          .then_inc(norm_steps, 1)


def rank_experts(nc, stepped, logits, rank, over, count):
    ALU = mybir.AluOpType
    stepped(nc.vector.memset(rank[:, :, :, :], 0.0))
    for j in range(count):
        for lo, hi, op in ((0, j, ALU.is_gt), (j + 1, count, ALU.is_ge)):
            if lo < hi:
                shape = [*logits.shape[:3], hi - lo]
                stepped(nc.vector.tensor_tensor(over[:, :, :, lo:hi], logits[:, :, :, j:j + 1].broadcast_to(shape),
                                                logits[:, :, :, lo:hi], op))
                stepped(nc.vector.tensor_tensor(rank[:, :, :, lo:hi], rank[:, :, :, lo:hi], over[:, :, :, lo:hi], ALU.add))


def attention_layer(nc, name, kind, x_in, x_out, context, weights, B, NP, KT):
    fp32, f32r = mybir.dt.float32, mybir.dt.float32r
    ALU, ACT, AX = mybir.AluOpType, mybir.ActivationFunctionType, mybir.AxisListType
    latent, cross, own = kind == "latent", kind == "cross", kind == "self"
    shifted = not latent
    NC = KT // 2
    KEYS = KT * P
    HALVES = KEYS // 512
    HEADS = 2 * NP
    NW = P * len(weights["slices"])
    NV = EXPERTS * DH
    NGATE = NV + 2 * HEADS * EXPERTS
    MAIN = (slice(0, 64), slice(64, 128))
    AUX = (slice(64, 128), slice(0, 64))

    ctx = ExitStack()
    with ctx:
        def sb(label, shape, dt=fp32):
            return ctx.enter_context(nc.sbuf_tensor(f"{name}_{label}", shape, dt))

        def sem(label, used=True):
            return ctx.enter_context(nc.semaphore(f"{name}_{label}")) if used else None

        X, XN = sb("X", [P, QT, D]), sb("XN", [P, QT, D])
        XTH, XTL = sb("XTH", [P, 2, NQ], f32r), sb("XTL", [P, 2, NQ], f32r)
        staging = [sb(f"staging{i}", [P, 512]) for i in range(2)]
        WRAW = sb("WRAW", [P, 2, NW])
        WH = [sb(f"WH{i}", [P, 2, NW], f32r) for i in range(2)]
        WL = [sb(f"WL{i}", [P, 2, NW], f32r) for i in range(2)]
        S1 = [sb(f"S1{i}", [P, 2, KEYS], f32r) for i in range(2)]
        S2 = [sb(f"S2{i}", [P, 2, KEYS], f32r) for i in range(2)] if shifted else S1
        Q1 = [sb(f"Q1{i}", [P, 2, NQ], f32r) for i in range(2)]
        Q2 = [sb(f"Q2{i}", [P, 2, NQ], f32r) for i in range(2)]
        probs = [[sb(f"probs{h}{i}", [P, 2, NQ]) for i in range(2)] for h in range(2)]
        acc = [sb(f"acc{h}", [P, 2, NQ]) for h in range(2)]
        folded = [sb(f"folded{h}", [P, NQ]) for h in range(2)]
        sums, recip = sb("sums", [P, NQ]), sb("recip", [P, NQ])
        ident, ones = sb("ident", [P, P]), sb("ones", [P, DH])
        neghalf, scale = sb("neghalf", [P, KT]), sb("scale", [P, 2])
        stats, mv = sb("stats", [P, KT, 6]), sb("mv", [P, KT, 2])
        varr, rstd = sb("varr", [P, KT]), sb("rstd", [P, KT])
        newton = [sb(f"newton{i}", [P, KT]) for i in range(4)]
        prime, carrier, primes = sb("prime", [P, 1]), sb("carrier", [P, 1]), sb("primes", [P, 20])
        VN = [sb(f"VN{i}", [P, KT, 256 if cross else 128]) for i in range(2)]
        VC = 128 if cross else 0
        if not own:
            C = sb("C", [P, KT, D])
            CTH, CTL = sb("CTH", [P, 2, KEYS], f32r), sb("CTL", [P, 2, KEYS], f32r)
            OT = sb("OT", [P, NP, NQ])
            WO = sb("WO", [P, NP, D])
            bo = sb("bo", [P, D])
        if latent:
            KR = sb("KR", [P, KT, P])
            cos, sin, nsin = (sb(n, [P, KT, 32]) for n in ("cos", "sin", "nsin"))
            rot1s, rot2s = ([sb(f"{n}{i}", [P, 2, P]) for i in range(2)] for n in ("rot1", "rot2"))
            gbx, gbc = sb("gbx", [P, 2, 2]), sb("gbc", [P, 2, 2])
        else:
            O32 = sb("O32", [P, NQ])
            part = sb("part", [P, 2, QT, HALVES])
            top, negtop = sb("top", [P, 2, QT]), sb("negtop", [P, 2, QT])
            diag = [sb(f"diag{h}", [P, QT, P], f32r) for h in range(2)]
            spread = sb("spread", [P, P], f32r)
        if cross:
            bqkv = sb("bqkv", [P, 3, NP])
            pair_bias = [sb(f"pair_bias{i}", [P, 2]) for i in range(2)]
        if own:
            WO = sb("WO", [P, 3, D])
            gates_raw = sb("gates_raw", [P, 2, NGATE])
            gates_hi, gates_lo = sb("gates_hi", [P, 2, NGATE], f32r), sb("gates_lo", [P, 2, NGATE], f32r)
            gated = sb("gated", [P, QT, NGATE])
            rank = sb("rank", [P, QT, 2 * HEADS, EXPERTS])
            over = sb("over", [P, QT, 2 * HEADS, EXPERTS])
            out_mask = sb("out_mask", [P, QT, HEADS, EXPERTS])
            sigm = sb("sigm", [P, QT, HEADS * EXPERTS])
            v_part, v_joined = sb("v_part", [P, QT, 2, DH]), sb("v_joined", [P, QT, DH])
            masked, joined = sb("masked", [P, QT, 2, DH]), sb("joined", [P, QT, DH])
            natural = [sb(f"natural{i}", [P, QT, P]) for i in range(2)]
            mixed = sb("mixed", [P, QT, 3 * P])
            mixedT = sb("mixedT", [P, 3, NQ])

        scores = [ctx.enter_context(nc.psum_tensor(f"{name}_scores{h}", [P, 2, NQ], fp32)) for h in range(2)]
        outT = [ctx.enter_context(nc.psum_tensor(f"{name}_outT{i}", [P, NQ], fp32)) for i in range(2)]
        ring = [ctx.enter_context(nc.psum_tensor(f"{name}_ring{i}", [P, 512], fp32)) for i in range(2)]

        x_loaded, rows_loaded, c_loaded, w_loaded = (sem(n) for n in ("x_loaded", "rows_loaded", "c_loaded", "w_loaded"))
        const_loaded, const_set, const_made = sem("const_loaded"), sem("const_set"), sem("const_made")
        x_stored = sem("x_stored")
        norm_steps, var_ready, rsqrt_ready = sem("norm_steps"), sem("var_ready"), sem("rsqrt_ready")
        w_scaled, w_high, w_split = sem("w_scaled"), sem("w_high"), sem("w_split")
        full = sem("full")
        free = [sem(f"free{i}") for i in range(2)]
        staged, turn_high, high = sem("staged"), sem("turn_high"), sem("high")
        v_copied, rotated = (sem(n, latent) for n in ("v_copied", "rotated"))
        top_found, negtop_ready, diag_ready = (sem(n, shifted) for n in ("top_found", "negtop_ready", "diag_ready"))
        s_full, exp_done, clipped, av_done = sem("s_full"), sem("exp_done"), sem("clipped", latent), sem("av_done")
        added = [sem(f"added{h}") for h in range(2)]
        fold_done = [sem(f"fold_done{h}") for h in range(2)]
        normed, recip_made, copied = sem("normed"), sem("recip_made"), sem("copied")
        rows_biased, out_biased, biases_ready = sem("rows_biased", not own), sem("out_biased", cross), sem("biases_ready", cross)
        gate_exp, gate_steps, v_steps, mask_kept, mix_steps, last_mix_steps = (
            sem(n, own) for n in ("gate_exp", "gate_steps", "v_steps", "mask_kept", "mix_steps", "last_mix_steps"))

        norm_tiles, norm_sems = (stats, mv, varr, rstd, newton, carrier), (norm_steps, var_ready, rsqrt_ready)
        p_ready, p_ahead = (clipped, 0) if latent else (exp_done, AHEAD)
        CONSTANTS = {"latent": 8, "cross": 5, "self": 4 + EXPERTS}[kind]
        MADE = {"latent": 9, "cross": 10, "self": 12}[kind]
        RANK_STEPS = 1 + 4 * (EXPERTS - 1)
        GATE_STEPS = RANK_STEPS + 4
        V_STEPS = 2 * EXPERTS - 1
        SHARE = 3

        def mix_steps_before(b, q):
            batch_steps = (3 * NP - 1) * EXPERTS - 3 * SHARE
            return b * batch_steps + (batch_steps if q == NP else (3 * q - 1) * EXPERTS if q else 0) + AHEAD

        head = [("load",)] + norm_order(kind) + [("split", 0), ("split", 1)] + enter_order(kind, KT)
        head += with_masks(step_plan(kind, KT, False, True, False))
        first_step = ([("kept",)] if own else []) + step_plan(kind, KT, True, True, False, split=True)
        step = step_plan(kind, KT, True, True, True, split=True)
        late_step = step_plan(kind, KT, True, True, True)
        last_step = step_plan(kind, KT, True, False, True)
        late_more = [("load",)] + among(step_plan(kind, KT, True, True, True, split=True), norm_order(kind))
        last_more = step_plan(kind, KT, True, True, True, split=True, enter=True)
        tail = step_plan(kind, KT, False, False, True)
        if own:
            tail += [("mixT", t) for t in range(QT)]
        tail += [("out", t) for t in range(QT)]

        def walk(eng, do):
            place = Place()

            def batch(b, late, last):
                do(place, b, 0, 0, first_step)
                loops = (NP - 3) // 2
                if loops:
                    with turns(eng, loops, place, [step, step]) as j:
                        do(place, b, 2 * j + 1, 1, step)
                        do(place, b, 2 * j + 2, 0, step)
                for p in range(1 + 2 * loops, NP - 2):
                    do(place, b, p, p % 2, step)
                do(place, b, NP - 2, NP % 2, late)
                do(place, b, NP - 1, 1 - NP % 2, last)
                do(place, b, NP, NP % 2, tail)

            do(place, 0, -1, 1, head)
            if B > 1:
                with turns(eng, B - 1, place, [first_step] + [step] * (NP - 3) + [late_more, last_more, tail]) as b:
                    batch(b, late_more, last_more)
            batch(B - 1, late_step, last_step)

        def following(p, ahead=1):
            return (p + ahead) % NP if isinstance(p, int) else p + ahead

        def evacuated(eng, mark):
            for i in range(2):
                eng.wait_ge(free[i], mark[i] + 1)

        behind_shift = QT * (KT // 4) // 2 + 1 if shifted else 0

        def copies(place):
            return place["q"] + place["k"] + place["kT"] if shifted else place["q"]

        def norm_count(place):
            return (AHEAD + place["moments_x"] * (2 * QT) + place["moments_c"] * (2 * KT) + place["scaled_x"] * (QT + 4)
                    + place["scaled_c"] * (KT + 4))

        def mix(eng, ops, q, e, turned_back, masked, joined, done, steps):
            eng.wait_ge(done, steps)
            pair = turned_back[:, :, :].rearrange("p t (h k) -> p t h k", h=2)
            into = mixed[:, :, e * DH:(e + 1) * DH]
            ops.tensor_tensor(masked[:, :, :, :], pair, out_mask[:, :, 2 * q:2 * q + 2, e:e + 1].broadcast_to([P, QT, 2, DH]),
                              ALU.mult).then_inc(done, 1)
            eng.wait_ge(done, steps + 1)
            ops.tensor_tensor(joined[:, :, :] if q else into, masked[:, :, 0, :], masked[:, :, 1, :], ALU.add).then_inc(done, 1)
            if q:
                eng.wait_ge(done, steps + 2)
                ops.tensor_tensor(into, into, joined[:, :, :], ALU.add).then_inc(done, 1)

        def add_up(eng, ops, place, h, c):
            steps = (NC - 1) * place.attends.value
            if c >= 1:
                eng.wait_ge(p_ready, place.attends.value * (2 * NC) + (2 * c + h + 1 + p_ahead))
                if c == 1:
                    eng.wait_ge(fold_done[h], place.attends.value + AHEAD)
                else:
                    eng.wait_ge(added[h], steps + (c - 1 + AHEAD))
                first = probs[h][0] if c == 1 else acc[h]
                ops.tensor_tensor(acc[h][:, :, :], first[:, :, :], probs[h][c % 2][:, :, :], ALU.add).then_inc(added[h], 1)
            if c == NC - 1:
                eng.wait_ge(added[h], steps + (NC - 1 + AHEAD))
                eng.wait_ge(normed, place["sum"] + AHEAD)
                ops.tensor_tensor(folded[h][:, :], acc[h][:, 0, :], acc[h][:, 1, :], ALU.add).then_inc(fold_done[h], 1)

        block = ctx.enter_context(nc.Block())

        @block.sync
        def _(sp):
            n_const = [0]

            def constant(dst, src, columns=False):
                sp.dma_start(dst, src, allow_slow_non_contiguous=columns).then_inc(const_loaded, 16)
                n_const[0] += 1

            if own:
                sp.wait_ge(const_set, 1)
                constant(WO[:, 0:2, :], weights["Wo"][0:256, :].rearrange("(c p) n -> p c n", p=P))
                constant(WO[0:64, 2, :], weights["Wo"][256:320, :])
                for e in range(EXPERTS):
                    constant(gates_raw[:, :, e * DH:(e + 1) * DH], weights["Wv"][e].rearrange("(c p) n -> p c n", p=P))
                for i, w in enumerate(("Ws", "Wd")):
                    at = NV + i * HEADS * EXPERTS
                    constant(gates_raw[:, :, at:at + HEADS * EXPERTS], weights[w].rearrange("(c p) n -> p c n", p=P))
            else:
                constant(WO[:, :, :], weights["Wo"].rearrange("(c p) n -> p c n", p=P))
                constant(bo[:, :], weights["bo"].rearrange("(a n) -> a n", a=1).broadcast_to([P, D]))
            if latent:
                constant(cos[:, :, :], weights["cos"].rearrange("(t p) n -> p t n", p=P))
                constant(sin[:, :, :], weights["sin"].rearrange("(t p) n -> p t n", p=P))
                for tile, g, b_ in ((gbx, "gx", "bx"), (gbc, "gc", "bc")):
                    constant(tile[:, 0, :], weights[g].rearrange("(c p) -> p c", p=P), columns=True)
                    constant(tile[:, 1, :], weights[b_].rearrange("(c p) -> p c", p=P), columns=True)
            if cross:
                for i, w in enumerate(("bq", "bk", "bv")):
                    constant(bqkv[:, i, :], weights[w].rearrange("(c p) -> p c", p=P), columns=True)
            assert n_const[0] == CONSTANTS

            def do(place, b, p, par, plan):
                for item in plan:
                    if item[0] == "load":
                        sp.wait_ge(full, place.units.value + AHEAD)
                        sp.dma_start(XN[:, :, :], x_in[bass.ds(place["load"] * NQ, NQ), :].rearrange("(t p) d -> p t d", p=P))\
                          .then_inc(rows_loaded, 16)
                        if not own:
                            sp.dma_start(C[:, :, :], context[bass.ds(place["load"] * KEYS, KEYS), :]
                                         .rearrange("(t p) d -> p t d", p=P)).then_inc(c_loaded, 16)
                    elif item[0] == "split":
                        sp.wait_ge(w_split, place["split"] + 1)
                        at = (following(p, 2) if item[1] is None else item[1]) * P
                        for i, (w, off) in enumerate(weights["slices"]):
                            sp.dma_start(WRAW[:, :, i * P:(i + 1) * P],
                                         w[:, bass.ds(at + off, P)].rearrange("(c p) n -> p c n", p=P)).then_inc(w_loaded, 16)
                    place.passed(item)
                if plan is first_step:
                    sp.wait_ge(x_stored, 16 * b + 16)
                    sp.dma_start(X[:, :, :], x_in[bass.ds(b * NQ, NQ), :].rearrange("(t p) d -> p t d", p=P))\
                      .then_inc(x_loaded, 16)
                if plan is tail:
                    sp.wait_ge(free[1 - place.ring], place.mark()[1 - place.ring] + 1)
                    sp.dma_start(x_out[bass.ds(b * NQ, NQ), :].rearrange("(t p) d -> p t d", p=P), X[:, :, :])\
                      .then_inc(x_stored, 16)

            walk(sp, do)
            sp.wait_ge(x_stored, 16 * B + 16)

        @block.gpsimd
        def _(pool):
            nc.gpsimd.memset(WO[:, 2, :] if own else prime[:, :], 0.0).then_inc(const_set, 1)
            nc.gpsimd.memset(ident[:, :], 0.0).then_inc(const_set, 1)
            pool.wait_ge(const_set, 2)
            nc.gpsimd.affine_select(out=ident[:, :], in_=ident[:, :], compare_op=ALU.not_equal, fill=1.0, base=0,
                                    pattern=[[-1, P]], channel_multiplier=1).then_inc(const_made, 1)
            nc.gpsimd.memset(ones[:, :], 1.0).then_inc(const_made, 1)
            nc.gpsimd.memset(neghalf[:, :], -0.5).then_inc(const_made, 1)
            nc.gpsimd.memset(scale[:, :], SCALE).then_inc(const_made, 1)
            if shifted:
                nc.gpsimd.memset(spread[:, :].bitcast(fp32), 1.0 / DH).then_inc(const_made, 1)
            for i in range(2):
                for h in range(2):
                    tile, value = (S2[i], 1.0) if shifted else (Q2[i], 0.0)
                    pool.wait_ge(const_made, 4 + shifted + 2 * i + h)
                    nc.gpsimd.memset(tile[AUX[h], h, :].bitcast(fp32), value).then_inc(const_made, 1)
            pool.wait_ge(const_loaded, 16 * CONSTANTS)
            if latent:
                nc.gpsimd.tensor_scalar(nsin[:, :, :], sin[:, :, :], -1.0, None, ALU.mult).then_inc(const_made, 1)
            if cross:
                nc.gpsimd.tensor_scalar(bqkv[:, 0, :], bqkv[:, 0, :], SCALE, None, ALU.mult).then_inc(const_made, 1)
            if own:
                nc.gpsimd.memset(mixed[:, :, :], 0.0).then_inc(const_made, 1)
                nc.gpsimd.tensor_copy(gates_hi[:, :, :], gates_raw[:, :, :]).then_inc(const_made, 1)
                pool.wait_ge(const_made, MADE - 1)
                nc.gpsimd.tensor_tensor(gates_lo[:, :, :], gates_raw[:, :, :], gates_hi[:, :, :].bitcast(fp32),
                                        ALU.subtract).then_inc(const_made, 1)
            pool.wait_ge(const_made, MADE)
            ahead = [(free[0], 1), (free[1], 1), (w_split, 1), (x_stored, 16)]
            ahead += [(s, AHEAD) for s in (full, exp_done, av_done, *added, *fold_done, normed, norm_steps, out_biased, rotated,
                                           v_steps, mask_kept, mix_steps, last_mix_steps) if s is not None]
            for i, (s, k) in enumerate(ahead):
                nc.gpsimd.memset(primes[:, i:i + 1], 0.0).then_inc(s, k)

            def do(place, b, p, par, plan):
                for item in plan:
                    if item[0] == "moments":
                        n = QT if item[1] == "x" else KT
                        pool.wait_ge(var_ready, place["moments_x"] + place["moments_c"] + 1)
                        nc.gpsimd.tensor_tensor(rstd[:, 0:n], varr[:, 0:n], neghalf[:, 0:n], ALU.pow)\
                          .then_inc(rsqrt_ready, 1)
                    elif item[0] == "split":
                        i = par if item[1] is None else item[1]
                        pool.wait_ge(w_loaded, 16 * len(weights["slices"]) * (place["split"] + 1))
                        pool.wait_ge(full, place.units.value + AHEAD)
                        nc.gpsimd.tensor_tensor(WRAW[:, :, 0:P], WRAW[:, :, 0:P],
                                                scale[:, :].unsqueeze(2).broadcast_to([P, 2, P]), ALU.mult).then_inc(w_scaled, 1)
                        pool.wait_ge(w_scaled, place["split"] + 1)
                        nc.gpsimd.tensor_tensor(WH[i][:, :, :], WRAW[:, :, :], ones[:, 0:2].unsqueeze(2).broadcast_to([P, 2, NW]),
                                                ALU.mult).then_inc(w_high, 1)
                        pool.wait_ge(w_high, place["split"] + 1)
                        nc.gpsimd.tensor_tensor(WL[i][:, :, :], WRAW[:, :, :], WH[i][:, :, :].bitcast(fp32), ALU.subtract)\
                          .then_inc(w_split, 1)
                    elif item[0] == "mix" and not (plan is tail and item[1] < SHARE):
                        q, e = p - 1, item[1]
                        begun = SHARE if plan is tail else 0
                        if e == begun:
                            evacuated(pool, place.mark())
                            pool.wait_ge(mask_kept, place["kept"] + AHEAD)
                            if q == 0:
                                pool.wait_ge(full, place.units.value + AHEAD)
                        mix(pool, nc.gpsimd, q, e, natural[1 - par], masked, joined, mix_steps,
                            mix_steps_before(b, q) + (3 if q else 2) * (e - begun))
                    elif item[0] == "kv" and latent:
                        t = item[1]
                        pool.wait_ge(free[place.ring], place.bank[place.ring].value + 2)
                        nc.gpsimd.tensor_tensor(KR[:, 2 * t:2 * t + 2, :], rot1s[t % 2][:, :, :], rot2s[t % 2][:, :, :], ALU.add)\
                          .then_inc(rotated, 1)
                    elif item[0] == "soft" and item[1] == 1:
                        add_up(pool, nc.gpsimd, place, 1, item[2])
                    elif item[0] == "max" and item[4] and cross:
                        h = item[1]
                        pool.wait_ge(negtop_ready, place["top"] + 1)
                        nc.gpsimd.tensor_tensor(diag[h][:, :, :], ident[:, :].unsqueeze(1).broadcast_to([P, QT, P]),
                                                negtop[:, h, :].unsqueeze(2).broadcast_to([P, QT, P]), ALU.mult)\
                          .then_inc(diag_ready, 1)
                    place.passed(item)

            walk(pool, do)

        @block.scalar
        def _(act):
            act.wait_ge(const_made, MADE)
            waited = act.alloc_register(f"{name}_waited")
            act.reg_mov(waited, 0)

            def take_wait():
                act.reg_add(waited, waited, 1)

            def do(place, b, p, par, plan):
                nxt = 1 - par
                for item in plan:
                    u = item[0]
                    bank = ring[place.ring]
                    if u in Place.UNITS and u not in ("max", "out"):
                        act.wait_ge(full, place.units.value + (1 + AHEAD))
                    taken = free[place.ring]
                    if u == "turn":
                        gb = {"x": gbx, "c": gbc}[item[1]] if latent else None
                        ch = item[2]
                        nc.scalar.activation(staging[place.ring][:, :], bank[:, :], ACT.Identity,
                                             scale=gb[:, 0, ch:ch + 1] if latent else 1.0,
                                             bias=gb[:, 1, ch:ch + 1] if latent else 0.0).then_inc(staged, 1)
                    elif u == "gate":
                        if item[1] == 0:
                            act.wait_ge(v_steps, V_STEPS * place["vmix"] + AHEAD)
                        nc.scalar.activation(gated[:, item[1], :], bank[:, 0:NGATE], ACT.Copy).then_inc(taken, 1)
                    elif u == "masks":
                        evacuated(act, place.mark())
                        nc.scalar.activation(sigm[:, :, :], gated[:, :, NV:NV + HEADS * EXPERTS], ACT.Exp, scale=-1.0)\
                          .then_inc(gate_exp, 1)
                    elif u == "biases":
                        nc.scalar.activation(pair_bias[nxt][:, :].unsqueeze(2), bqkv[:, 0:2, bass.ds(following(p), 1)], ACT.Copy)\
                          .then_inc(biases_ready, 1)
                    elif u == "kv":
                        t = item[1]
                        src = bank[:, :].rearrange("p (s n) -> p s n", s=2)
                        if t == 0:
                            act.wait_ge(av_done, NC * place.attends.value + AHEAD)
                        if latent:
                            nc.scalar.activation(VN[nxt][:, 2 * t:2 * t + 2, :], src[:, :, 128:256], ACT.Copy)\
                              .then_inc(v_copied, 1)
                        else:
                            nc.scalar.activation(VN[nxt][:, 2 * t:2 * t + 2, :], src[:, :, :], ACT.Copy).then_inc(taken, 1)
                    elif u in ("k", "kT"):
                        cols = slice(item[1] * 512, item[1] * 512 + 512) if u == "kT" else slice(0, 512)
                        for h in range(2):
                            last = nc.scalar.activation(S1[nxt][MAIN[h], h, cols], bank[MAIN[h], :], ACT.Identity,
                                                        bias=pair_bias[nxt][MAIN[h], 1:2] if cross else 0.0)
                        last.then_inc(high, 1)
                        if own or cross and item[1] == HALVES - 1:
                            act.wait_ge(high, place["k"] + place["kT"] + place["q"] + 1)
                            for h in range(2):
                                last = nc.scalar.activation(S2[nxt][MAIN[h], h, :], S1[nxt][MAIN[h], h, :].bitcast(fp32),
                                                            ACT.Copy)
                            last.then_inc(copied, HALVES)
                    elif u == "q":
                        if cross:
                            act.wait_ge(biases_ready, place["biases"])
                        for h in range(2):
                            last = nc.scalar.activation(Q1[nxt][MAIN[h], h, :], bank[MAIN[h], :], ACT.Identity,
                                                        bias=pair_bias[nxt][MAIN[h], 0:1] if cross else 0.0)
                        last.then_inc(high, 1)
                        act.wait_ge(high, place["k"] + place["kT"] + place["q"] + 1)
                        for h in range(2):
                            last = nc.scalar.activation(Q1[nxt][AUX[h], h, :], Q1[nxt][MAIN[h], h, :].bitcast(fp32), ACT.Copy)
                        last.then_inc(copied, 1)
                    elif u == "shift":
                        h = item[1]
                        nc.scalar.activation(Q2[nxt][AUX[h], h, :], bank[AUX[h], :], ACT.Copy).then_inc(taken, 1)
                    elif u == "S":
                        _, h, c = item
                        act.wait_ge(s_full, place.attends.value * (2 * NC) + (2 * c + h + 1))
                        act.wait_ge(av_done, place.attends.value * NC + (c - 1 + AHEAD))
                        rel = max(NC - 2, 1) - (NC - 1) if c == 0 else 0 if c == 1 else 1
                        act.wait_ge(added[h], place.attends.value * (NC - 1) + (rel + AHEAD))
                        nc.scalar.activation(probs[h][c % 2][:, :, :], scores[h][:, :, :], ACT.Exp).then_inc(exp_done, 1)
                    elif u == "sum":
                        act.wait_ge(normed, place["sum"] + AHEAD)
                        nc.scalar.activation(sums[:, :], bank[:, :], ACT.Copy).then_inc(taken, 1)
                    elif u == "biased":
                        act.wait_ge(normed, place["sum"] + AHEAD)
                        take_wait()
                        nc.scalar.activation(OT[:, bass.ds(p - 1, 1), :], O32[:, :].unsqueeze(1), ACT.Identity,
                                             bias=bqkv[:, 2, bass.ds(p - 1, 1)]).then_inc(out_biased, 1)
                    elif u == "back":
                        act.wait_ge(mix_steps, mix_steps_before(b, max(p - 2, 0)))
                        nc.scalar.activation(natural[nxt][:, :, :],
                                             bank[:, :].rearrange("p (t n) -> p t n", t=QT), ACT.Copy).then_inc(taken, 1)
                    elif u == "mixT":
                        nc.scalar.activation(mixedT[:, :, item[1] * P:(item[1] + 1) * P],
                                             bank[:, 0:3 * P].rearrange("p (c n) -> p c n", c=3), ACT.Copy).then_inc(taken, 1)
                    place.passed(item)

            walk(act, do)

        @block.vector
        def _(dve):
            dve.wait_ge(const_made, MADE)

            def masks(place, b):
                base = place["masks"] * GATE_STEPS
                n = [0]

                def stepped(ins):
                    ins.then_inc(gate_steps, 1)
                    n[0] += 1
                    dve.wait_ge(gate_steps, base + n[0])

                G = gated[:, :, NV:NGATE].rearrange("p t (g e) -> p t g e", e=EXPERTS)
                rank_experts(nc, stepped, G, rank, over, EXPERTS)
                stepped(nc.vector.tensor_scalar(rank[:, :, :, :], rank[:, :, :, :], 1.5, None, ALU.is_lt))
                dve.wait_ge(gate_exp, place["masks"] + 1)
                stepped(nc.vector.tensor_scalar(sigm[:, :, :], sigm[:, :, :], 1.0, None, ALU.add))
                stepped(nc.vector.reciprocal(sigm[:, :, :], sigm[:, :, :]))
                wv = rank[:, :, 0:HEADS, :]
                stepped(nc.vector.tensor_tensor(wv, wv, sigm[:, :, :].rearrange("p t (h e) -> p t h e", e=EXPERTS), ALU.mult))
                assert n[0] == GATE_STEPS

            def do(place, b, p, par, plan):
                nxt = 1 - par
                for item in plan:
                    u = item[0]
                    bank = ring[place.ring]
                    taken = free[place.ring]
                    bank_count = place.bank[place.ring].value
                    this_full = place.units.value + (1 + AHEAD)
                    if u in ("moments", "scaled"):
                        rows, n, loaded = (XN, QT, rows_loaded) if item[1] == "x" else (C, KT, c_loaded)
                        if u == "moments":
                            dve.wait_ge(loaded, 16 * place["load"])
                            if latent:
                                dve.wait_ge(norm_steps, norm_count(place))
                            take_moments(nc, dve, norm_tiles, norm_sems, lambda t: rows[:, t, :], n, norm_count(place))
                        else:
                            scale_rows(nc, dve, norm_tiles, norm_sems, lambda t: rows[:, t, :], rows, n, norm_count(place),
                                       place["scaled_x"] + place["scaled_c"])
                    elif u == "turn":
                        _, src, ch, g = item
                        H, L = (XTH, XTL) if src == "x" else (CTH, CTL)
                        cols = slice(g * 512, g * 512 + 512)
                        dve.wait_ge(staged, place["turn"] + 1)
                        nc.vector.tensor_copy(H[:, ch, cols], staging[place.ring][:, :]).then_inc(turn_high, 1)
                        dve.wait_ge(turn_high, place["turn"] + 1)
                        nc.vector.tensor_tensor(L[:, ch, cols], staging[place.ring][:, :], H[:, ch, cols].bitcast(fp32),
                                                ALU.subtract).then_inc(taken, 1)
                    elif u == "kept":
                        dve.wait_ge(mix_steps, mix_steps_before(b, 0))
                        nc.vector.tensor_copy(out_mask[:, :, :, :], rank[:, :, HEADS:, :]).then_inc(mask_kept, 1)
                    elif u == "masks":
                        evacuated(dve, place.mark())
                        dve.wait_ge(v_steps, V_STEPS * place["vmix"] + AHEAD)
                        dve.wait_ge(mask_kept, place["masks"] + AHEAD)
                        masks(place, b)
                    elif u == "kv" and latent:
                        t = item[1]
                        rot1, rot2 = rot1s[t % 2], rot2s[t % 2]
                        tiles = slice(2 * t, 2 * t + 2)
                        K = bank[:, :].rearrange("p (s n) -> p s n", s=2)[:, :, 0:128]
                        K4 = K.rearrange("p s (g i) -> p s g i", i=32)
                        K5 = K.rearrange("p s (h f i) -> p s h f i", f=2, i=32)
                        R5 = rot2[:, :, :].rearrange("p s (h f i) -> p s h f i", f=2, i=32)
                        dve.wait_ge(rotated, place["kv"] + (AHEAD - 1))
                        dve.wait_ge(taken, bank_count + 1)
                        dve.wait_ge(v_copied, place["kv"] + 1)
                        nc.vector.tensor_tensor(rot1[:, :, :].rearrange("p s (g i) -> p s g i", i=32), K4,
                                                cos[:, tiles, :].unsqueeze(2).broadcast_to([P, 2, 4, 32]), ALU.mult)
                        for f, table in ((0, nsin), (1, sin)):
                            last = nc.vector.tensor_tensor(R5[:, :, :, f, :], K5[:, :, :, 1 - f, :],
                                                           table[:, tiles, :].unsqueeze(2).broadcast_to([P, 2, 2, 32]),
                                                           ALU.mult)
                        last.then_inc(taken, 1)
                    elif u in ("k", "kT"):
                        cols = slice(item[1] * 512, item[1] * 512 + 512) if u == "kT" else slice(0, 512)
                        dve.wait_ge(high, place["k"] + place["kT"] + place["q"] + 1)
                        for h in range(2):
                            last = nc.vector.scalar_tensor_tensor(
                                out=S1[nxt][AUX[h], h, cols], in0=bank[MAIN[h], :],
                                scalar=pair_bias[nxt][MAIN[h], 1:2] if cross else 0.0,
                                in1=S1[nxt][MAIN[h], h, cols].bitcast(fp32), op0=ALU.add, op1=ALU.subtract)
                        last.then_inc(taken, 1)
                    elif u == "q":
                        dve.wait_ge(high, place["k"] + place["kT"] + place["q"] + 1)
                        for h in range(2):
                            last = nc.vector.scalar_tensor_tensor(
                                out=Q2[nxt][MAIN[h], h, :], in0=bank[MAIN[h], :],
                                scalar=pair_bias[nxt][MAIN[h], 0:1] if cross else 0.0,
                                in1=Q1[nxt][MAIN[h], h, :].bitcast(fp32), op0=ALU.add, op1=ALU.subtract)
                        last.then_inc(taken, 1)
                    elif u == "max":
                        _, h, qt, i, is_last = item
                        dve.wait_ge(full, this_full)
                        nc.vector.reduce_max(part[:, h, qt, i:i + 1], bank[:, :], AX.X).then_inc(taken, 1)
                        if is_last:
                            dve.wait_ge(taken, bank_count + 2)
                            dve.wait_ge(free[1 - place.ring], place.bank[1 - place.ring].value + 1)
                            nc.vector.reduce_max(top[:, h, :], part[:, h, :, :], AX.X).then_inc(top_found, 1)
                            dve.wait_ge(top_found, place["top"] + 1)
                            nc.vector.tensor_scalar(negtop[:, h, :], top[:, h, :], -1.0, None, ALU.mult)\
                              .then_inc(negtop_ready, 1)
                            if own:
                                dve.wait_ge(negtop_ready, place["top"] + 1)
                                nc.vector.tensor_tensor(diag[h][:, :, :], ident[:, :].unsqueeze(1).broadcast_to([P, QT, P]),
                                                        negtop[:, h, :].unsqueeze(2).broadcast_to([P, QT, P]), ALU.mult)\
                                  .then_inc(diag_ready, 1)
                    elif u == "soft":
                        _, h, c = item
                        if latent:
                            tile = probs[h][c % 2]
                            s = place.attends.value * (2 * NC) + (2 * c + h + 1)
                            dve.wait_ge(exp_done, s + AHEAD)
                            nc.vector.tensor_scalar(tile[:, :, :], tile[:, :, :], exp(CLIP), exp(-CLIP), ALU.min, ALU.max)\
                              .then_inc(clipped, 1)
                        if h == 0:
                            add_up(dve, nc.vector, place, 0, c)
                    elif u == "sum":
                        dve.wait_ge(taken, bank_count + 2)
                        nc.vector.reciprocal(recip[:, :], sums[:, :]).then_inc(recip_made, 1)
                        dve.wait_ge(recip_made, place["sum"] + 1)
                        dve.wait_ge(av_done, NC * (place["sum"] + 1) + AHEAD)
                        if latent:
                            dst = OT[:, bass.ds(p - 1, 1), :]
                        else:
                            dst = O32[:, :].unsqueeze(1)
                        if cross:
                            dve.wait_ge(out_biased, place["sum"] + AHEAD)
                        nc.vector.tensor_tensor(dst, outT[nxt][:, :].unsqueeze(1), recip[:, :].unsqueeze(1), ALU.mult)\
                          .then_inc(normed, 1)
                    elif u == "vmix":
                        q, e = following(p), item[1]
                        base = V_STEPS * place["vmix"] + AHEAD
                        shape = [P, QT, 2, DH]
                        V = VN[nxt][:, :, :].rearrange("p t (h k) -> p t h k", h=2)
                        if e == 0:
                            dve.wait_ge(av_done, NC * place.attends.value + AHEAD)
                        if e > 1:
                            dve.wait_ge(v_steps, base + (2 * e - 1))
                        nc.vector.tensor_tensor(v_part[:, :, :, :] if e else V,
                                                gated[:, :, e * DH:(e + 1) * DH].unsqueeze(2).broadcast_to(shape),
                                                rank[:, :, 2 * q:2 * q + 2, e:e + 1].broadcast_to(shape), ALU.mult)\
                          .then_inc(v_steps, 1)
                        if e:
                            dve.wait_ge(v_steps, base + 2 * e)
                            nc.vector.tensor_tensor(V, V, v_part[:, :, :, :], ALU.add).then_inc(v_steps, 1)
                    elif u == "mix" and plan is tail and item[1] < SHARE:
                        if item[1] == 0:
                            evacuated(dve, place.mark())
                            dve.wait_ge(mix_steps, mix_steps_before(b, NP - 1))
                            dve.wait_ge(v_steps, V_STEPS * place["vmix"] + AHEAD)
                        mix(dve, nc.vector, NP - 1, item[1], natural[1 - par], v_part, v_joined, last_mix_steps,
                            b * (3 * SHARE) + (3 * item[1] + AHEAD))
                    elif u == "out":
                        t = item[1]
                        if t == 0:
                            dve.wait_ge(x_loaded, 16 * b + 16)
                        if t == 0 and not own:
                            nc.vector.tensor_tensor(X[:, :, :], X[:, :, :], bo[:, :].unsqueeze(1).broadcast_to([P, QT, D]),
                                                    ALU.add).then_inc(rows_biased, 1)
                            dve.wait_ge(rows_biased, b + 1)
                        dve.wait_ge(full, this_full)
                        nc.vector.tensor_tensor(X[:, t, :], bank[:, 0:D], X[:, t, :], ALU.add).then_inc(taken, 1)
                    place.passed(item)

            walk(dve, do)

        @block.tensor
        def _(pe):
            pe.wait_ge(const_made, MADE)

            def product(out, passes, start=True, stop=True):
                for i, (still, moving) in enumerate(passes):
                    last = nc.tensor.matmul(out, still, moving, start=start and i == 0, stop=stop and i == len(passes) - 1)
                return last

            def three(highs, lows, highs2, lows2):
                return [pair for a, al, w, wl in zip(highs, lows, highs2, lows2) for pair in ((a, w), (a, wl), (al, w))]

            def do(place, b, p, par, plan):
                nxt = 1 - par
                made, rows_entered = place.mark(), False
                last_bank, made0 = 1 - place.ring, list(made)
                if plan is not first_step:
                    made0[last_bank] = made0[last_bank] - (behind_shift + 1) // 2
                    made0[1 - last_bank] = made0[1 - last_bank] - behind_shift // 2
                kv_mark = None
                for item in plan:
                    u = item[0]
                    bank = ring[place.ring]
                    if u in Place.UNITS:
                        pe.wait_ge(free[place.ring], place.bank[place.ring].value + 1)
                    if u == "turned":
                        rows_entered = True
                    if rows_entered and u in ("gate", "q"):
                        evacuated(pe, place.mark())
                        rows_entered = False
                    if u == "turn":
                        _, src, ch, g = item
                        if src == "x" or latent:
                            pe.wait_ge(norm_steps, norm_count(place))
                        elif cross:
                            pe.wait_ge(c_loaded, 16 * place["load"])
                        rows = XN if src == "x" else C
                        for k in range(4):
                            last = nc.tensor.transpose(bank[:, k * P:(k + 1) * P],
                                                       rows[:, 4 * g + k, ch * P:(ch + 1) * P], ident[:, :])
                        last.then_inc(full, 1)
                    elif u == "gate":
                        t = item[1]
                        ts = slice(t * P, (t + 1) * P)
                        product(bank[:, 0:NGATE], three(*([T[:, ch, ts] for ch in range(2)] for T in (XTH, XTL)),
                                                        *([T[:, ch, :] for ch in range(2)] for T in (gates_hi, gates_lo))))\
                            .then_inc(full, 1)
                    elif u == "kv":
                        t = item[1]
                        for s in range(2):
                            ts = slice((2 * t + s) * P, (2 * t + s + 1) * P)
                            last = product(bank[:, s * 256:(s + 1) * 256],
                                           three(*([T[:, ch, ts] for ch in range(2)] for T in (CTH, CTL)),
                                                 *([T[nxt][:, ch, P:3 * P] for ch in range(2)] for T in (WH, WL))))
                        last.then_inc(full, 1)
                    elif u in ("q", "k"):
                        if u == "k" or not own:
                            pe.wait_ge(w_split, place["q"] + 2)
                        at = P if u == "k" else 0
                        product(bank[:, :], three(*([T[nxt][:, ch, at:at + P] for ch in range(2)] for T in (WH, WL)),
                                                  *([T[:, ch, :] for ch in range(2)] for T in (XTH, XTL)))).then_inc(full, 1)
                    elif u == "kT":
                        evacuated(pe, kv_mark)
                        if latent:
                            pe.wait_ge(rotated, place["kv"] + AHEAD)
                        for k in range(4):
                            t = 4 * item[1] + k
                            last = nc.tensor.transpose(bank[:, k * P:(k + 1) * P],
                                                       KR[:, t, :] if latent else VN[nxt][:, t, 0:P], ident[:, :])
                        last.then_inc(full, 1)
                    elif u == "max":
                        _, h, qt, i, _ = item
                        if (h, qt, i) == (0, 0, 0):
                            evacuated(pe, place.mark())
                            pe.wait_ge(copied, copies(place) - (HALVES if cross else 0))
                        nc.tensor.matmul(bank[:, :], Q1[nxt][:, h, qt * P:(qt + 1) * P], S1[nxt][:, h, i * 512:(i + 1) * 512],
                                         start=True, stop=True).then_inc(full, 1)
                    elif u == "shift":
                        pe.wait_ge(diag_ready, place["shift"] + 1)
                        nc.tensor.matmul(bank[:, :], spread[:, :], diag[item[1]][:, :, :].rearrange("p t n -> p (t n)"),
                                         start=True, stop=True).then_inc(full, 1)
                    elif u == "S":
                        _, h, c = item
                        if c == 0:
                            evacuated(pe, made if h else made0)
                        if c == 0 and h == 0:
                            pe.wait_ge(copied, copies(place))
                        pe.wait_ge(exp_done, place.attends.value * (2 * NC) + (2 * c + h - 1 + AHEAD))
                        for k in range(2):
                            ks = slice((2 * c + k) * P, (2 * c + k + 1) * P)
                            last = product(scores[h][:, k, :], [(S1[par][:, h, ks], Q1[par][:, h, :]),
                                                                (S2[par][:, h, ks], Q2[par][:, h, :])])
                        last.then_inc(s_full, 1)
                    elif u == "AV":
                        _, c, k = item
                        if k == 0:
                            pe.wait_ge(p_ready, place.attends.value * (2 * NC) + (2 * c + 2 + p_ahead))
                            if c == 0:
                                pe.wait_ge(normed, place.attends.value + (AHEAD - 1))
                                if own:
                                    pe.wait_ge(v_steps, V_STEPS * place.attends.value + (V_STEPS + AHEAD))
                        whose, tile = (par, 2 * c + k) if c >= 0 else (nxt, 2 * (NC - 1) + k)
                        for h in range(2):
                            last = nc.tensor.matmul(outT[whose][MAIN[h], :], VN[whose][:, tile, VC + h * DH:VC + (h + 1) * DH],
                                                    probs[h][c % 2][:, k, :], start=(c == 0 and k == 0),
                                                    stop=(c == -1 and k == 1))
                        if k == 1:
                            last.then_inc(av_done, 1)
                    elif u == "sum":
                        for h in range(2):
                            pe.wait_ge(fold_done[h], place["sum"] + (1 + AHEAD))
                            last = nc.tensor.matmul(bank[MAIN[h], :], ones[:, :], folded[h][:, :], start=True, stop=True)
                        last.then_inc(full, 1)
                    elif u == "back":
                        pe.wait_ge(normed, place["back"] + (1 + AHEAD))
                        for t in range(QT):
                            last = nc.tensor.transpose(bank[:, t * P:(t + 1) * P], O32[:, t * P:(t + 1) * P], ident[:, :])
                        last.then_inc(full, 1)
                    elif u == "mixT":
                        t = item[1]
                        if t == 0:
                            pe.wait_ge(mix_steps, mix_steps_before(b, NP))
                            pe.wait_ge(last_mix_steps, b * (3 * SHARE) + (3 * SHARE + AHEAD))
                        for c in range(3):
                            last = nc.tensor.transpose(bank[:, c * P:(c + 1) * P], mixed[:, t, c * P:(c + 1) * P], ident[:, :])
                        last.then_inc(full, 1)
                    elif u == "out":
                        t = item[1]
                        ts = slice(t * P, (t + 1) * P)
                        if t == 0:
                            if own:
                                evacuated(pe, place.mark())
                            else:
                                pe.wait_ge(normed if latent else out_biased, place["sum"] + AHEAD)
                        O, chunks = (mixedT, 3) if own else (OT, NP)
                        product(bank[:, 0:D], [(O[:, c, ts], WO[:, c, :]) for c in range(chunks)]).then_inc(full, 1)
                    place.passed(item)
                    if u == "kv":
                        kv_mark = place.mark()

            walk(pe, do)



def expert_layer(nc, name, x_in, x_out, weights, B):
    fp32, f32r = mybir.dt.float32, mybir.dt.float32r
    ALU, ACT, AX = mybir.AluOpType, mybir.ActivationFunctionType, mybir.AxisListType
    E = ROUTED
    WIDE = E * D
    BANKS = 4
    SETUP = 2 * E
    PER_BATCH = QT * E // 2

    ctx = ExitStack()
    with ctx:
        def sb(label, shape, dt=fp32):
            return ctx.enter_context(nc.sbuf_tensor(f"{name}_{label}", shape, dt))

        def sem(label):
            return ctx.enter_context(nc.semaphore(f"{name}_{label}"))

        X, XN = sb("X", [P, QT, D]), sb("XN", [P, QT, D])
        XT = [sb(f"XT{part}", [P, 2, NQ], f32r) for part in ("high", "low")]
        raw = sb("raw", [P, 2 * E, D])
        W = [sb(f"W{part}", [P, 2, WIDE], f32r) for part in ("high", "low")]
        router_raw = sb("router_raw", [P, 2, E])
        router = [sb(f"router_{part}", [P, 2, E], f32r) for part in ("high", "low")]
        router_b = sb("router_b", [P, E])
        bias_raw, bias_high = sb("bias_raw", [64, WIDE]), sb("bias_high", [64, WIDE], f32r)
        bias, ones = sb("bias", [P, WIDE], f32r), sb("ones", [P, P], f32r)
        ident, neghalf = sb("ident", [P, P]), sb("neghalf", [P, QT])
        tiles = (sb("stats", [P, QT, 6]), sb("mv", [P, QT, 2]), sb("varr", [P, QT]), sb("rstd", [P, QT]),
                 [sb(f"newton{i}", [P, QT]) for i in range(4)], sb("carrier", [P, 1]))
        varr, rstd = tiles[2], tiles[3]
        logits, less = sb("logits", [P, QT, 1, E]), sb("less", [P, QT, E])
        rank, over = sb("rank", [P, QT, 1, E]), sb("over", [P, QT, 1, E])
        top, total, weight = sb("top", [P, QT]), sb("total", [P, QT]), sb("weight", [P, QT])
        pick = sb("pick", [P, QT, E])

        turned = [ctx.enter_context(nc.psum_tensor(f"{name}_turned{i}", [P, NQ], fp32)) for i in range(2)]
        routed = ctx.enter_context(nc.psum_tensor(f"{name}_routed", [P, QT, E], fp32))
        ring = [ctx.enter_context(nc.psum_tensor(f"{name}_ring{i}", [P, 512], fp32)) for i in range(BANKS)]

        const_loaded, const_made, router_split = sem("const_loaded"), sem("const_made"), sem("router_split")
        bias_steps = sem("bias_steps")
        x_loaded, rows_loaded, x_stored = sem("x_loaded"), sem("rows_loaded"), sem("x_stored")
        norm_steps, var_ready, rsqrt_ready = sem("norm_steps"), sem("var_ready"), sem("rsqrt_ready")
        w_full, w_high = sem("w_full"), sem("w_high")
        free = [sem(f"free{i}") for i in range(BANKS)]
        turn_full, turn_high, turn_done = sem("turn_full"), sem("turn_high"), sem("turn_done")
        route_full, route_steps, exp_done = sem("route_full"), sem("route_steps"), sem("exp_done")
        full, first_added = sem("full"), sem("first_added")

        ROUTE_STEPS = 3 + (4 * (E - 1) + 1) + 4
        NORM_STEPS = 3 * QT + 4
        block = ctx.enter_context(nc.Block())

        @block.sync
        def _(sp):
            sp.dma_start(raw[:, :, :], weights["L0_ffn_expert_w"].rearrange("e (c p) d -> p (e c) d", p=P))\
              .then_inc(const_loaded, 16)
            sp.dma_start(router_b[:, :], weights["L0_ffn_router_b"].rearrange("(a n) -> a n", a=1).broadcast_to([P, E]))\
              .then_inc(const_loaded, 16)
            for c in range(2):
                sp.dma_start(router_raw[:, c, :], weights["L0_ffn_router_w"][:, c * P:(c + 1) * P].rearrange("e p -> p e"),
                             allow_slow_non_contiguous=True).then_inc(const_loaded, 16)
            for row in (0, 32):
                sp.dma_start(bias_raw[row:row + 1, :], weights["L0_ffn_expert_b"].rearrange("(a e) d -> a (e d)", a=1))\
                  .then_inc(const_loaded, 16)

            def load(b):
                sp.dma_start(XN[:, :, :], x_in[bass.ds(b * NQ, NQ), :].rearrange("(t p) d -> p t d", p=P))\
                  .then_inc(rows_loaded, 16)

            def batch(b, more):
                if more:
                    sp.wait_ge(turn_full, 2 * b + 2)
                    load(b + 1)
                sp.wait_ge(x_stored, 16 * b + 16)
                sp.dma_start(X[:, :, :], x_in[bass.ds(b * NQ, NQ), :].rearrange("(t p) d -> p t d", p=P)).then_inc(x_loaded, 16)
                for i in range(BANKS):
                    sp.wait_ge(free[i], (SETUP + PER_BATCH) // BANKS + (PER_BATCH // BANKS) * b)
                sp.dma_start(x_out[bass.ds(b * NQ, NQ), :].rearrange("(t p) d -> p t d", p=P), X[:, :, :]).then_inc(x_stored, 16)

            load(0)
            with sp.Fori(0, B - 1) as b:
                batch(b, True)
            batch(B - 1, False)
            sp.wait_ge(x_stored, 16 * B + 16)

        @block.gpsimd
        def _(pool):
            nc.gpsimd.memset(ident[:, :], 0.0).then_inc(const_made, 1)
            nc.gpsimd.memset(bias[:, :].bitcast(fp32), 0.0).then_inc(const_made, 1)
            nc.gpsimd.memset(ones[:, :].bitcast(fp32), 1.0).then_inc(const_made, 1)
            nc.gpsimd.memset(neghalf[:, :], -0.5).then_inc(x_stored, 16)
            pool.wait_ge(const_made, 3)
            nc.gpsimd.affine_select(out=ident[:, :], in_=ident[:, :], compare_op=ALU.not_equal, fill=1.0, base=0,
                                    pattern=[[-1, P]], channel_multiplier=1).then_inc(const_made, 1)
            pool.wait_ge(const_made, 4)
            pool.wait_ge(x_stored, 16)
            with pool.Fori(0, B) as b:
                pool.wait_ge(var_ready, b + 1)
                nc.gpsimd.tensor_tensor(rstd[:, :], varr[:, :], neghalf[:, :], ALU.pow).then_inc(rsqrt_ready, 1)

        @block.scalar
        def _(act):
            for u in range(SETUP):
                ch, pair = u % 2, u // 2
                act.wait_ge(w_full, u + 1)
                nc.scalar.activation(W[0][:, ch, pair * 256:pair * 256 + 256], ring[u % BANKS][:, 0:256], ACT.Copy)\
                  .then_inc(w_high, 1)
            with act.Fori(0, B) as b:
                for ch in range(2):
                    act.wait_ge(turn_full, 2 * b + (ch + 1))
                    nc.scalar.activation(XT[0][:, ch, :], turned[ch][:, :], ACT.Copy).then_inc(turn_high, 1)
                act.wait_ge(route_steps, ROUTE_STEPS * b + 3)
                nc.scalar.activation(less[:, :, :], less[:, :, :], ACT.Exp).then_inc(exp_done, 1)

        @block.vector
        def _(dve):
            dve.wait_ge(const_made, 4)
            dve.wait_ge(const_loaded, 96)
            nc.vector.tensor_copy(router[0][:, :, :], router_raw[:, :, :]).then_inc(router_split, 1)
            dve.wait_ge(router_split, 1)
            nc.vector.tensor_tensor(router[1][:, :, :], router_raw[:, :, :], router[0][:, :, :].bitcast(fp32), ALU.subtract)\
              .then_inc(router_split, 1)
            nc.vector.tensor_copy(bias[0:1, :], bias_raw[0:1, :]).then_inc(bias_steps, 1)
            nc.vector.tensor_copy(bias_high[32:33, :], bias_raw[32:33, :]).then_inc(bias_steps, 1)
            dve.wait_ge(bias_steps, 2)
            nc.vector.tensor_tensor(bias[32:33, :], bias_raw[32:33, :], bias_high[32:33, :].bitcast(fp32), ALU.subtract)\
              .then_inc(bias_steps, 1)
            for u in range(SETUP):
                ch, pair = u % 2, u // 2
                dve.wait_ge(w_high, u + 1)
                nc.vector.tensor_tensor(W[1][:, ch, pair * 256:pair * 256 + 256], ring[u % BANKS][:, 0:256],
                                        W[0][:, ch, pair * 256:pair * 256 + 256].bitcast(fp32), ALU.subtract)\
                  .then_inc(free[u % BANKS], 1)
            norm = (nc, dve, tiles, (norm_steps, var_ready, rsqrt_ready), lambda t: XN[:, t, :])

            def moments(b):
                dve.wait_ge(rows_loaded, 16 * b + 16)
                take_moments(*norm, QT, NORM_STEPS * b)

            def scaled(b):
                scale_rows(*norm, XN, QT, NORM_STEPS * b + 2 * QT, b)

            def batch(b, more):
                for ch in range(2):
                    dve.wait_ge(turn_high, 2 * b + (ch + 1))
                    nc.vector.tensor_tensor(XT[1][:, ch, :], turned[ch][:, :], XT[0][:, ch, :].bitcast(fp32), ALU.subtract)\
                      .then_inc(turn_done, 1)
                n = [0]

                def stepped(ins):
                    ins.then_inc(route_steps, 1)
                    n[0] += 1
                    dve.wait_ge(route_steps, ROUTE_STEPS * b + n[0])

                dve.wait_ge(route_full, b + 1)
                stepped(nc.vector.tensor_tensor(logits[:, :, 0, :], routed[:, :, :],
                                                router_b[:, :].unsqueeze(1).broadcast_to([P, QT, E]), ALU.add))
                stepped(nc.vector.reduce_max(top[:, :], logits[:, :, 0, :], AX.X))
                stepped(nc.vector.tensor_tensor(less[:, :, :], logits[:, :, 0, :],
                                                top[:, :].unsqueeze(2).broadcast_to([P, QT, E]), ALU.subtract))
                rank_experts(nc, stepped, logits, rank, over, E)
                dve.wait_ge(exp_done, b + 1)
                stepped(nc.vector.reduce_sum(total[:, :], less[:, :, :], AX.X))
                stepped(nc.vector.reciprocal(weight[:, :], total[:, :]))
                stepped(nc.vector.tensor_scalar(pick[:, :, :], rank[:, :, 0, :], 0.5, None, ALU.is_lt))
                stepped(nc.vector.tensor_tensor(pick[:, :, :], pick[:, :, :],
                                                weight[:, :].unsqueeze(2).broadcast_to([P, QT, E]), ALU.mult))
                assert n[0] == ROUTE_STEPS
                dve.wait_ge(x_loaded, 16 * b + 16)
                for k in range(PER_BATCH):
                    t, pair = k // (E // 2), k % (E // 2)
                    if more and k == PER_BATCH // 4:
                        moments(b + 1)
                    if more and k == PER_BATCH // 2:
                        scaled(b + 1)
                    dve.wait_ge(full, PER_BATCH * b + (k + 1))
                    if k:
                        dve.wait_ge(free[(k - 1) % BANKS], (PER_BATCH // BANKS) * b + (SETUP // BANKS + (k - 1) // BANKS + 1))
                    for i in range(2):
                        e = 2 * pair + i
                        ins = nc.vector.scalar_tensor_tensor(out=X[:, t, :], in0=ring[k % BANKS][:, i * D:(i + 1) * D],
                                                             scalar=pick[:, t, e:e + 1], in1=X[:, t, :],
                                                             op0=ALU.mult, op1=ALU.add)
                        if i == 0:
                            ins.then_inc(first_added, 1)
                            dve.wait_ge(first_added, PER_BATCH * b + (k + 1))
                        else:
                            ins.then_inc(free[k % BANKS], 1)

            moments(0)
            scaled(0)
            with dve.Fori(0, B - 1) as b:
                batch(b, True)
            batch(B - 1, False)

        @block.tensor
        def _(pe):
            pe.wait_ge(const_made, 4)
            pe.wait_ge(const_loaded, 96)
            for u in range(SETUP):
                ch, e = u % 2, u // 2
                if u >= BANKS:
                    pe.wait_ge(free[u % BANKS], u // BANKS)
                for c in range(2):
                    last = nc.tensor.transpose(ring[u % BANKS][:, c * P:(c + 1) * P], raw[:, 2 * e + c, ch * P:(ch + 1) * P],
                                               ident[:, :])
                last.then_inc(w_full, 1)
            pe.wait_ge(router_split, 2)
            pe.wait_ge(bias_steps, 3)
            with pe.Fori(0, B) as b:
                pe.wait_ge(norm_steps, NORM_STEPS * b + NORM_STEPS)
                for ch in range(2):
                    for t in range(QT):
                        last = nc.tensor.transpose(turned[ch][:, t * P:(t + 1) * P], XN[:, t, ch * P:(ch + 1) * P], ident[:, :])
                    last.then_inc(turn_full, 1)
                pe.wait_ge(turn_done, 2 * b + 2)
                for t in range(QT):
                    ts = slice(t * P, (t + 1) * P)
                    for i, (a, w, ch) in enumerate([(a, w, ch) for ch in range(2) for a, w in ((0, 0), (0, 1), (1, 0))]):
                        last = nc.tensor.matmul(routed[:, t, :], XT[a][:, ch, ts], router[w][:, ch, :],
                                                start=(i == 0), stop=(i == 5))
                last.then_inc(route_full, 1)
                for k in range(PER_BATCH):
                    t, pair = k // (E // 2), k % (E // 2)
                    ts, es = slice(t * P, (t + 1) * P), slice(pair * 512, pair * 512 + 512)
                    pe.wait_ge(free[k % BANKS], (PER_BATCH // BANKS) * b + (SETUP // BANKS + k // BANKS))
                    nc.tensor.matmul(ring[k % BANKS][:, :], ones[:, :], bias[:, es], start=True, stop=False)
                    for i, (a, w, ch) in enumerate([(a, w, ch) for ch in range(2) for a, w in ((0, 0), (0, 1), (1, 0))]):
                        last = nc.tensor.matmul(ring[k % BANKS][:, :], XT[a][:, ch, ts], W[w][:, ch, es], start=False,
                                                stop=(i == 5))
                    last.then_inc(full, 1)


def latent_weights(i):
    return {"slices": [(i["L0_xattn_Wq"], 0), (i["L0_xattn_Wkv"], 0), (i["L0_xattn_Wkv"], 1024)],
            "Wo": i["L0_xattn_Wo"], "bo": i["L0_xattn_bo"], "cos": i["L0_xattn_cos"], "sin": i["L0_xattn_sin"],
            "gx": i["L0_xattn_ln_lat_g"], "bx": i["L0_xattn_ln_lat_b"], "gc": i["L0_xattn_ln_ctx_g"],
            "bc": i["L0_xattn_ln_ctx_b"]}


def cross_weights(i):
    flat = {w: i[f"L1_xattn_{w}"].rearrange("d h k -> d (h k)") for w in ("Wq", "Wk", "Wv")}
    return {"slices": [(flat["Wq"], 0), (flat["Wk"], 0), (flat["Wv"], 0)],
            "Wo": i["L1_xattn_Wo"].rearrange("h k d -> (h k) d"), "bo": i["L1_xattn_bo"],
            **{b: i[f"L1_xattn_{b}"].rearrange("h k -> (h k)") for b in ("bq", "bk", "bv")}}


def self_weights(i):
    return {"slices": [(i["L1_ffn_Wq"], 0), (i["L1_ffn_Wk"], 0)], "Wo": i["L1_ffn_Wo"].rearrange("e k d -> (e k) d"),
            "Wv": i["L1_ffn_Wv"], "Ws": i["L1_ffn_Ws"], "Wd": i["L1_ffn_Wd"]}


def build(nc, ins, out):
    B, S, _ = ins["x"].shape
    assert S == NQ
    KEYS = ins["ctx_1024"].shape[1]
    between = [nc.dram_tensor(f"x_after_{i}", (B * S, D), mybir.dt.float32).ap() for i in range(3)]
    x, y = ins["x"].rearrange("b n d -> (b n) d"), out.rearrange("b n d -> (b n) d")
    context = ins["ctx_1024"].rearrange("b n d -> (b n) d")
    attention_layer(nc, "latent", "latent", x, between[0], context, latent_weights(ins), B, 8, KEYS // P)
    expert_layer(nc, "experts", between[0], between[1], ins, B)
    attention_layer(nc, "cross", "cross", between[1], between[2], context, cross_weights(ins), B, 8, KEYS // P)
    attention_layer(nc, "self", "self", between[2], y, None, self_weights(ins), B, 4, S // P)


_INS = ["x", "ctx_1024", "L0_xattn_cos", "L0_xattn_sin", "L0_xattn_ln_lat_g", "L0_xattn_ln_lat_b", "L0_xattn_ln_ctx_g",
        "L0_xattn_ln_ctx_b", "L0_xattn_Wq", "L0_xattn_Wkv", "L0_xattn_Wo", "L0_xattn_bo", "L0_ffn_router_w",
        "L0_ffn_router_b", "L0_ffn_expert_w", "L0_ffn_expert_b", "L1_xattn_Wq", "L1_xattn_bq", "L1_xattn_Wk",
        "L1_xattn_bk", "L1_xattn_Wv", "L1_xattn_bv", "L1_xattn_Wo", "L1_xattn_bo", "L1_ffn_Wq", "L1_ffn_Wk", "L1_ffn_Ws",
        "L1_ffn_Wd", "L1_ffn_Wv", "L1_ffn_Wo"]


def kernel(**inputs):
    import numpy as _np
    import concourse.bacc as _bacc
    from concourse import mybir as _mybir
    from concourse.bass_utils import run_bass_kernel_spmd as _run

    nc = _bacc.Bacc("TRN2", target_bir_lowering=False, num_devices=1)
    arrays, ins = {}, {}
    for name in _INS:
        a = _np.ascontiguousarray(inputs[name])
        arrays[f"in_{name}_dram"] = a
        ins[name] = nc.dram_tensor(f"in_{name}_dram", a.shape, _mybir.dt.from_np(a.dtype), kind="ExternalInput").ap()
    shape = inputs["x"].shape
    out = nc.dram_tensor("out_0_dram", shape, _mybir.dt.float32, kind="ExternalOutput").ap()
    build(nc, ins, out)
    r = _run(nc, [arrays], core_ids=[0])
    return r.results[0]["out_0_dram"]
```
